# Optimizing a Trainium2 kernel written in Bass

```python
import numpy as np
import jax
import jax.numpy as jnp

def _softmax(x, axis=-1):
    return jax.nn.softmax(x, axis=axis)

def _gelu(x):
    return jax.nn.gelu(x, approximate=True)

def _silu(x):
    return jax.nn.silu(x)

def _sigmoid(x):
    return jax.nn.sigmoid(x)

def _layernorm(x, axis=-1, eps=1e-05):
    m = jnp.mean(x, axis=axis, keepdims=True)
    v = jnp.var(x, axis=axis, keepdims=True)
    return (x - m) / jnp.sqrt(v + eps)

def _scatter_add(tgt, idx, src, axis=0):
    return tgt.at[idx].add(src)

def _segment_sum(src, seg, n):
    return jax.ops.segment_sum(src, seg, n)
kernel_name = 'mk_gnn_preln_d2_gnn_r8_8da96c'

def setup_inputs(seed: int=0):
    np.random.seed(seed)
    _w = jnp.asarray

    def _rec_inputs():
        import jax
        import jax.numpy as jnp
        _gk = jax.random.key(seed)
        x = -0.0006008 + 1.001 * jax.random.normal(jax.random.fold_in(_gk, 1), (1250, 512), jnp.float32)
        _s = jax.random.randint(jax.random.fold_in(_gk, 2), (10000,), 0, 1250, jnp.int32)
        _d = jax.random.randint(jax.random.fold_in(_gk, 3), (10000,), 0, 1250, jnp.int32)
        _loop = jnp.arange(1250, dtype=jnp.int32)
        src = jnp.concatenate([_s, _d, _loop])
        dst = jnp.concatenate([_d, _s, _loop])
        _o = jnp.argsort(dst, stable=True)
        src = src[_o]
        dst = dst[_o]
        edge_attr_20 = jax.random.uniform(jax.random.fold_in(_gk, 12), (21250, 20), jnp.float32, 0.0, 0.999999)
        edge_attr_3 = -0.0005747 + 0.998114 * jax.random.normal(jax.random.fold_in(_gk, 13), (21250, 3), jnp.float32)
        edge_weight = jax.random.uniform(jax.random.fold_in(_gk, 15), (21250,), jnp.float32, 0.0, 0.999973)
        return (x, src, dst, edge_attr_20, edge_attr_3, edge_weight)
    x, src, dst, edge_attr_20, edge_attr_3, edge_weight = _rec_inputs()

    def _L0_gnn_setup():
        import jax, jax.numpy as jnp
        import numpy as np
        N_ATOMS = 625
        N_EDGES = 6250
        C = 128
        F = 128
        N_RBF = 20
        LOG2 = float(np.log(2.0))
        Y0 = float(1.0 / np.sqrt(4.0 * np.pi))
        Y1_SCALE = float(np.sqrt(3.0 / (4.0 * np.pi)))

        def shifted_softplus(x):
            return jax.nn.softplus(x) - LOG2

        def _forward(x, idx_i, idx_j, f_ij, rcut_ij, r_ij, W_in2f_s, W_in2f_v, Wf1, bf1, Wf2, bf2, W1_s, W1_v, W2_s, W2_v):
            n = x.shape[0]
            e = r_ij.shape[0]
            xs = x[:, :C] @ (W_in2f_s / np.sqrt(C))
            xv = jnp.einsum('nci,cf->nfi', x[:, C:].reshape(n, C, 3), W_in2f_v) / np.sqrt(C)
            sj = xs[idx_j]
            vj = xv[idx_j]
            u = r_ij / jnp.linalg.norm(r_ij, axis=-1, keepdims=True)
            Yv = Y1_SCALE * u
            o0a = sj * Y0
            o0b = jnp.einsum('efi,ei->ef', vj, Yv) / np.sqrt(3.0)
            s2 = jnp.stack([o0a, o0b], axis=-1).reshape(e, 2 * F)
            ova = sj[:, :, None] * Yv[:, None, :]
            ovb = vj * Y0
            v2 = jnp.stack([ova, ovb], axis=2)
            w1 = jnp.cross(vj, Yv[:, None, :]) / np.sqrt(2.0)
            ax, ay, az = (vj[..., 0], vj[..., 1], vj[..., 2])
            bx, by, bz = (Yv[:, None, 0], Yv[:, None, 1], Yv[:, None, 2])
            t = jnp.stack([(ax * by + ay * bx) / np.sqrt(2.0), (ay * bz + az * by) / np.sqrt(2.0), (2.0 * az * bz - ax * bx - ay * by) / np.sqrt(6.0), (az * bx + ax * bz) / np.sqrt(2.0), (ax * bx - ay * by) / np.sqrt(2.0)], axis=-1)
            h = shifted_softplus(f_ij @ Wf1 + bf1)
            W = (h @ Wf2 + bf2) * rcut_ij[:, None]
            m_s = s2 * W[:, :2 * F]
            m_v = (v2.reshape(e, 2 * F, 3) * W[:, 2 * F:4 * F, None]).reshape(e, 6 * F)
            m_w = (w1 * W[:, 4 * F:5 * F, None]).reshape(e, 3 * F)
            m_t = (t * W[:, 5 * F:6 * F, None]).reshape(e, 5 * F)
            x_ij = jnp.concatenate([m_s, m_v, m_w, m_t], axis=1)
            agg = jax.ops.segment_sum(x_ij, idx_i, num_segments=n)
            S = agg[:, :2 * F] @ (W1_s / np.sqrt(2 * F))
            V = jnp.einsum('nmi,mc->nci', agg[:, 2 * F:8 * F].reshape(n, 2 * F, 3), W1_v) / np.sqrt(2 * F)
            S = shifted_softplus(S)
            S = S @ (W2_s / np.sqrt(C))
            V = jnp.einsum('nci,cd->ndi', V, W2_v) / np.sqrt(C)
            return jnp.concatenate([S, V.reshape(n, 3 * C)], axis=1)
        key = jax.random.key(seed)
        ks = jax.random.split(key, 16)
        f32 = jnp.float32
        x = jax.random.normal(ks[0], (N_ATOMS, 4 * C), f32)
        idx_i = jnp.sort(jax.random.randint(ks[1], (N_EDGES,), 0, N_ATOMS))
        idx_j = jax.random.randint(ks[2], (N_EDGES,), 0, N_ATOMS)
        f_ij = jax.random.uniform(ks[3], (N_EDGES, N_RBF), f32)
        rcut_ij = jax.random.uniform(ks[4], (N_EDGES,), f32)
        r_ij = jax.random.normal(ks[5], (N_EDGES, 3), f32)
        W_in2f_s = jax.random.normal(ks[6], (C, F), f32)
        W_in2f_v = jax.random.normal(ks[7], (C, F), f32)
        Wf1 = jax.random.normal(ks[8], (N_RBF, F), f32) / np.sqrt(N_RBF)
        bf1 = 0.1 * jax.random.normal(ks[9], (F,), f32)
        Wf2 = jax.random.normal(ks[10], (F, 6 * F), f32) / np.sqrt(F)
        bf2 = 0.1 * jax.random.normal(ks[11], (6 * F,), f32)
        W1_s = jax.random.normal(ks[12], (2 * F, C), f32)
        W1_v = jax.random.normal(ks[13], (2 * F, C), f32)
        W2_s = jax.random.normal(ks[14], (C, C), f32)
        W2_v = jax.random.normal(ks[15], (C, C), f32)
        return dict(x=x, idx_i=idx_i, idx_j=idx_j, f_ij=f_ij, rcut_ij=rcut_ij, r_ij=r_ij, W_in2f_s=W_in2f_s, W_in2f_v=W_in2f_v, Wf1=Wf1, bf1=bf1, Wf2=Wf2, bf2=bf2, W1_s=W1_s, W1_v=W1_v, W2_s=W2_s, W2_v=W2_v)
    _L0_gnn_all = _L0_gnn_setup()
    _L0_gnn_in = {k: v for k, v in _L0_gnn_all.items() if k in ('W_in2f_s', 'W_in2f_v', 'Wf1', 'bf1', 'Wf2', 'bf2', 'W1_s', 'W1_v', 'W2_s', 'W2_v')}
    del _L0_gnn_all

    def _L1_gnn_setup():
        import jax, jax.numpy as jnp
        import numpy as np
        N = 6250
        E = 200000
        IN_DIM, HID, LAT = (512, 128, 64)
        DEC_DIMS = [128, 256]
        OUT_DIM = 512

        def _glorot(key, shape):
            fan_in, fan_out = (shape[1], shape[0])
            lim = (6.0 / (fan_in + fan_out)) ** 0.5
            return jax.random.uniform(key, shape, jnp.float32, -lim, lim)

        def gcn_conv(x, W, b, src, dst, n):
            h = x @ W.T
            loop = jnp.arange(n, dtype=src.dtype)
            s = jnp.concatenate([src, loop])
            d = jnp.concatenate([dst, loop])
            deg = jnp.zeros((n,), h.dtype).at[d].add(1.0)
            dinv = jnp.where(deg > 0, deg ** (-0.5), 0.0)
            norm = dinv[s] * dinv[d]
            msg = h[s] * norm[:, None]
            out = jax.ops.segment_sum(msg, d, num_segments=n)
            return out + b
        key = jax.random.key(seed)
        ks = jax.random.split(key, 12)
        x = jax.random.normal(ks[0], (N, IN_DIM), jnp.float32)
        edge_index = jax.random.randint(ks[1], (2, E), 0, N, jnp.int64)
        W1 = _glorot(ks[2], (HID, IN_DIM))
        b1 = jnp.zeros((HID,), jnp.float32)
        W2 = _glorot(ks[3], (LAT, HID))
        b2 = jnp.zeros((LAT,), jnp.float32)
        Wd1 = _glorot(ks[4], (DEC_DIMS[0], LAT))
        bd1 = jnp.zeros((DEC_DIMS[0],), jnp.float32)
        Wd2 = _glorot(ks[5], (DEC_DIMS[1], DEC_DIMS[0]))
        bd2 = jnp.zeros((DEC_DIMS[1],), jnp.float32)
        Wd3 = _glorot(ks[6], (OUT_DIM, DEC_DIMS[1]))
        bd3 = jnp.zeros((OUT_DIM,), jnp.float32)
        return dict(x=x, edge_index=edge_index, W1=W1, b1=b1, W2=W2, b2=b2, Wd1=Wd1, bd1=bd1, Wd2=Wd2, bd2=bd2, Wd3=Wd3, bd3=bd3)
    _L1_gnn_all = _L1_gnn_setup()
    _L1_gnn_in = {k: v for k, v in _L1_gnn_all.items() if k in ('W1', 'b1', 'W2', 'b2', 'Wd1', 'bd1', 'Wd2', 'bd2', 'Wd3', 'bd3')}
    del _L1_gnn_all
    return {'x': x, 'src': src, 'dst': dst, 'edge_attr_20': edge_attr_20, 'edge_attr_3': edge_attr_3, 'edge_weight': edge_weight, 'L0_gnn_W_in2f_s': _L0_gnn_in['W_in2f_s'], 'L0_gnn_W_in2f_v': _L0_gnn_in['W_in2f_v'], 'L0_gnn_Wf1': _L0_gnn_in['Wf1'], 'L0_gnn_bf1': _L0_gnn_in['bf1'], 'L0_gnn_Wf2': _L0_gnn_in['Wf2'], 'L0_gnn_bf2': _L0_gnn_in['bf2'], 'L0_gnn_W1_s': _L0_gnn_in['W1_s'], 'L0_gnn_W1_v': _L0_gnn_in['W1_v'], 'L0_gnn_W2_s': _L0_gnn_in['W2_s'], 'L0_gnn_W2_v': _L0_gnn_in['W2_v'], 'L1_gnn_W1': _L1_gnn_in['W1'], 'L1_gnn_b1': _L1_gnn_in['b1'], 'L1_gnn_W2': _L1_gnn_in['W2'], 'L1_gnn_b2': _L1_gnn_in['b2'], 'L1_gnn_Wd1': _L1_gnn_in['Wd1'], 'L1_gnn_bd1': _L1_gnn_in['bd1'], 'L1_gnn_Wd2': _L1_gnn_in['Wd2'], 'L1_gnn_bd2': _L1_gnn_in['bd2'], 'L1_gnn_Wd3': _L1_gnn_in['Wd3'], 'L1_gnn_bd3': _L1_gnn_in['bd3']}

def reference(x, src, dst, edge_attr_20, edge_attr_3, edge_weight, L0_gnn_W_in2f_s, L0_gnn_W_in2f_v, L0_gnn_Wf1, L0_gnn_bf1, L0_gnn_Wf2, L0_gnn_bf2, L0_gnn_W1_s, L0_gnn_W1_v, L0_gnn_W2_s, L0_gnn_W2_v, L1_gnn_W1, L1_gnn_b1, L1_gnn_W2, L1_gnn_b2, L1_gnn_Wd1, L1_gnn_bd1, L1_gnn_Wd2, L1_gnn_bd2, L1_gnn_Wd3, L1_gnn_bd3):
    import jax
    import jax.numpy as jnp

    def _L0_gnn_ref(x, idx_i, idx_j, f_ij, rcut_ij, r_ij, W_in2f_s, W_in2f_v, Wf1, bf1, Wf2, bf2, W1_s, W1_v, W2_s, W2_v):
        import jax, jax.numpy as jnp
        import numpy as np
        N_ATOMS = 625
        N_EDGES = 6250
        C = 128
        F = 128
        N_RBF = 20
        LOG2 = float(np.log(2.0))
        Y0 = float(1.0 / np.sqrt(4.0 * np.pi))
        Y1_SCALE = float(np.sqrt(3.0 / (4.0 * np.pi)))

        def shifted_softplus(x):
            return jax.nn.softplus(x) - LOG2

        def _forward(x, idx_i, idx_j, f_ij, rcut_ij, r_ij, W_in2f_s, W_in2f_v, Wf1, bf1, Wf2, bf2, W1_s, W1_v, W2_s, W2_v):
            n = x.shape[0]
            e = r_ij.shape[0]
            xs = x[:, :C] @ (W_in2f_s / np.sqrt(C))
            xv = jnp.einsum('nci,cf->nfi', x[:, C:].reshape(n, C, 3), W_in2f_v) / np.sqrt(C)
            sj = xs[idx_j]
            vj = xv[idx_j]
            u = r_ij / jnp.linalg.norm(r_ij, axis=-1, keepdims=True)
            Yv = Y1_SCALE * u
            o0a = sj * Y0
            o0b = jnp.einsum('efi,ei->ef', vj, Yv) / np.sqrt(3.0)
            s2 = jnp.stack([o0a, o0b], axis=-1).reshape(e, 2 * F)
            ova = sj[:, :, None] * Yv[:, None, :]
            ovb = vj * Y0
            v2 = jnp.stack([ova, ovb], axis=2)
            w1 = jnp.cross(vj, Yv[:, None, :]) / np.sqrt(2.0)
            ax, ay, az = (vj[..., 0], vj[..., 1], vj[..., 2])
            bx, by, bz = (Yv[:, None, 0], Yv[:, None, 1], Yv[:, None, 2])
            t = jnp.stack([(ax * by + ay * bx) / np.sqrt(2.0), (ay * bz + az * by) / np.sqrt(2.0), (2.0 * az * bz - ax * bx - ay * by) / np.sqrt(6.0), (az * bx + ax * bz) / np.sqrt(2.0), (ax * bx - ay * by) / np.sqrt(2.0)], axis=-1)
            h = shifted_softplus(f_ij @ Wf1 + bf1)
            W = (h @ Wf2 + bf2) * rcut_ij[:, None]
            m_s = s2 * W[:, :2 * F]
            m_v = (v2.reshape(e, 2 * F, 3) * W[:, 2 * F:4 * F, None]).reshape(e, 6 * F)
            m_w = (w1 * W[:, 4 * F:5 * F, None]).reshape(e, 3 * F)
            m_t = (t * W[:, 5 * F:6 * F, None]).reshape(e, 5 * F)
            x_ij = jnp.concatenate([m_s, m_v, m_w, m_t], axis=1)
            agg = jax.ops.segment_sum(x_ij, idx_i, num_segments=n)
            S = agg[:, :2 * F] @ (W1_s / np.sqrt(2 * F))
            V = jnp.einsum('nmi,mc->nci', agg[:, 2 * F:8 * F].reshape(n, 2 * F, 3), W1_v) / np.sqrt(2 * F)
            S = shifted_softplus(S)
            S = S @ (W2_s / np.sqrt(C))
            V = jnp.einsum('nci,cd->ndi', V, W2_v) / np.sqrt(C)
            return jnp.concatenate([S, V.reshape(n, 3 * C)], axis=1)
        return _forward(x, idx_i, idx_j, f_ij, rcut_ij, r_ij, W_in2f_s, W_in2f_v, Wf1, bf1, Wf2, bf2, W1_s, W1_v, W2_s, W2_v)

    def _L1_gnn_ref(x, edge_index, W1, b1, W2, b2, Wd1, bd1, Wd2, bd2, Wd3, bd3):
        import jax, jax.numpy as jnp
        import numpy as np
        N = 6250
        E = 200000
        IN_DIM, HID, LAT = (512, 128, 64)
        DEC_DIMS = [128, 256]
        OUT_DIM = 512

        def _glorot(key, shape):
            fan_in, fan_out = (shape[1], shape[0])
            lim = (6.0 / (fan_in + fan_out)) ** 0.5
            return jax.random.uniform(key, shape, jnp.float32, -lim, lim)

        def gcn_conv(x, W, b, src, dst, n):
            h = x @ W.T
            loop = jnp.arange(n, dtype=src.dtype)
            s = jnp.concatenate([src, loop])
            d = jnp.concatenate([dst, loop])
            deg = jnp.zeros((n,), h.dtype).at[d].add(1.0)
            dinv = jnp.where(deg > 0, deg ** (-0.5), 0.0)
            norm = dinv[s] * dinv[d]
            msg = h[s] * norm[:, None]
            out = jax.ops.segment_sum(msg, d, num_segments=n)
            return out + b
        src, dst = (edge_index[0], edge_index[1])
        n = x.shape[0]
        h = gcn_conv(x, W1, b1, src, dst, n)
        h = jax.nn.relu(h)
        z = gcn_conv(h, W2, b2, src, dst, n)
        y = jax.nn.relu(z @ Wd1.T + bd1)
        y = jax.nn.relu(y @ Wd2.T + bd2)
        return y @ Wd3.T + bd3
    edge_index = jnp.stack([src, dst])
    h = jnp.maximum(_layernorm(x, axis=-1), 0.0)
    x = x + _L0_gnn_ref(h, src, dst, edge_attr_20, edge_weight, edge_attr_3, L0_gnn_W_in2f_s, L0_gnn_W_in2f_v, L0_gnn_Wf1, L0_gnn_bf1, L0_gnn_Wf2, L0_gnn_bf2, L0_gnn_W1_s, L0_gnn_W1_v, L0_gnn_W2_s, L0_gnn_W2_v)
    h = jnp.maximum(_layernorm(x, axis=-1), 0.0)
    x = x + _L1_gnn_ref(h, edge_index, L1_gnn_W1, L1_gnn_b1, L1_gnn_W2, L1_gnn_b2, L1_gnn_Wd1, L1_gnn_bd1, L1_gnn_Wd2, L1_gnn_bd2, L1_gnn_Wd3, L1_gnn_bd3)
    return x

_drawn_inputs = setup_inputs


def setup_inputs(seed=0):
    import zlib

    import numpy as np

    out = dict(_drawn_inputs(seed))
    spreads = {'L1_gnn_b1': (0.0, 0.47),
     'L1_gnn_b2': (0.0, 0.372),
     'L1_gnn_bd1': (0.0, 0.305),
     'L1_gnn_bd2': (0.0, 0.1),
     'L1_gnn_bd3': (0.0, 0.1)}
    factors = {}
    for name, (base, spread) in spreads.items():
        noise = np.random.default_rng([zlib.crc32(name.encode()), seed]).standard_normal(out[name].shape)
        drawn = base * np.exp(spread * noise) if base else spread * noise
        out[name] = jnp.asarray(drawn.astype(out[name].dtype))
    for name, factor in factors.items():
        out[name] = (out[name] * factor).astype(out[name].dtype)
    return out
```

```python
from contextlib import ExitStack

import numpy as np

import concourse.bass as bass
import concourse.mybir as mybir

F32 = mybir.dt.float32
BF16 = mybir.dt.bfloat16
F16 = mybir.dt.float16
I32 = mybir.dt.int32
U32 = mybir.dt.uint32
ALU = mybir.AluOpType
ACT = mybir.ActivationFunctionType
AX_X = mybir.AxisListType.X

P = 128
N = 1250
NB = (N + P - 1) // P
NPAD = NB * P
LAST = N - (NB - 1) * P
E = 21250
EP, EC = 125, 170
SW = 64
SB = NPAD // SW
HALF = NPAD // 2
GT = 3
GROUPS = 62
NT = GROUPS * GT
assert NT >= (E + SB * (P - 1)) // P and GROUPS % 2 == 0
NTX = NT + 3 * GT
D = 512
C = 128
RBF = 20
RW = 32
CO, SRCL, KEYS, KEYD, DST = 20, 24, 25, 26, 27
NOBODY = 2000.0
Y0 = float(1.0 / np.sqrt(4.0 * np.pi))
Y1 = float(np.sqrt(3.0 / (4.0 * np.pi)))
EPS = 1e-5
UN = 2 * GT
SORT_UNROLL = 10


def gnn_kernel(nc, a, out):
    ctx = ExitStack()
    with ctx:
        def sem(name):
            return ctx.enter_context(nc.semaphore(name))

        def keep(name, shape, dt):
            return ctx.enter_context(nc.sbuf_tensor(name, shape, dt))

        rec_dram = nc.dram_tensor("rec_dram", [E + 1, RW], F32).ap()
        node_dram = nc.dram_tensor("node_dram", [NPAD, D], F32).ap()

        AGG = keep("AGG", [P, SB, D], F32)
        AT = keep("AT", [P, SB, HALF], F32)
        X = keep("X", [P, NB, D], F32)
        EIDX = keep("EIDX", [P, NTX], U32)
        FLUSH = keep("FLUSH", [1, NT // UN], I32)
        BLOCK = keep("BLOCK", [1, NT + 1], I32)
        ident = keep("ident", [P, P], F32)
        onesf = keep("onesf", [P, P], F32)
        w2p = keep("w2p", [P, 4, C], F32)
        bias3 = keep("bias3", [3, D], BF16)
        ones3 = keep("ones3", [3, P], BF16)
        wf1 = keep("wf1", [GT * RW, GT, C], F32)
        bf1c = keep("bf1c", [P, 1], F32)
        w1s = keep("w1s", [P, 2, C], F32)
        w1v = keep("w1v", [P, 2, C], F32)
        w2s = keep("w2s", [P, C], F32)
        w2v = keep("w2v", [P, C], F32)
        w1T = keep("w1T", [P, 4, P], F32)
        w2T = keep("w2T", [P, SW], F32)
        wd1T = keep("wd1T", [P, P], F32)
        wd2T = keep("wd2T", [P, 2 * P], F32)
        wd3T = keep("wd3T", [P, 2, D], F32)
        b1c = keep("b1c", [P, 1], F32)
        b2c = keep("b2c", [P, 1], F32)
        bd1c = keep("bd1c", [P, 1], F32)
        bd2c = keep("bd2c", [P, 2], F32)
        bd3r = keep("bd3r", [P, D], F32)
        epsc = keep("epsc", [P, 1], F32)
        halfc = keep("halfc", [P, 1], F32)
        iota64 = keep("iota64", [P, SW], F32)
        iotah = keep("iotah", [P, HALF], F16)

        prologue(nc, a, locals())
        edge_loop(nc, locals())
        epilogue(nc, out, locals())


def spread(ap, axis, n):
    shape = list(ap.shape)
    shape[axis] = n
    return ap.broadcast_to(shape)


class Chain:

    def __init__(self, engine, semaphore):
        self.engine, self.semaphore, self.count = engine, semaphore, 0

    def link(self, instruction):
        self.count += 1
        instruction.then_inc(self.semaphore, 1)
        self.engine.wait_ge(self.semaphore, self.count)


def prologue(nc, a, k):
    AGG, AT, X, EIDX, FLUSH = k["AGG"], k["AT"], k["X"], k["EIDX"], k["FLUSH"]
    ident, onesf = k["ident"], k["onesf"]
    rec_dram, node_dram = k["rec_dram"], k["node_dram"]
    w2p, bias3, ones3, wf1 = k["w2p"], k["bias3"], k["ones3"], k["wf1"]
    with ExitStack() as ctx:
        def sb(name, shape, dt):
            return ctx.enter_context(nc.sbuf_tensor("sort_" + name, shape, dt))

        def ps(name, shape, dt=F32):
            return ctx.enter_context(nc.psum_tensor("sort_" + name, shape, dt))

        def sem(name):
            return ctx.enter_context(nc.semaphore("sort_" + name))

        REC = sb("REC", [EP, EC, RW], F32)
        rec0 = sb("rec0", [1, RW], F32)
        srci = sb("srci", [EP, EC], I32)
        dsti = sb("dsti", [EP, EC], I32)
        tmpi = sb("tmpi", [EP, EC], I32)
        dirs = sb("dirs", [EP, EC, 3], F32)
        rcut = sb("rcut", [EP, EC], F32)
        norm = sb("norm", [EP, EC], F32)
        gain = sb("gain", [EP, EC], F32)
        hi = sb("hi", [EP, EC], F32)
        blkf = sb("blkf", [EP, EC], F32)
        lane = sb("lane", [EP, EC], F32)
        tile = sb("tile", [EP, EC], F32)
        MASK = AT[0:EP, :, 0:EC]
        scanflat = AGG[:, :, :].rearrange("p b d -> p (b d)")[0:EP, 0:SB * EC]
        SCAN = scanflat.rearrange("p (b c) -> p b c", b=SB)
        zeros = sb("zeros", [EP, 2 * NTX], BF16)
        le = AGG[0:1, :, :].rearrange("p b d -> p (b d)")[:, 0:(NT + 1) * (SB - 1)].rearrange("p (t b) -> p t b", b=SB - 1)
        cum = sb("cum", [EP, SB], F32)
        cumx = sb("cumx", [EP, SB], F32)
        cnt = sb("cnt", [EP, SB], F32)
        adj = sb("adj", [EP, SB], F32)
        nti = sb("nti", [P, SB], I32)
        ntf = sb("ntf", [P, SB], F32)
        incl = sb("incl", [P, SB], F32)
        excl = sb("excl", [P, SB], F32)
        tcol = sb("tcol", [1, NT + 1], F32)
        blkt = sb("blkt", [1, NT + 2], F32)
        neq = sb("neq", [1, NT + 1], F32)
        bits = sb("bits", [1, NT // UN, UN], F32)
        mask = sb("mask", [1, NT // UN], F32)
        upper = sb("upper", [P, P], F32)
        iotab = sb("iotab", [P, SB], F32)
        iotal = sb("iotal", [P, P], BF16)
        iotat = sb("iotat", [P, NTX], BF16)
        colno = sb("colno", [P, EC], F32)
        partno = sb("partno", [P, 1], F32)
        RING = SORT_UNROLL
        lhot = sb("lhot", [EP, RING, P], BF16)
        thot = sb("thot", [EP, RING, 2, NTX], BF16)
        eidf = sb("eidf", [P, NTX], F32)
        win = sb("win", [P, 2, C], F32)
        w1raw = sb("w1raw", [P, D], F32)
        w2raw = sb("w2raw", [SW, P], F32)
        wd1raw = sb("wd1raw", [P, 2, SW], F32)
        wd2raw = sb("wd2raw", [P, 2, P], F32)
        wd3raw = sb("wd3raw", [P, 4, 2 * P], F32)
        wf2raw = sb("wf2raw", [P, D], F32)
        bf2r = sb("bf2r", [3, D], F32)
        bhi = sb("bhi", [3, D], BF16)
        bmid = sb("bmid", [3, D], BF16)
        bres = sb("bres", [3, D], F32)
        bsum = sb("bsum", [3, D], F32)
        stats = sb("stats", [P, NB, 6], F32)
        mv = sb("mv", [P, NB, 2], F32)
        std = sb("std", [P, NB], F32)
        rstd = sb("rstd", [P, NB], F32)
        shift = sb("shift", [P, NB], F32)
        spare = AGG[:, :, :].rearrange("p b d -> p (b d)")[:, SB * EC + EC:]
        H = spare[:, 0:2 * D].rearrange("p (i d) -> p i d", i=2)
        sq = spare[0:EP, 2 * D:2 * D + 3 * EC].rearrange("p (c i) -> p c i", i=3)
        HT = sb("HT", [P, 2, 4, P], F32)
        GS = sb("GS", [P, 2, D], F32)

        psT = ps("psT", [P, 2, D])
        psG = ps("psG", [P, 2, D])
        psW = ps("psW", [P, D])
        psC = ps("psC", [P, D])
        psE = ps("psE", [P, D])

        s_edges = sem("s_edges")
        s_attr = sem("s_attr")
        s_dirs = sem("s_dirs")
        s_x = sem("s_x")
        s_weights = sem("s_weights")
        s_raw = sem("s_raw")
        s_xzero = sem("s_xzero")
        s_const = sem("s_const")
        s_iden = sem("s_iden")
        s_rec = sem("s_rec")
        s_recs = sem("s_recs")
        s_norm2 = sem("s_norm2")
        s_norm = sem("s_norm")
        s_cnt = sem("s_cnt")
        s_tot = sem("s_tot")
        s_pos = sem("s_pos")
        s_le = sem("s_le")
        s_hot = sem("s_hot")
        s_hotfree = sem("s_hotfree")
        s_perm = sem("s_perm")
        s_eidx = sem("s_eidx")
        s_var = sem("s_var")
        s_std = sem("s_std")
        s_ln = sem("s_ln")
        s_h = sem("s_h")
        s_ht = sem("s_ht")
        s_htc = sem("s_htc")
        s_g = sem("s_g")
        s_gc = sem("s_gc")
        s_gout = [sem(f"s_gout{i}") for i in range(2)]
        s_wt = sem("s_wt")
        s_wtc = sem("s_wtc")
        s_wcast = sem("s_wcast")
        v_chain = sem("v_chain")
        p_chain = sem("p_chain")
        p_zero = sem("p_zero")
        block = ctx.enter_context(nc.Block())

        @block.sync
        def _(sp):
            sp.dma_start(srci[:, :], a["src"].rearrange("(p c) -> p c", p=EP)).then_inc(s_edges, 16)
            sp.dma_start(dsti[:, :], a["dst"].rearrange("(p c) -> p c", p=EP)).then_inc(s_edges, 16)
            sp.dma_start(dirs[:, :, :], a["edge_attr_3"].rearrange("(p c) i -> p c i", p=EP)).then_inc(s_dirs, 16)
            sp.dma_start(rcut[:, :], a["edge_weight"].rearrange("(p c) -> p c", p=EP)).then_inc(s_dirs, 16)
            sp.wait_ge(s_xzero, 1)
            sp.dma_start(X[:, 0:NB - 1, :],
                         a["x"][0:(NB - 1) * P, :].rearrange("(b p) d -> p b d", p=P)).then_inc(s_x, 16)
            sp.dma_start(X[0:LAST, NB - 1, :], a["x"][(NB - 1) * P:N, :]).then_inc(s_x, 16)
            for i, name in enumerate(("W_in2f_s", "W_in2f_v")):
                sp.dma_start(win[:, i, :], a["L0_gnn_" + name]).then_inc(s_raw, 16)
            sp.dma_start(w1raw[:, :], a["L1_gnn_W1"]).then_inc(s_raw, 16)
            sp.dma_start(w2raw[:, :], a["L1_gnn_W2"]).then_inc(s_raw, 16)
            for i in range(2):
                sp.dma_start(wd1raw[:, i, :], a["L1_gnn_Wd1"]).then_inc(s_raw, 16)
            sp.dma_start(wd2raw[:, :, :], a["L1_gnn_Wd2"].rearrange("(j p) n -> p j n", p=P)).then_inc(s_raw, 16)
            sp.dma_start(wd3raw[:, :, :], a["L1_gnn_Wd3"].rearrange("(j p) n -> p j n", p=P)).then_inc(s_raw, 16)
            sp.dma_start(wf2raw[:, :], a["L0_gnn_Wf2"][:, 0:D]).then_inc(s_raw, 16)
            for i in range(3):
                sp.dma_start(bf2r[i:i + 1, :], a["L0_gnn_bf2"][0:D].rearrange("(o n) -> o n", o=1)).then_inc(s_raw, 16)
            sp.wait_ge(s_rec, 1)
            sp.dma_start(rec_dram[1:E + 1, :].rearrange("(p c) w -> p c w", p=EP), REC[:, :, :]).then_inc(s_recs, 16)
            sp.dma_start(rec_dram[0:1, :], rec0[:, :]).then_inc(s_recs, 16)
            for b in range(NB):
                sp.wait_ge(s_gc, b + 1)
                sp.dma_start(node_dram[b * P:(b + 1) * P, :], GS[:, b % 2, :]).then_inc(s_gout[b % 2], 16)
            for i in range(2):
                sp.wait_ge(s_gout[i], 16 * (NB // 2))
            sp.wait_ge(s_recs, 32)

        @block.scalar
        def _(act):
            act.dma_start(REC[:, :, 0:RBF], a["edge_attr_20"].rearrange("(p c) w -> p c w", p=EP)).then_inc(s_attr, 16)
            n = 0
            act.wait_ge(s_xzero, 2)
            for i in range(GT):
                act.dma_start(wf1[RW * i:RW * i + RBF, i, :], a["L0_gnn_Wf1"]).then_inc(s_weights, 16)
            act.dma_start(k["bf1c"][:, :], a["L0_gnn_bf1"].rearrange("(p o) -> p o", o=1)).then_inc(s_weights, 16)
            for w, name in ((k["w1s"], "W1_s"), (k["w1v"], "W1_v")):
                act.dma_start(w[:, :, :], a["L0_gnn_" + name].rearrange("(f k) c -> f k c", k=2)).then_inc(s_weights, 16)
            for w, name in ((k["w2s"], "W2_s"), (k["w2v"], "W2_v")):
                act.dma_start(w[:, :], a["L0_gnn_" + name]).then_inc(s_weights, 16)
            act.dma_start(k["b1c"][:, :], a["L1_gnn_b1"].rearrange("(p o) -> p o", o=1)).then_inc(s_weights, 16)
            for i in range(2):
                act.dma_start(k["b2c"][SW * i:SW * i + SW, :],
                              a["L1_gnn_b2"].rearrange("(p o) -> p o", o=1)).then_inc(s_weights, 16)
            act.dma_start(k["bd1c"][:, :], a["L1_gnn_bd1"].rearrange("(p o) -> p o", o=1)).then_inc(s_weights, 16)
            for i in range(2):
                act.dma_start(k["bd2c"][:, i:i + 1],
                              a["L1_gnn_bd2"][P * i:P * i + P].rearrange("(p o) -> p o", o=1)).then_inc(s_weights, 16)
            act.dma_start(k["bd3r"][:, :], spread(a["L1_gnn_bd3"].rearrange("(o n) -> o n", o=1), 0, P)).then_inc(s_weights, 16)
            act.wait_ge(s_norm2, 1)
            act.activation(norm[:, :], gain[:, :], ACT.Sqrt).then_inc(s_norm, 1)
            act.wait_ge(s_var, 1)
            act.wait_ge(s_const, 1)
            act.activation(std[:, :], mv[:, :, 1], ACT.Sqrt, bias=k["epsc"][:, 0:1]).then_inc(s_std, 1)
            act.wait_ge(s_ln, 1)

            def normalise(b):
                if b >= 2:
                    act.wait_ge(s_ht, b - 1)
                act.activation(H[:, b % 2, :], X[:, b, :], ACT.Relu, bias=shift[:, b:b + 1],
                               scale=rstd[:, b:b + 1]).then_inc(s_h, 1)

            normalise(0)
            for b in range(NB):
                if b + 1 < NB:
                    normalise(b + 1)
                act.wait_ge(s_ht, b + 1)
                act.copy(HT[:, b % 2, :, :].rearrange("p c n -> p (c n)"), psT[:, b % 2, :]).then_inc(s_htc, 1)
                act.wait_ge(s_g, b + 1)
                if b >= 2:
                    act.wait_ge(s_gout[b % 2], 16 * (b // 2))
                act.mul(GS[:, b % 2, :], psG[:, b % 2, :], float(C) ** -0.5).then_inc(s_gc, 1)
            for n, dst in enumerate((k["w1T"][:, :, :].rearrange("p c n -> p (c n)"), None,
                                     k["wd3T"][:, 0, :], k["wd3T"][:, 1, :])):
                act.wait_ge(s_wt, n + 1)
                if dst is not None:
                    act.copy(dst, psW[:, :]).then_inc(s_wtc, 1)
                else:
                    act.copy(k["w2T"][:, :], psW[:, 0:SW])
                    act.copy(k["wd1T"][:, :], psW[:, P:2 * P])
                    act.copy(k["wd2T"][:, :], psW[:, 2 * P:4 * P]).then_inc(s_wtc, 1)
            act.wait_ge(s_weights, 16 * 15)

        @block.gpsimd
        def _(pool):
            chain = Chain(pool, p_chain)
            pool.memset(X[:, NB - 1, :], 0.0).then_inc(s_xzero, 1)
            pool.memset(wf1[:, :, :], 0.0).then_inc(s_xzero, 1)
            pool.memset(k["epsc"][:, :], EPS)
            pool.memset(k["halfc"][:, :], 0.5)
            pool.memset(zeros[:, :], 0.0)
            pool.memset(ones3[:, :], 1.0)
            pool.memset(REC[:, :, DST + 1:RW], 0.0)
            chain.link(pool.memset(rec0[:, :], 0.0))
            chain.link(pool.memset(rec0[:, SRCL:KEYD + 1], NOBODY))
            pool.iota(iotab[:, :], [[1, SB]], base=0, channel_multiplier=0, allow_small_or_imprecise_dtypes=True)
            pool.iota(iotal[:, :], [[1, P]], base=0, channel_multiplier=0, allow_small_or_imprecise_dtypes=True)
            pool.iota(iotat[:, :], [[1, NTX]], base=0, channel_multiplier=0, allow_small_or_imprecise_dtypes=True)
            pool.iota(colno[:, :], [[1, EC]], base=1, channel_multiplier=0, allow_small_or_imprecise_dtypes=True)
            pool.iota(partno[:, :], [[0, 1]], base=0, channel_multiplier=1, allow_small_or_imprecise_dtypes=True)
            pool.iota(tcol[:, :], [[1, NT + 1]], base=0, channel_multiplier=0, allow_small_or_imprecise_dtypes=True)
            pool.iota(k["iota64"][:, :], [[1, SW]], base=0, channel_multiplier=0, allow_small_or_imprecise_dtypes=True)
            pool.iota(k["iotah"][:, :], [[1, HALF]], base=0, channel_multiplier=0, allow_small_or_imprecise_dtypes=True)
            chain.link(pool.memset(onesf[:, :], 1.0))
            chain.link(pool.affine_select(out=ident[:, :], in_=onesf[:, :], compare_op=ALU.is_equal, fill=0.0, base=0,
                                          pattern=[[-1, P]], channel_multiplier=1))
            pool.affine_select(out=upper[:, :], in_=onesf[:, :], compare_op=ALU.is_ge, fill=0.0, base=-1,
                               pattern=[[1, P]], channel_multiplier=-1).then_inc(s_const, 1)
            pool.wait_ge(s_const, 1)
            pool.sem_inc(s_iden, 1)
            pool.wait_ge(s_pos, 1)
            pool.memset(AT[:, :, :], 0.0).then_inc(p_zero, 1)
            pool.wait_ge(s_le, 1)
            pool.wait_ge(s_ht, NB)
            pool.memset(AGG[:, :, :], 0.0).then_inc(p_zero, 1)
            pool.wait_ge(p_zero, 2)

        @block.vector
        def _(dve):
            chain = Chain(dve, v_chain)
            link = chain.link
            dve.wait_ge(s_edges, 32)
            link(dve.tensor_scalar(tmpi[:, :], srci[:, :], 6, None, ALU.logical_shift_right))
            link(dve.tensor_copy(blkf[:, :], tmpi[:, :]))
            link(dve.tensor_scalar(tmpi[:, :], srci[:, :], SW - 1, None, ALU.bitwise_and))
            dve.tensor_scalar(hi[:, :], dsti[:, :], float(HALF), None, ALU.is_ge).then_inc(v_chain, 1)
            chain.count += 1
            dve.tensor_copy(REC[:, :, SRCL], tmpi[:, :]).then_inc(v_chain, 1)
            chain.count += 1
            link(dve.tensor_copy(REC[:, :, DST].bitcast(U32), dsti[:, :]))
            dve.scalar_tensor_tensor(out=REC[:, :, KEYS], in0=hi[:, :], scalar=float(SW), in1=REC[:, :, SRCL],
                                     op0=ALU.mult, op1=ALU.add)
            dve.scalar_tensor_tensor(out=REC[:, :, KEYD], in0=hi[:, :], scalar=-float(HALF), in1=dsti[:, :],
                                     op0=ALU.mult, op1=ALU.add)
            dve.wait_ge(s_iden, 1)
            link(dve.tensor_tensor(MASK, spread(blkf[:, :].rearrange("p (o c) -> p o c", o=1), 1, SB),
                                   spread(iotab[0:EP, :].rearrange("p (b o) -> p b o", o=1), 2, EC), ALU.is_equal))
            link(dve.tensor_copy(SCAN, MASK))
            link(dve.tensor_tensor_scan(scanflat, scanflat, spread(zeros[:, 0:1], 1, SB * EC), 0.0, ALU.add, ALU.add))
            link(dve.tensor_copy(cum[:, :], SCAN[:, :, EC - 1]))
            link(dve.memset(cumx[:, 0:1], 0.0))
            link(dve.tensor_copy(cumx[:, 1:SB], cum[:, 0:SB - 1]))
            dve.tensor_tensor(cnt[:, :], cum[:, :], cumx[:, :], ALU.subtract).then_inc(s_cnt, 1)
            dve.wait_ge(s_x, 32)
            for b in range(NB):
                bn = dve.bn_stats(stats[:, b, :], X[:, b, :])
            link(bn)
            for b in range(NB):
                bn = dve.bn_aggr(mv[:, b, :], stats[:, b, :])
            bn.then_inc(s_var, 1)
            dve.wait_ge(s_dirs, 32)
            link(dve.tensor_tensor(sq, dirs[:, :, :], dirs[:, :, :], ALU.mult))
            dve.tensor_reduce(gain[:, :], sq, AX_X, ALU.add).then_inc(s_norm2, 1)
            dve.wait_ge(s_tot, 1)
            link(dve.tensor_scalar(nti[:, :], psC[:, SB:2 * SB], float(P - 1), None, ALU.add))
            link(dve.tensor_scalar(nti[:, :], nti[:, :], 7, None, ALU.logical_shift_right))
            link(dve.tensor_copy(ntf[:, :], nti[:, :]))
            link(dve.tensor_tensor_scan(incl[:, :], ntf[:, :], onesf[:, 0:SB], 0.0, ALU.add, ALU.mult))
            link(dve.tensor_tensor(excl[:, :], incl[:, :], ntf[:, :], ALU.subtract))
            link(dve.tensor_tensor(adj[:, :], psC[0:EP, 0:SB], cumx[:, :], ALU.subtract))
            link(dve.scalar_tensor_tensor(out=adj[:, :], in0=excl[0:EP, :], scalar=float(P), in1=adj[:, :],
                                          op0=ALU.mult, op1=ALU.add))
            link(dve.tensor_tensor(SCAN, SCAN,
                                   spread(adj[:, :].rearrange("p (b o) -> p b o", o=1), 2, EC), ALU.add))
            link(dve.tensor_tensor(SCAN, SCAN, MASK, ALU.mult))
            link(dve.tensor_reduce(lane[:, :], SCAN.rearrange("p b c -> p c b"), AX_X, ALU.add))
            link(dve.tensor_scalar(tmpi[:, :], lane[:, :], -1.0, None, ALU.add))
            link(dve.tensor_scalar(dsti[:, :], tmpi[:, :], 7, None, ALU.logical_shift_right))
            link(dve.tensor_copy(tile[:, :], dsti[:, :]))
            link(dve.tensor_scalar(tmpi[:, :], tmpi[:, :], P - 1, None, ALU.bitwise_and))
            dve.tensor_copy(lane[:, :], tmpi[:, :]).then_inc(s_pos, 1)
            dve.wait_ge(s_pos, 1)
            dve.wait_ge(s_norm, 1)
            link(dve.reciprocal(norm[:, :], norm[:, :]))
            link(dve.scalar_tensor_tensor(out=gain[:, :], in0=norm[:, :], scalar=Y1, in1=rcut[:, :],
                                          op0=ALU.mult, op1=ALU.mult))
            dve.wait_ge(s_attr, 16)
            for i in range(3):
                link(dve.tensor_tensor(REC[:, :, CO + 1 + i], dirs[:, :, i], gain[:, :], ALU.mult))
            dve.tensor_scalar(REC[:, :, CO], rcut[:, :], Y0, None, ALU.mult).then_inc(s_rec, 1)
            dve.wait_ge(s_std, 1)
            link(dve.reciprocal(rstd[:, :], std[:, :]))
            dve.scalar_tensor_tensor(out=shift[:, :], in0=mv[:, :, 0], scalar=-1.0, in1=rstd[:, :],
                                     op0=ALU.mult, op1=ALU.mult).then_inc(s_ln, 1)
            link(dve.tensor_tensor(le, spread(tcol[:, :].rearrange("p (t o) -> p t o", o=1), 2, SB - 1),
                                   spread(incl[0:1, 0:SB - 1].rearrange("p (o b) -> p o b", o=1), 1, NT + 1), ALU.is_ge))
            link(dve.tensor_reduce(blkt[:, 1:NT + 2], le, AX_X, ALU.add))
            dve.sem_inc(s_le, 1)
            link(dve.tensor_scalar(blkt[:, 0:1], blkt[:, 1:2], 0.0, None, ALU.add))
            link(dve.memset(blkt[:, NT + 1:NT + 2], float(SB)))
            link(dve.tensor_tensor(neq[:, :], blkt[:, 0:NT + 1], blkt[:, 1:NT + 2], ALU.not_equal))
            for u in range(UN):
                last = dve.tensor_scalar(bits[:, :, u], neq[:, 0:NT].rearrange("p (i u) -> p i u", u=UN)[:, :, u],
                                         float(1 << u), None, ALU.mult)
            link(last)
            link(dve.tensor_reduce(mask[:, :], bits[:, :, :], AX_X, ALU.add))
            dve.tensor_copy(FLUSH[:, :], mask[:, :])
            dve.tensor_copy(k["BLOCK"][:, :], blkt[:, 0:NT + 1])
            dve.wait_ge(s_raw, 16 * 12)
            dve.tensor_copy(w2p[:, :, :].rearrange("p (k h) f -> p h f k", k=2),
                            wf2raw[:, :].rearrange("p (h f k) -> p h f k", h=2, k=2))
            link(dve.tensor_copy(bsum[:, :].rearrange("p (k h f) -> p h f k", k=2, h=2),
                                 bf2r[:, :].rearrange("p (h f k) -> p h f k", h=2, k=2)))
            link(dve.tensor_copy(bhi[:, :], bsum[:, :]))
            link(dve.tensor_tensor(bres[:, :], bsum[:, :], bhi[:, :], ALU.subtract))
            link(dve.tensor_copy(bmid[:, :], bres[:, :]))
            link(dve.tensor_tensor(bres[:, :], bres[:, :], bmid[:, :], ALU.subtract))
            link(dve.tensor_scalar(bsum[:, :], bhi[:, :], ident[0:3, 0:1], None, ALU.mult))
            link(dve.scalar_tensor_tensor(out=bsum[:, :], in0=bmid[:, :], scalar=ident[0:3, 1:2], in1=bsum[:, :],
                                          op0=ALU.mult, op1=ALU.add))
            link(dve.scalar_tensor_tensor(out=bias3[:, :], in0=bres[:, :], scalar=ident[0:3, 2:3], in1=bsum[:, :],
                                          op0=ALU.mult, op1=ALU.add))
            dve.wait_ge(s_weights, 16 * 15)
            dve.tensor_scalar(k["w1s"][:, 0, :], k["w1s"][:, 0, :], float(2 * C) ** -0.5, None, ALU.mult)
            dve.tensor_scalar(k["w1s"][:, 1, :], k["w1s"][:, 1, :], float(6 * C) ** -0.5, None, ALU.mult)
            dve.tensor_scalar(k["w1v"][:, :, :], k["w1v"][:, :, :], float(2 * C) ** -0.5, None, ALU.mult)
            dve.tensor_scalar(k["w2s"][:, :], k["w2s"][:, :], float(C) ** -0.5, None, ALU.mult)
            link(dve.tensor_scalar(k["w2v"][:, :], k["w2v"][:, :], float(C) ** -0.5, None, ALU.mult))
            with dve.Fori(0, EC // SORT_UNROLL) as i:
                for u in range(SORT_UNROLL):
                    c = SORT_UNROLL * i + u
                    r = u
                    if u % (RING // 2) == 0:
                        dve.wait_ge(s_hotfree, 2 * i + u // (RING // 2) + 1)
                    dve.tensor_scalar(lhot[:, r, :], iotal[0:EP, :], lane[:, bass.ds(c, 1)], None, ALU.is_equal)
                    dve.tensor_scalar(thot[:, r, 0, :], iotat[0:EP, :], tile[:, bass.ds(c, 1)], partno[0:EP, :],
                                      ALU.is_equal, ALU.mult)
                    dve.tensor_scalar(thot[:, r, 1, :], iotat[0:EP, :], tile[:, bass.ds(c, 1)],
                                      colno[0:EP, bass.ds(c, 1)], ALU.is_equal, ALU.mult).then_inc(s_hot, 1)
            dve.wait_ge(s_perm, 1)
            link(dve.tensor_scalar(eidf[:, :], psE[:, 0:NTX], float(EC), None, ALU.mult))
            link(dve.tensor_tensor(EIDX[:, :], psE[:, NTX:2 * NTX], eidf[:, :], ALU.add))

        @block.tensor
        def _(pe):
            pe.wait_ge(s_cnt, 1)
            pe.wait_ge(s_iden, 1)
            pe.matmul(psC[0:EP, 0:SB], upper[0:EP, 0:EP], cnt[:, :], start=True, stop=True)
            pe.matmul(psC[:, SB:2 * SB], onesf[0:EP, :], cnt[:, :], start=True, stop=True).then_inc(s_tot, 1)

            def transposes(b):
                pe.wait_ge(s_h, b + 1)
                if b >= 2:
                    pe.wait_ge(s_htc, b - 1)
                h = H[:, b % 2, :]
                hv = h[:, C:D].rearrange("p (c i) -> p i c", i=3)
                pe.transpose(psT[:, b % 2, 0:P], h[:, 0:C], ident[:, :])
                for i in range(3):
                    last = pe.transpose(psT[:, b % 2, P * (i + 1):P * (i + 2)], hv[:, i, :], ident[:, :])
                last.then_inc(s_ht, 1)

            pe.wait_ge(s_raw, 16 * 12)
            transposes(0)
            for b in range(NB):
                if b + 1 < NB:
                    transposes(b + 1)
                pe.wait_ge(s_htc, b + 1)
                if b >= 2:
                    pe.wait_ge(s_gc, b - 1)
                for c in range(4):
                    last = pe.matmul(psG[:, b % 2, P * c:P * (c + 1)], HT[:, b % 2, c, :], win[:, min(c, 1), :],
                                     start=True, stop=True)
                last.then_inc(s_g, 1)
            wd1v = wd1raw[:, :, :].rearrange("p i n -> p (i n)")
            jobs = [
                [(w1raw[:, P * j:P * j + P], P * j, P) for j in range(4)],
                [(w2raw[:, :], 0, SW), (wd1v, P, P), (wd2raw[:, 0, :], 2 * P, P), (wd2raw[:, 1, :], 3 * P, P)],
                [(wd3raw[:, j, 0:P], P * j, P) for j in range(4)],
                [(wd3raw[:, j, P:2 * P], P * j, P) for j in range(4)],
            ]
            for n, job in enumerate(jobs):
                if n:
                    pe.wait_ge(s_wtc, n)
                for src, at, rows in job:
                    last = pe.transpose(psW[:, at:at + rows], src, ident[0:rows, 0:rows])
                last.then_inc(s_wt, 1)
            pe.matmul(psE[:, 0:2 * NTX], zeros[0:1, 0:P], zeros[0:1, 0:2 * NTX], start=True, stop=False,
                      skip_group_check=True).then_inc(s_hotfree, 2)
            with pe.Fori(0, EC // SORT_UNROLL) as i:
                for u in range(SORT_UNROLL):
                    r = u
                    pe.wait_ge(s_hot, SORT_UNROLL * i + u + 1)
                    mm = pe.matmul(psE[:, 0:2 * NTX], lhot[:, r, :], thot[:, r, :, :].rearrange("p k t -> p (k t)"),
                                   start=False, stop=False, skip_group_check=True)
                    if (r + 1) % (RING // 2) == 0:
                        mm.then_inc(s_hotfree, 1)
            pe.matmul(psE[:, 0:2 * NTX], zeros[0:1, 0:P], zeros[0:1, 0:2 * NTX], start=False, stop=True,
                      skip_group_check=True).then_inc(s_perm, 1)


def edge_loop(nc, k):
    AGG, AT, EIDX, FLUSH, BLOCK = k["AGG"], k["AT"], k["EIDX"], k["FLUSH"], k["BLOCK"]
    ident, w2p, bias3, ones3, wf1, bf1c = k["ident"], k["w2p"], k["bias3"], k["ones3"], k["wf1"], k["bf1c"]
    halfc, iota64, iotah = k["halfc"], k["iota64"], k["iotah"]
    rec_dram, node_dram = k["rec_dram"], k["node_dram"]
    with ExitStack() as ctx:
        def sb(name, shape, dt):
            return ctx.enter_context(nc.sbuf_tensor("loop_" + name, shape, dt))

        def ps(name, shape, dt=F32):
            return ctx.enter_context(nc.psum_tensor("loop_" + name, shape, dt))

        def sem(name):
            return ctx.enter_context(nc.semaphore("loop_" + name))

        stage = sb("stage", [P, 2, GT], U32)
        rec = sb("rec", [P, 2, GT, RW], F32)
        node = sb("node", [P, 2, GT, D], F32)
        fT = sb("fT", [GT * RW, P], F32)
        absz = sb("absz", [P, GT * P], F32)
        expz = sb("expz", [P, GT * P], F32)
        logz = sb("logz", [P, GT * P], F32)
        relz = sb("relz", [P, GT * P], F32)
        h = sb("h", [P, 2, GT * P], F32)
        hot = sb("hot", [P, 2, GT, SW], F32)
        shot = sb("shot", [P, 2, GT, 4, SW], F32)
        khot = sb("khot", [P, 2, GT, P], BF16)
        dhot = sb("dhot", [P, 2, GT, HALF], BF16)
        prod = sb("prod", [P, 2, 8, C], F32)
        zrow = sb("zrow", [1, D], BF16)

        psW = ps("psW", [P, 2, D])
        psZ = ps("psZ", [P, D])
        psF = ps("psF", [P, D])
        psA = ps("psA", [P, D])
        psN = ps("psN", [P, 2, D])

        staged = sem("staged")
        rec_in = [sem(f"rec_in{q}") for q in range(2)]
        node_in = [sem(f"node_in{q}") for q in range(2)]
        rec_turned = sem("rec_turned")
        fT_ready = sem("fT_ready")
        z_ready = sem("z_ready")
        z_used = sem("z_used")
        abs_done = sem("abs_done")
        exp_done = sem("exp_done")
        soft_done = sem("soft_done")
        h_ready = sem("h_ready")
        hot_ready = sem("hot_ready")
        keys_ready = sem("keys_ready")
        shot_ready = sem("shot_ready")
        w_ready = sem("w_ready")
        prod_done = sem("prod_done")
        summed = sem("summed")
        copied = sem("copied")
        flushed = sem("flushed")
        zeroed = sem("zeroed")
        pool_turn = sem("pool_turn")
        block = ctx.enter_context(nc.Block())

        @block.gpsimd
        def _(pool):
            def gather_rec(q):
                for j in range(GT):
                    pool.indirect_dma_start(out=rec[:, q, j, :], out_offset=None, in_=rec_dram,
                                            in_offset=bass.IndirectOffsetOnAxis(ap=stage[:, q, j:j + 1], axis=0)
                                            ).then_inc(rec_in[q], 16)

            def gather_node(q):
                for j in range(GT):
                    pool.indirect_dma_start(out=node[:, q, j, :], out_offset=None, in_=node_dram,
                                            in_offset=bass.IndirectOffsetOnAxis(
                                                ap=rec[:, q, j, DST:DST + 1].bitcast(U32), axis=0)
                                            ).then_inc(node_in[q], 16)

            pool.wait_ge(staged, 1)
            gather_rec(0)
            pool.wait_ge(staged, 2)
            gather_rec(1)
            pool.wait_ge(rec_in[0], 16 * GT)
            gather_node(0)
            with pool.Fori(0, GROUPS // 2) as i:
                for q in range(2):
                    s = 2 * i + q
                    pool.wait_ge(staged, s + 3)
                    pool.wait_ge(keys_ready, s + 1)
                    pool.wait_ge(shot_ready, s + 1)
                    pool.wait_ge(rec_turned, s + 1)
                    pool.wait_ge(node_in[q], 16 * GT * (i + 1))
                    pool.sem_inc(pool_turn, 1)
                    gather_rec(q)
                    pool.wait_ge(rec_in[1 - q], 16 * GT * (i + 1 + q))
                    pool.wait_ge(prod_done, GT * s + 1)
                    pool.sem_inc(pool_turn, 1)
                    gather_node(1 - q)
            for q in range(2):
                pool.wait_ge(rec_in[q], 16 * GT * (GROUPS // 2 + 1))
            pool.wait_ge(node_in[0], 16 * GT * (GROUPS // 2 + 1))

        @block.scalar
        def _(act):
            def attributes():
                for j in range(GT):
                    rows = slice(RW * j, RW * j + RBF)
                    last = act.copy(fT[rows, :], psF[rows, 0:P])
                last.then_inc(fT_ready, 1)

            def soften(n):
                act.wait_ge(z_ready, n + 1)
                act.wait_ge(h_ready, n + 1)
                act.activation(absz[:, :], psZ[:, 0:GT * P], ACT.Abs, bias=bf1c[:, 0:1]).then_inc(abs_done, 1)
                act.activation(relz[:, :], psZ[:, 0:GT * P], ACT.Relu, bias=bf1c[:, 0:1]).then_inc(z_used, 1)
                act.wait_ge(abs_done, n + 1)
                act.activation(expz[:, :], absz[:, :], ACT.Exp, scale=-1.0).then_inc(exp_done, 1)
                act.wait_ge(exp_done, n + 1)
                act.activation(logz[:, :], expz[:, :], ACT.Ln, bias=halfc[:, 0:1], scale=0.5).then_inc(soft_done, 1)

            def factors(q, n):
                act.wait_ge(hot_ready, n + 1)
                for j in range(GT):
                    for c in range(4):
                        last = act.activation(shot[:, q, j, c, :], hot[:, q, j, :], ACT.Copy,
                                              scale=rec[:, q, j, CO + c:CO + c + 1])
                last.then_inc(shot_ready, 1)

            act.preload_act_table_set("natural_log_exp_and_others")
            act.wait_ge(zeroed, 2)
            act.wait_ge(rec_turned, 1)
            attributes()
            soften(0)
            factors(0, 0)
            act.wait_ge(rec_turned, 2)
            act.wait_ge(z_ready, 1)
            attributes()
            with act.Fori(0, GROUPS // 2) as i:
                for q in range(2):
                    s = 2 * i + q
                    soften(s + 1)
                    act.wait_ge(summed, GT * s + 1)
                    factors(1 - q, s + 1)
                    act.wait_ge(rec_turned, s + 3)
                    attributes()

        @block.vector
        def _(dve):
            def number(q, n):
                dve.tensor_copy(stage[:, q, :], EIDX[:, bass.ds(GT * n, GT)]).then_inc(staged, 1)

            def hots(q, n):
                dve.tensor_tensor(hot[:, q, :, :], spread(iota64[:, :].rearrange("p (o w) -> p o w", o=1), 1, GT),
                                  spread(rec[:, q, :, SRCL:SRCL + 1], 2, SW), ALU.is_equal).then_inc(hot_ready, 1)

            def keys(q):
                for j in range(GT):
                    dve.tensor_scalar(khot[:, q, j, :], iotah[:, 0:P], rec[:, q, j, KEYS:KEYS + 1], None, ALU.is_equal)
                    last = dve.tensor_scalar(dhot[:, q, j, :], iotah[:, :], rec[:, q, j, KEYD:KEYD + 1], None,
                                             ALU.is_equal)
                last.then_inc(keys_ready, 1)

            def hidden(q, n, free=None):
                dve.wait_ge(soft_done, n + 1)
                dve.wait_ge(z_used, n + 1)
                dve.tensor_tensor(h[:, q, :], relz[:, :], logz[:, :], ALU.add).then_inc(h_ready, 1)

            def products(q, j, r):
                xs = spread(node[:, q, j, 0:C].rearrange("p (o f) -> p o f", o=1), 1, 2)
                dve.tensor_tensor(prod[:, r, 0:2, :], psW[:, r, 0:2 * C].rearrange("p (k f) -> p k f", k=2), xs, ALU.mult)
                xv = spread(node[:, q, j, C:D].rearrange("p (i o f) -> p i o f", i=3, o=1), 2, 2)
                wv = spread(psW[:, r, 2 * C:4 * C].rearrange("p (o k f) -> p o k f", o=1, k=2), 1, 3)
                dve.tensor_tensor(prod[:, r, 2:8, :].rearrange("p (i k) f -> p i k f", k=2), wv, xv,
                                  ALU.mult).then_inc(prod_done, 1)

            def empty(t):
                b = dve.value_load(BLOCK[0:1, bass.ds(t, 1)], min_val=0, max_val=SB - 1)
                dve.tensor_copy(AGG[:, bass.ds(b, 1), :].rearrange("p o d -> p (o d)"), psA[:, :])
                dve.tensor_copy(AT[:, bass.ds(b, 1), 0:D].rearrange("p o d -> p (o d)"), psN[:, 0, :])
                dve.tensor_copy(AT[:, bass.ds(b, 1), D:HALF].rearrange("p o d -> p (o d)"),
                                psN[:, 1, 0:HALF - D]).then_inc(copied, 1)
                dve.wait_ge(copied, t + 1)
                dve.memset(psA[:, :], 0.0)
                dve.memset(psN[:, 0, :], 0.0)
                dve.memset(psN[:, 1, 0:HALF - D], 0.0).then_inc(flushed, 1)

            def flush(t, ended):
                dve.wait_ge(summed, t + 1)
                with dve.If(ended > 0):
                    empty(t)
                with dve.Else():
                    dve.sem_inc(copied, 1)
                    dve.sem_inc(flushed, 1)

            dve.memset(zrow[:, :], 0.0).then_inc(zeroed, 1)
            dve.memset(fT[:, :], 0.0).then_inc(zeroed, 1)
            number(0, 0)
            number(1, 1)
            dve.sem_inc(prod_done, 1)
            dve.sem_inc(h_ready, 1)
            dve.wait_ge(rec_in[0], 16 * GT)
            number(0, 2)
            hots(0, 0)
            keys(0)
            hidden(0, 0)
            with dve.Fori(0, GROUPS // 2) as i:
                for q in range(2):
                    s = 2 * i + q
                    for j in range(GT):
                        u = GT * q + j
                        t = UN * i + u
                        if u == 0:
                            ends = dve.value_load(FLUSH[0:1, bass.ds(i, 1)], min_val=0, max_val=(1 << UN) - 1)
                        if j == 0:
                            dve.wait_ge(node_in[q], 16 * GT * (i + 1))
                        dve.wait_ge(w_ready, t + 1)
                        products(q, j, u % 2)
                        if j == 0:
                            dve.wait_ge(rec_in[1 - q], 16 * GT * (i + 1 + q))
                            dve.wait_ge(shot_ready, s + 1)
                            hots(1 - q, s + 1)
                            number(1 - q, s + 3)
                        if j == 1:
                            keys(1 - q)
                            hidden(1 - q, s + 1)
                        flush(t, (ends >> u) & 1)
            dve.wait_ge(summed, NT + 1)
            empty(NT)

        @block.tensor
        def _(pe):
            def turn(q):
                pe.transpose(psF[0:GT * RW, 0:P], rec[:, q, :, :].rearrange("p j w -> p (j w)"),
                             ident[:, :]).then_inc(rec_turned, 1)

            def z():
                for j in range(GT):
                    last = pe.matmul(psZ[:, P * j:P * (j + 1)], wf1[:, j, :], fT[:, :], start=True, stop=True)
                last.then_inc(z_ready, 1)

            def filter_(q, j, r):
                pe.matmul(psW[:, r, :], ones3[:, :], bias3[:, :], start=True, stop=False)
                pe.matmul(psW[:, r, :], h[:, q, P * j:P * (j + 1)], w2p[:, :, :].rearrange("p k f -> p (k f)"),
                          start=False, stop=True).then_inc(w_ready, 1)

            def open_sums(start, stop):
                pe.matmul(psA[:, :], zrow[:, 0:P], zrow[:, :], start=start, stop=stop, skip_group_check=True)
                pe.matmul(psN[:, 0, :], zrow[:, 0:P], zrow[:, :], start=start, stop=stop, skip_group_check=True)
                return pe.matmul(psN[:, 1, 0:HALF - D], zrow[:, 0:P], zrow[:, 0:HALF - D], start=start, stop=stop,
                                 skip_group_check=True)

            def add(dst, left, right):
                return pe.matmul(dst, left, right, start=False, stop=False, skip_group_check=True)

            def sums(q, j, r):
                def to(kind):
                    return psA[:, SW * kind:SW * (kind + 1)]

                add(to(0), prod[:, r, 0, :], shot[:, q, j, 0, :])
                for i in range(3):
                    add(to(2 + i), prod[:, r, 1, :], shot[:, q, j, 1 + i, :])
                for i in range(3):
                    add(to(1), prod[:, r, 2 + 2 * i, :], shot[:, q, j, 1 + i, :])
                    add(to(5 + i), prod[:, r, 3 + 2 * i, :], shot[:, q, j, 0, :])
                add(psN[:, 0, :], khot[:, q, j, :], dhot[:, q, j, 0:D])
                add(psN[:, 1, 0:HALF - D], khot[:, q, j, :], dhot[:, q, j, D:HALF]).then_inc(summed, 1)

            pe.wait_ge(zeroed, 2)
            open_sums(True, False).then_inc(summed, 1)
            pe.wait_ge(rec_in[0], 16 * GT)
            turn(0)
            pe.wait_ge(fT_ready, 1)
            z()
            pe.wait_ge(rec_in[1], 16 * GT)
            turn(1)
            pe.wait_ge(h_ready, 2)
            filter_(0, 0, 0)
            with pe.Fori(0, GROUPS // 2) as i:
                for q in range(2):
                    s = 2 * i + q
                    for j in range(GT):
                        u = GT * q + j
                        t = UN * i + u
                        if j == 0:
                            pe.wait_ge(fT_ready, s + 2)
                            pe.wait_ge(z_used, s + 1)
                            z()
                        if j == GT - 1:
                            pe.wait_ge(h_ready, s + 3)
                        pe.wait_ge(prod_done, t + 1)
                        filter_(q if j < GT - 1 else 1 - q, (j + 1) % GT, (u + 1) % 2)
                        if j == 0:
                            pe.wait_ge(keys_ready, s + 1)
                            pe.wait_ge(shot_ready, s + 1)
                        pe.wait_ge(prod_done, t + 2)
                        pe.wait_ge(flushed, t + 1)
                        sums(q, j, u % 2)
                        if j == GT - 1:
                            pe.wait_ge(rec_in[q], 16 * GT * (i + 2))
                            pe.wait_ge(fT_ready, s + 2)
                            turn(q)
            pe.wait_ge(flushed, NT + 1)
            open_sums(False, True)


def epilogue(nc, out, k):
    AGG, AT, X, ident, onesf = k["AGG"], k["AT"], k["X"], k["ident"], k["onesf"]
    w1s, w1v, w2s, w2v = k["w1s"], k["w1v"], k["w2s"], k["w2v"]
    w1T, w2T, wd1T, wd2T, wd3T = k["w1T"], k["w2T"], k["wd1T"], k["wd2T"], k["wd3T"]
    b1c, b2c, bd1c, bd2c, bd3r, epsc, halfc = (k[n] for n in ("b1c", "b2c", "bd1c", "bd2c", "bd3r", "epsc", "halfc"))
    COLS = [(0, 512), (512, 512), (1024, 256)]
    HCOLS = [(0, 512), (512, HALF - 512)]
    with ExitStack() as ctx:
        def sb(name, shape, dt):
            return ctx.enter_context(nc.sbuf_tensor("end_" + name, shape, dt))

        def ps(name, shape, dt=F32):
            return ctx.enter_context(nc.psum_tensor("end_" + name, shape, dt))

        def sem(name):
            return ctx.enter_context(nc.semaphore("end_" + name))

        ST = sb("ST", [P, NPAD], F32)
        VT = sb("VT", [P, 3, NPAD], F32)
        absS = sb("absS", [P, NPAD], F32)
        relS = sb("relS", [P, NPAD], F32)
        stats = sb("stats2", [P, NB, 6], F32)
        mv = sb("mv2", [P, NB, 2], F32)
        std = sb("std2", [P, NB], F32)
        rstd = sb("rstd2", [P, NB], F32)
        shift = sb("shift2", [P, NB], F32)
        H = sb("H2", [P, 2, D], F32)
        dsum = sb("dsum", [P, HALF], F32)
        dinv = sb("dinv", [P, NPAD], F32)
        dcol = sb("dcol", [P, NB], F32)
        N1 = sb("N1", [P, NB, P], F32)
        N2 = sb("N2", [P, NB, SW], F32)
        YO = sb("YO", [P, 2, D], F32)
        agg = AGG[:, :, :].rearrange("p b d -> p (b d)")
        HT = agg[:, 0:4 * NPAD].rearrange("p (c n) -> p c n", c=4)
        G1 = agg[:, 4 * NPAD:6 * NPAD].rearrange("p (b f) -> p b f", b=SB)
        G2 = agg[:, 6 * NPAD:8 * NPAD].rearrange("p (b f) -> p b f", b=SB)
        vt = VT[:, :, :].rearrange("p i n -> p (i n)")
        Y2T = vt[:, 0:2 * NPAD].rearrange("p (m n) -> p m n", m=2)
        Y1T = vt[:, 2 * NPAD:3 * NPAD]
        H1T = ST[:, :]
        Z = absS[:, 0:HALF]
        SC = relS[:, :]

        psA = [ps(f"psA{i}", [P, D]) for i in range(4)]
        psB = [ps(f"psB{i}", [P, D]) for i in range(4)]

        mm1 = sem("mm1")
        ev1 = sem("ev1")
        softS = sem("softS")
        a_chain = sem("a_chain")
        v_chain = sem("v_chain2")
        mm2 = sem("mm2")
        x_new = sem("x_new")
        var_ok = sem("var_ok")
        std_ok = sem("std_ok")
        ln_ok = sem("ln_ok")
        h_ok = sem("h_ok")
        tr = sem("tr")
        trc = sem("trc")
        deg_ok = sem("deg_ok")
        deg_mm = sem("deg_mm")
        sqrt_ok = sem("sqrt_ok")
        dinv_ok = sem("dinv_ok")
        col_mm = sem("col_mm")
        col_ok = sem("col_ok")
        g1m = sem("g1m")
        g1c = sem("g1c")
        g1d = sem("g1d")
        g2d = sem("g2d")
        l1m = sem("l1m")
        l1v = sem("l1v")
        l1c = sem("l1c")
        g2z = sem("g2z")
        g2m = sem("g2m")
        g2c = sem("g2c")
        l2m = sem("l2m")
        l2v = sem("l2v")
        zc = sem("zc")
        y1m = sem("y1m")
        y1c = sem("y1c")
        y2m = sem("y2m")
        y2c = sem("y2c")
        y3m = sem("y3m")
        y3c = sem("y3c")
        s_out = [sem(f"s_out{i}") for i in range(2)]
        block = ctx.enter_context(nc.Block())

        @block.sync
        def _(sp):
            sp.wait_ge(g1c, NB)
            for par in range(2):
                for hf in range(2):
                    sp.dma_start(G1[SW * hf:SW * hf + SW, par::2, :], N1[SW * par:SW * par + SW, :, :]).then_inc(g1d, 16)
            sp.wait_ge(g2z, 1)
            sp.wait_ge(g2c, NB)
            for par in range(2):
                for hf in range(2):
                    sp.dma_start(G2[SW * hf:SW * hf + SW, par::2, SW * hf:SW * hf + SW],
                                 N2[SW * par:SW * par + SW, :, :]).then_inc(g2d, 16)
            for b in range(NB):
                sp.wait_ge(y3c, b + 1)
                rows = P if b < NB - 1 else LAST
                sp.dma_start(out[b * P:b * P + rows, :], YO[0:rows, b % 2, :]).then_inc(s_out[b % 2], 16)
            for i in range(2):
                sp.wait_ge(s_out[i], 16 * (NB // 2))

        @block.gpsimd
        def _(pool):
            pool.wait_ge(mm1, 12)
            pool.memset(G2, 0.0).then_inc(g2z, 1)

        @block.tensor
        def _(pe):
            def sums(kind, c0, n):
                return AGG[:, c0 // SW:(c0 + n) // SW, SW * kind:SW * (kind + 1)]

            n = 0
            for c0, w in COLS:
                for o in range(4):
                    if n >= 4:
                        pe.wait_ge(ev1, n - 3)
                    left = w1s if o == 0 else w1v
                    even, odd = (0, 1) if o == 0 else (1 + o, 4 + o)
                    pe.matmul(psA[n % 4][:, 0:w], left[:, 0, :], sums(even, c0, w), start=True, stop=False)
                    pe.matmul(psA[n % 4][:, 0:w], left[:, 1, :], sums(odd, c0, w), start=False, stop=True).then_inc(mm1, 1)
                    n += 1
            pe.wait_ge(ev1, 12)
            pe.wait_ge(deg_ok, 1)
            for hf in range(2):
                for m, (c0, w) in enumerate(HCOLS):
                    last = pe.matmul(psA[2 * hf + m][:, 0:w], onesf[SW * hf:SW * hf + SW, :],
                                     dsum[SW * hf:SW * hf + SW, c0:c0 + w], start=True, stop=True)
            last.then_inc(deg_mm, 1)
            pe.wait_ge(ev1, 12)
            pe.wait_ge(softS, 1)
            for b in range(NB):
                if b >= 2:
                    pe.wait_ge(x_new, b - 1)
                bank = psB[b % 2]
                cols = slice(b * P, (b + 1) * P)
                pe.matmul(bank[:, 0:C], ST[:, cols], w2s[:, :], start=True, stop=True)
                for i in range(3):
                    last = pe.matmul(bank[:, C * (i + 1):C * (i + 2)], VT[:, i, cols], w2v[:, :], start=True, stop=True)
                last.then_inc(mm2, 1)
            pe.wait_ge(dinv_ok, 1)
            for b in range(NB):
                last = pe.matmul(psA[0][:, b:b + 1], dinv[0:1, b * P:(b + 1) * P], onesf[0:1, 0:1], start=True, stop=True)
            last.then_inc(col_mm, 1)
            for b in range(NB):
                pe.wait_ge(h_ok, b + 1)
                if b >= 2:
                    pe.wait_ge(trc, b - 1)
                for c in range(4):
                    last = pe.transpose(psB[2 + b % 2][:, P * c:P * (c + 1)], H[:, b % 2, P * c:P * (c + 1)], ident[:, :])
                last.then_inc(tr, 1)
            pe.wait_ge(trc, NB)
            pe.wait_ge(col_ok, 1)
            for b in range(NB):
                if b >= 2:
                    pe.wait_ge(g1c, b - 1)
                for c in range(4):
                    last = pe.matmul(psB[b % 2][:, 0:P], HT[:, c, b * P:(b + 1) * P], w1T[:, c, :],
                                     start=(c == 0), stop=(c == 3))
                last.then_inc(g1m, 1)
            pe.wait_ge(g1d, 64)
            for b in range(SB):
                for hf in range(2):
                    rows = slice(SW * hf, SW * hf + SW)
                    for m, (c0, w) in enumerate(HCOLS):
                        last = pe.matmul(psA[2 * hf + m][:, 0:w], G1[rows, b, :], AT[rows, b, c0:c0 + w],
                                         start=(b == 0), stop=(b == SB - 1))
            last.then_inc(l1m, 1)
            pe.wait_ge(l1c, 4)
            for b in range(NB):
                if b >= 2:
                    pe.wait_ge(g2c, b - 1)
                pe.matmul(psB[b % 2][:, 0:SW], H1T[:, b * P:(b + 1) * P], w2T[:, :], start=True, stop=True).then_inc(g2m, 1)
            pe.wait_ge(g2d, 64)
            for b in range(SB):
                for m, (c0, w) in enumerate(HCOLS):
                    last = pe.matmul(psA[m][:, 0:w], G2[:, b, :], AT[:, b, c0:c0 + w], start=(b == 0), stop=(b == SB - 1))
            last.then_inc(l2m, 1)
            pe.wait_ge(zc, 1)
            for hf in range(2):
                rows = slice(SW * hf, SW * hf + SW)
                for m, (c0, w) in enumerate(HCOLS):
                    pe.matmul(psB[2 * hf + m][:, 0:w], wd1T[rows, :], Z[rows, c0:c0 + w], start=True,
                              stop=True).then_inc(y1m, 1)
            pe.wait_ge(y1c, 4)
            n = 0
            for c0, w in COLS:
                for m in range(2):
                    if n >= 4:
                        pe.wait_ge(y2c, n - 3)
                    pe.matmul(psA[n % 4][:, 0:w], wd2T[:, P * m:P * m + P], Y1T[:, c0:c0 + w], start=True,
                              stop=True).then_inc(y2m, 1)
                    n += 1
            pe.wait_ge(y2c, 6)
            for b in range(NB):
                if b >= 4:
                    pe.wait_ge(y3c, b - 3)
                cols = slice(b * P, (b + 1) * P)
                pe.matmul(psB[b % 4][:, :], Y2T[:, 0, cols], wd3T[:, 0, :], start=True, stop=False)
                pe.matmul(psB[b % 4][:, :], Y2T[:, 1, cols], wd3T[:, 1, :], start=False, stop=True).then_inc(y3m, 1)

        @block.scalar
        def _(act):
            chain = Chain(act, a_chain)
            n = 0
            for c0, w in COLS:
                for o in range(4):
                    act.wait_ge(mm1, n + 1)
                    dst = relS[:, c0:c0 + w] if o == 0 else VT[:, o - 1, c0:c0 + w]
                    act.copy(dst, psA[n % 4][:, 0:w]).then_inc(ev1, 1)
                    n += 1
            act.preload_act_table_set("natural_log_exp_and_others")
            act.wait_ge(ev1, 12)
            chain.link(act.activation(absS[:, :], relS[:, :], ACT.Abs))
            chain.link(act.activation(absS[:, :], absS[:, :], ACT.Exp, scale=-1.0))
            chain.link(act.activation(absS[:, :], absS[:, :], ACT.Ln, bias=halfc[:, 0:1], scale=0.5))
            act.activation(relS[:, :], relS[:, :], ACT.Relu).then_inc(ev1, 1)
            act.wait_ge(deg_mm, 1)
            for hf in range(2):
                for m, (c0, w) in enumerate(HCOLS):
                    act.activation(dinv[:, HALF * hf + c0:HALF * hf + c0 + w], psA[2 * hf + m][:, 0:w],
                                   ACT.Sqrt).then_inc(sqrt_ok, 1)
            act.wait_ge(var_ok, 1)
            act.activation(std[:, :], mv[:, :, 1], ACT.Sqrt, bias=epsc[:, 0:1]).then_inc(std_ok, 1)
            act.wait_ge(ln_ok, 1)

            def normalise(b):
                if b >= 2:
                    act.wait_ge(tr, b - 1)
                act.activation(H[:, b % 2, :], X[:, b, :], ACT.Relu, bias=shift[:, b:b + 1],
                               scale=rstd[:, b:b + 1]).then_inc(h_ok, 1)

            normalise(0)
            for b in range(NB):
                if b + 1 < NB:
                    normalise(b + 1)
                act.wait_ge(tr, b + 1)
                act.copy(HT[:, :, b * P:(b + 1) * P],
                         psB[2 + b % 2][:, :].rearrange("p (c n) -> p c n", c=4)).then_inc(trc, 1)
            act.wait_ge(col_ok, 1)
            for b in range(NB):
                act.wait_ge(g1m, b + 1)
                act.activation(N1[:, b, :], psB[b % 2][:, 0:P], ACT.Copy, scale=dcol[:, b:b + 1]).then_inc(g1c, 1)
            n = 0
            for hf in range(2):
                for c0, w in HCOLS:
                    act.wait_ge(l1v, n + 1)
                    at = HALF * hf + c0
                    act.activation(H1T[:, at:at + w], SC[:, at:at + w], ACT.Relu, bias=b1c[:, 0:1]).then_inc(l1c, 1)
                    n += 1
            for b in range(NB):
                act.wait_ge(g2m, b + 1)
                act.activation(N2[:, b, :], psB[b % 2][:, 0:SW], ACT.Copy, scale=dcol[:, b:b + 1]).then_inc(g2c, 1)
            act.wait_ge(l2v, 1)
            act.activation(Z, SC[:, 0:HALF], ACT.Identity, bias=b2c[:, 0:1]).then_inc(zc, 1)
            n = 0
            for hf in range(2):
                for m, (c0, w) in enumerate(HCOLS):
                    act.wait_ge(y1m, n + 1)
                    at = HALF * hf + c0
                    act.activation(Y1T[:, at:at + w], psB[2 * hf + m][:, 0:w], ACT.Relu, bias=bd1c[:, 0:1]).then_inc(y1c, 1)
                    n += 1
            n = 0
            for c0, w in COLS:
                for m in range(2):
                    act.wait_ge(y2m, n + 1)
                    act.activation(Y2T[:, m, c0:c0 + w], psA[n % 4][:, 0:w], ACT.Relu,
                                   bias=bd2c[:, m:m + 1]).then_inc(y2c, 1)
                    n += 1

        @block.vector
        def _(dve):
            chain = Chain(dve, v_chain)
            for b in range(SB):
                hf = b * SW // HALF
                rows = slice(SW * hf, SW * hf + SW)
                col = b * SW - HALF * hf
                last = dve.tensor_tensor(AT[rows, b, col:col + SW], AT[rows, b, col:col + SW], ident[rows, rows], ALU.add)
            chain.link(last)
            dve.tensor_reduce(dsum[:, :], AT[:, :, :].rearrange("p b n -> p n b"), AX_X, ALU.add).then_inc(deg_ok, 1)
            dve.wait_ge(ev1, 13)
            dve.tensor_tensor(ST[:, :], relS[:, :], absS[:, :], ALU.add).then_inc(softS, 1)
            dve.wait_ge(sqrt_ok, 4)
            dve.reciprocal(dinv[:, :], dinv[:, :]).then_inc(dinv_ok, 1)
            for b in range(NB):
                dve.wait_ge(mm2, b + 1)
                dve.tensor_tensor(X[:, b, 0:C], psB[b % 2][:, 0:C], X[:, b, 0:C], ALU.add)
                xv = X[:, b, C:D].rearrange("p (d i) -> p i d", i=3)
                dve.tensor_tensor(xv, psB[b % 2][:, C:D].rearrange("p (i d) -> p i d", i=3), xv, ALU.add).then_inc(x_new, 1)
                dve.wait_ge(x_new, b + 1)
                last = dve.bn_stats(stats[:, b, :], X[:, b, :])
            chain.link(last)
            for b in range(NB):
                last = dve.bn_aggr(mv[:, b, :], stats[:, b, :])
            last.then_inc(var_ok, 1)
            dve.wait_ge(std_ok, 1)
            chain.link(dve.reciprocal(rstd[:, :], std[:, :]))
            dve.scalar_tensor_tensor(out=shift[:, :], in0=mv[:, :, 0], scalar=-1.0, in1=rstd[:, :],
                                     op0=ALU.mult, op1=ALU.mult).then_inc(ln_ok, 1)
            dve.wait_ge(col_mm, 1)
            dve.tensor_copy(dcol[:, :], psA[0][:, 0:NB]).then_inc(col_ok, 1)
            dve.wait_ge(h_ok, NB)
            chain.link(dve.tensor_tensor(X[:, :, :], X[:, :, :],
                                         spread(bd3r[:, :].rearrange("p (o d) -> p o d", o=1), 1, NB), ALU.add))
            dve.wait_ge(l1m, 1)
            for hf in range(2):
                for m, (c0, w) in enumerate(HCOLS):
                    at = HALF * hf + c0
                    dve.tensor_tensor(SC[:, at:at + w], psA[2 * hf + m][:, 0:w], dinv[:, at:at + w],
                                      ALU.mult).then_inc(l1v, 1)
            dve.wait_ge(l2m, 1)
            dve.wait_ge(l1c, 4)
            for hf in range(2):
                rows = slice(SW * hf, SW * hf + SW)
                for m, (c0, w) in enumerate(HCOLS):
                    at = HALF * hf + c0
                    last = dve.tensor_tensor(SC[rows, c0:c0 + w], psA[m][rows, 0:w], dinv[rows, at:at + w], ALU.mult)
            last.then_inc(l2v, 1)
            for b in range(NB):
                dve.wait_ge(y3m, b + 1)
                if b >= 2:
                    dve.wait_ge(s_out[b % 2], 16 * (b // 2))
                dve.tensor_tensor(YO[:, b % 2, :], psB[b % 4][:, :], X[:, b, :], ALU.add).then_inc(y3c, 1)


_INS = ["x", "src", "dst", "edge_attr_20", "edge_attr_3", "edge_weight",
        "L0_gnn_W_in2f_s", "L0_gnn_W_in2f_v", "L0_gnn_Wf1", "L0_gnn_bf1", "L0_gnn_Wf2", "L0_gnn_bf2",
        "L0_gnn_W1_s", "L0_gnn_W1_v", "L0_gnn_W2_s", "L0_gnn_W2_v",
        "L1_gnn_W1", "L1_gnn_b1", "L1_gnn_W2", "L1_gnn_b2", "L1_gnn_Wd1", "L1_gnn_bd1",
        "L1_gnn_Wd2", "L1_gnn_bd2", "L1_gnn_Wd3", "L1_gnn_bd3"]


def kernel(**inputs):
    import numpy as _np
    import concourse.bacc as _bacc
    from concourse import mybir as _mybir
    from concourse.bass_utils import run_bass_kernel_spmd as _run

    nc = _bacc.Bacc("TRN2", target_bir_lowering=False, num_devices=1)
    arrays, args = {}, {}
    for name in _INS:
        v = _np.ascontiguousarray(inputs[name])
        arrays[f"in_{name}_dram"] = v
        args[name] = nc.dram_tensor(f"in_{name}_dram", v.shape, _mybir.dt.from_np(v.dtype), kind="ExternalInput").ap()
    out = nc.dram_tensor("out_0_dram", (N, D), _mybir.dt.float32, kind="ExternalOutput").ap()
    gnn_kernel(nc, args, out)
    r = _run(nc, [arrays], core_ids=[0])
    return r.results[0]["out_0_dram"]
```

```python
from contextlib import ExitStack

import numpy as np

import concourse.bass as bass
import concourse.mybir as mybir

F32 = mybir.dt.float32
BF16 = mybir.dt.bfloat16
F16 = mybir.dt.float16
I32 = mybir.dt.int32
U32 = mybir.dt.uint32
ALU = mybir.AluOpType
ACT = mybir.ActivationFunctionType
AX_X = mybir.AxisListType.X

P = 128
N = 1250
NB = (N + P - 1) // P
NPAD = NB * P
LAST = N - (NB - 1) * P
E = 21250
EP, EC = 125, 170
SW = 64
SB = NPAD // SW
HALF = NPAD // 2
GT = 3
GROUPS = 62
NT = GROUPS * GT
assert NT >= (E + SB * (P - 1)) // P and GROUPS % 2 == 0
NTX = NT + 3 * GT
D = 512
C = 128
RBF = 20
RW = 32
CO, SRCL, KEYS, KEYD, DST = 20, 24, 25, 26, 27
NOBODY = 2000.0
Y0 = float(1.0 / np.sqrt(4.0 * np.pi))
Y1 = float(np.sqrt(3.0 / (4.0 * np.pi)))
EPS = 1e-5
UN = 2 * GT
TW = NTX + NTX % 2
BC = 10
BATCHES = EC // BC
assert BATCHES % 2 == 1 and EC % BC == 0


def gnn_kernel(nc, a, out):
    ctx = ExitStack()
    with ctx:
        def sem(name):
            return ctx.enter_context(nc.semaphore(name))

        def keep(name, shape, dt):
            return ctx.enter_context(nc.sbuf_tensor(name, shape, dt))

        rec_dram = nc.dram_tensor("rec_dram", [E + 1, RW], F32).ap()
        node_dram = nc.dram_tensor("node_dram", [NPAD, D], F32).ap()

        AGG = keep("AGG", [P, SB, D], F32)
        AT = keep("AT", [P, SB, HALF], F32)
        X = keep("X", [P, NB, D], F32)
        EIDX = keep("EIDX", [P, NTX], U32)
        FLUSH = keep("FLUSH", [1, NT // UN], I32)
        BLOCK = keep("BLOCK", [1, NT + 1], I32)
        ident = keep("ident", [P, P], F32)
        onesf = keep("onesf", [P, P], F32)
        w2p = keep("w2p", [P, 4, C], F32)
        bias3 = keep("bias3", [3, D], BF16)
        ones3 = keep("ones3", [3, P], BF16)
        wf1 = keep("wf1", [GT * RW, GT, C], F32)
        bf1c = keep("bf1c", [P, 1], F32)
        w1s = keep("w1s", [P, 2, C], F32)
        w1v = keep("w1v", [P, 2, C], F32)
        w2s = keep("w2s", [P, C], F32)
        w2v = keep("w2v", [P, C], F32)
        w1T = keep("w1T", [P, 4, P], F32)
        w2T = keep("w2T", [P, SW], F32)
        wd1T = keep("wd1T", [P, P], F32)
        wd2T = keep("wd2T", [P, 2 * P], F32)
        wd3T = keep("wd3T", [P, 2, D], F32)
        b1c = keep("b1c", [P, 1], F32)
        b2c = keep("b2c", [P, 1], F32)
        bd1c = keep("bd1c", [P, 1], F32)
        bd2c = keep("bd2c", [P, 2], F32)
        bd3r = keep("bd3r", [P, D], F32)
        epsc = keep("epsc", [P, 1], F32)
        halfc = keep("halfc", [P, 1], F32)
        iota64 = keep("iota64", [P, SW], F32)
        iotah = keep("iotah", [P, HALF], F16)

        prologue(nc, a, locals())
        edge_loop(nc, locals())
        epilogue(nc, out, locals())


def spread(ap, axis, n):
    shape = list(ap.shape)
    shape[axis] = n
    return ap.broadcast_to(shape)


class Chain:

    def __init__(self, engine, semaphore):
        self.engine, self.semaphore, self.count = engine, semaphore, 0

    def link(self, instruction):
        self.count += 1
        instruction.then_inc(self.semaphore, 1)
        self.engine.wait_ge(self.semaphore, self.count)


def prologue(nc, a, k):
    AGG, AT, X, EIDX, FLUSH = k["AGG"], k["AT"], k["X"], k["EIDX"], k["FLUSH"]
    ident, onesf = k["ident"], k["onesf"]
    rec_dram, node_dram = k["rec_dram"], k["node_dram"]
    w2p, bias3, ones3, wf1 = k["w2p"], k["bias3"], k["ones3"], k["wf1"]
    with ExitStack() as ctx:
        def sb(name, shape, dt):
            return ctx.enter_context(nc.sbuf_tensor("sort_" + name, shape, dt))

        def ps(name, shape, dt=F32):
            return ctx.enter_context(nc.psum_tensor("sort_" + name, shape, dt))

        def sem(name):
            return ctx.enter_context(nc.semaphore("sort_" + name))

        REC = sb("REC", [EP, EC, RW], F32)
        rec0 = sb("rec0", [1, RW], F32)
        srci = sb("srci", [EP, EC], I32)
        dsti = sb("dsti", [EP, EC], I32)
        tmpi = sb("tmpi", [EP, EC], I32)
        dirs = sb("dirs", [EP, EC, 3], F32)
        rcut = sb("rcut", [EP, EC], F32)
        norm = sb("norm", [EP, EC], F32)
        gain = sb("gain", [EP, EC], F32)
        hi = sb("hi", [EP, EC], F32)
        blkf = sb("blkf", [EP, EC], F32)
        lane = sb("lane", [EP, EC], BF16)
        tile = sb("tile", [EP, EC], BF16)
        maskflat = AT[:, :, :].rearrange("p b d -> p (b d)")[0:EP, 0:SB * EC]
        MASK = maskflat.rearrange("p (b c) -> p b c", b=SB)
        scanflat = AGG[:, :, :].rearrange("p b d -> p (b d)")[0:EP, 0:SB * EC]
        SCAN = scanflat.rearrange("p (b c) -> p b c", b=SB)
        zeros = sb("zeros", [EP, 2 * TW], BF16)
        le = AGG[0:1, :, :].rearrange("p b d -> p (b d)")[:, 0:(NT + 1) * (SB - 1)].rearrange("p (t b) -> p t b", b=SB - 1)
        cum = sb("cum", [EP, SB], F32)
        cumx = sb("cumx", [EP, SB], F32)
        cnt = sb("cnt", [EP, SB], F32)
        adj = sb("adj", [EP, SB], F32)
        nti = sb("nti", [P, SB], I32)
        ntf = sb("ntf", [P, SB], F32)
        incl = sb("incl", [P, SB], F32)
        excl = sb("excl", [P, SB], F32)
        tcol = sb("tcol", [1, NT + 1], F32)
        blkt = sb("blkt", [1, NT + 2], F32)
        neq = sb("neq", [1, NT + 1], F32)
        bits = sb("bits", [1, NT // UN, UN], F32)
        mask = sb("mask", [1, NT // UN], F32)
        upper = sb("upper", [P, P], F32)
        iotab = sb("iotab", [P, SB], F32)
        steps = sb("steps", [P, TW, BC], BF16)
        colno = sb("colno", [P, EC], BF16)
        partno = sb("partno", [P, 1], F32)
        lhot = sb("lhot", [EP, 2, P, BC], BF16)
        lpart = sb("lpart", [EP, 2, P, BC], BF16)
        lcol = sb("lcol", [EP, 2, P, BC], BF16)
        thot = sb("thot", [EP, 2, TW, BC], BF16)
        eidf = sb("eidf", [P, NTX], F32)
        win = sb("win", [P, 2, C], F32)
        w1raw = sb("w1raw", [P, D], F32)
        w2raw = sb("w2raw", [SW, P], F32)
        wd1raw = sb("wd1raw", [P, 2, SW], F32)
        wd2raw = sb("wd2raw", [P, 2, P], F32)
        wd3raw = sb("wd3raw", [P, 4, 2 * P], F32)
        wf2raw = sb("wf2raw", [P, D], F32)
        stats = sb("stats", [P, NB, 6], F32)
        mv = sb("mv", [P, NB, 2], F32)
        std = sb("std", [P, NB], F32)
        rstd = sb("rstd", [P, NB], F32)
        shift = sb("shift", [P, NB], F32)
        spare = AGG[:, :, :].rearrange("p b d -> p (b d)")[:, SB * EC + EC:]
        H = spare[:, 0:2 * D].rearrange("p (i d) -> p i d", i=2)
        HT = spare[:, 2 * D:4 * D].rearrange("p (i c n) -> p i c n", i=2, c=4)
        GS = spare[:, 4 * D:6 * D].rearrange("p (i d) -> p i d", i=2)
        bf2r, bsum, bres = (spare[0:3, D * i:D * (i + 1)] for i in (6, 7, 8))
        bhi, bmid = (spare[0:3, D * 9:D * 10].bitcast(BF16)[:, D * i:D * (i + 1)] for i in (0, 1))
        sq = spare[0:EP, 10 * D:10 * D + 3 * EC].rearrange("p (c i) -> p c i", i=3)

        psT = ps("psT", [P, 2, D])
        psG = ps("psG", [P, 2, D])
        psW = ps("psW", [P, D])
        psC = ps("psC", [P, D])
        psE = ps("psE", [P, D])

        s_edges = sem("s_edges")
        s_attr = sem("s_attr")
        s_dirs = sem("s_dirs")
        s_x = sem("s_x")
        s_weights = sem("s_weights")
        s_raw = sem("s_raw")
        s_xzero = sem("s_xzero")
        s_const = sem("s_const")
        s_iden = sem("s_iden")
        s_steps = sem("s_steps")
        s_rec = sem("s_rec")
        s_recs = sem("s_recs")
        s_norm2 = sem("s_norm2")
        s_norm = sem("s_norm")
        s_cnt = sem("s_cnt")
        s_tot = sem("s_tot")
        s_pos = sem("s_pos")
        s_le = sem("s_le")
        s_lane = sem("s_lane")
        s_hot = sem("s_hot")
        s_part = sem("s_part")
        s_hotfree = sem("s_hotfree")
        s_perm = sem("s_perm")
        s_eidx = sem("s_eidx")
        s_var = sem("s_var")
        s_std = sem("s_std")
        s_ln = sem("s_ln")
        s_h = sem("s_h")
        s_ht = sem("s_ht")
        s_htc = sem("s_htc")
        s_g = sem("s_g")
        s_gc = sem("s_gc")
        s_gout = [sem(f"s_gout{i}") for i in range(2)]
        s_wt = sem("s_wt")
        s_wtc = sem("s_wtc")
        s_bias = sem("s_bias")
        v_chain = sem("v_chain")
        p_chain = sem("p_chain")
        p_zero = sem("p_zero")
        block = ctx.enter_context(nc.Block())

        @block.sync
        def _(sp):
            sp.dma_start(srci[:, :], a["src"].rearrange("(p c) -> p c", p=EP)).then_inc(s_edges, 16)
            sp.dma_start(dsti[:, :], a["dst"].rearrange("(p c) -> p c", p=EP)).then_inc(s_edges, 16)
            sp.dma_start(dirs[:, :, :], a["edge_attr_3"].rearrange("(p c) i -> p c i", p=EP)).then_inc(s_dirs, 16)
            sp.dma_start(rcut[:, :], a["edge_weight"].rearrange("(p c) -> p c", p=EP)).then_inc(s_dirs, 16)
            sp.wait_ge(s_xzero, 1)
            sp.dma_start(X[:, 0:NB - 1, :],
                         a["x"][0:(NB - 1) * P, :].rearrange("(b p) d -> p b d", p=P)).then_inc(s_x, 16)
            sp.dma_start(X[0:LAST, NB - 1, :], a["x"][(NB - 1) * P:N, :]).then_inc(s_x, 16)
            for i, name in enumerate(("W_in2f_s", "W_in2f_v")):
                sp.dma_start(win[:, i, :], a["L0_gnn_" + name]).then_inc(s_raw, 16)
            sp.dma_start(w1raw[:, :], a["L1_gnn_W1"]).then_inc(s_raw, 16)
            sp.dma_start(w2raw[:, :], a["L1_gnn_W2"]).then_inc(s_raw, 16)
            for i in range(2):
                sp.dma_start(wd1raw[:, i, :], a["L1_gnn_Wd1"]).then_inc(s_raw, 16)
            sp.dma_start(wd2raw[:, :, :], a["L1_gnn_Wd2"].rearrange("(j p) n -> p j n", p=P)).then_inc(s_raw, 16)
            sp.dma_start(wd3raw[:, :, :], a["L1_gnn_Wd3"].rearrange("(j p) n -> p j n", p=P)).then_inc(s_raw, 16)
            sp.dma_start(wf2raw[:, :], a["L0_gnn_Wf2"][:, 0:D]).then_inc(s_raw, 16)
            for i in range(3):
                sp.dma_start(bf2r[i:i + 1, :], a["L0_gnn_bf2"][0:D].rearrange("(o n) -> o n", o=1)).then_inc(s_raw, 16)
            sp.wait_ge(s_rec, 1)
            sp.dma_start(rec_dram[1:E + 1, :].rearrange("(p c) w -> p c w", p=EP), REC[:, :, :]).then_inc(s_recs, 16)
            sp.dma_start(rec_dram[0:1, :], rec0[:, :]).then_inc(s_recs, 16)
            for b in range(NB):
                sp.wait_ge(s_gc, b + 1)
                sp.dma_start(node_dram[b * P:(b + 1) * P, :], GS[:, b % 2, :]).then_inc(s_gout[b % 2], 16)
            for i in range(2):
                sp.wait_ge(s_gout[i], 16 * (NB // 2))
            sp.wait_ge(s_recs, 32)

        @block.scalar
        def _(act):
            act.dma_start(REC[:, :, 0:RBF], a["edge_attr_20"].rearrange("(p c) w -> p c w", p=EP)).then_inc(s_attr, 16)
            n = 0
            act.wait_ge(s_xzero, 2)
            for i in range(GT):
                act.dma_start(wf1[RW * i:RW * i + RBF, i, :], a["L0_gnn_Wf1"]).then_inc(s_weights, 16)
            act.dma_start(k["bf1c"][:, :], a["L0_gnn_bf1"].rearrange("(p o) -> p o", o=1)).then_inc(s_weights, 16)
            for w, name in ((k["w1s"], "W1_s"), (k["w1v"], "W1_v")):
                act.dma_start(w[:, :, :], a["L0_gnn_" + name].rearrange("(f k) c -> f k c", k=2)).then_inc(s_weights, 16)
            for w, name in ((k["w2s"], "W2_s"), (k["w2v"], "W2_v")):
                act.dma_start(w[:, :], a["L0_gnn_" + name]).then_inc(s_weights, 16)
            act.dma_start(k["b1c"][:, :], a["L1_gnn_b1"].rearrange("(p o) -> p o", o=1)).then_inc(s_weights, 16)
            for i in range(2):
                act.dma_start(k["b2c"][SW * i:SW * i + SW, :],
                              a["L1_gnn_b2"].rearrange("(p o) -> p o", o=1)).then_inc(s_weights, 16)
            act.dma_start(k["bd1c"][:, :], a["L1_gnn_bd1"].rearrange("(p o) -> p o", o=1)).then_inc(s_weights, 16)
            for i in range(2):
                act.dma_start(k["bd2c"][:, i:i + 1],
                              a["L1_gnn_bd2"][P * i:P * i + P].rearrange("(p o) -> p o", o=1)).then_inc(s_weights, 16)
            act.dma_start(k["bd3r"][:, :], spread(a["L1_gnn_bd3"].rearrange("(o n) -> o n", o=1), 0, P)).then_inc(s_weights, 16)
            act.wait_ge(s_var, 1)
            act.wait_ge(s_const, 1)
            act.activation(std[:, :], mv[:, :, 1], ACT.Sqrt, bias=k["epsc"][:, 0:1]).then_inc(s_std, 1)
            act.wait_ge(s_norm2, 1)
            act.activation(norm[:, :], gain[:, :], ACT.Sqrt).then_inc(s_norm, 1)
            act.wait_ge(s_ln, 1)

            def normalise(b):
                if b >= 2:
                    act.wait_ge(s_ht, b - 1)
                act.activation(H[:, b % 2, :], X[:, b, :], ACT.Relu, bias=shift[:, b:b + 1],
                               scale=rstd[:, b:b + 1]).then_inc(s_h, 1)

            def turned(b):
                act.wait_ge(s_ht, b + 1)
                if b >= 2:
                    act.wait_ge(s_g, b - 1)
                act.copy(HT[:, b % 2, :, :].rearrange("p c n -> p (c n)"), psT[:, b % 2, :]).then_inc(s_htc, 1)

            normalise(0)
            normalise(1)
            turned(0)
            for b in range(NB):
                if b + 2 < NB:
                    normalise(b + 2)
                if b + 1 < NB:
                    turned(b + 1)
                act.wait_ge(s_g, b + 1)
                if b >= 2:
                    act.wait_ge(s_gout[b % 2], 16 * (b // 2))
                act.mul(GS[:, b % 2, :], psG[:, b % 2, :], float(C) ** -0.5).then_inc(s_gc, 1)
            for n, dst in enumerate((k["w1T"][:, :, :].rearrange("p c n -> p (c n)"), None,
                                     k["wd3T"][:, 0, :], k["wd3T"][:, 1, :])):
                act.wait_ge(s_wt, n + 1)
                if dst is not None:
                    act.copy(dst, psW[:, :]).then_inc(s_wtc, 1)
                else:
                    act.copy(k["w2T"][:, :], psW[:, 0:SW])
                    act.copy(k["wd1T"][:, :], psW[:, P:2 * P])
                    act.copy(k["wd2T"][:, :], psW[:, 2 * P:4 * P]).then_inc(s_wtc, 1)

            def scale_lanes(n, r):
                act.wait_ge(s_lane, n + 1)
                act.activation(lpart[:, r, :, :], lhot[:, r, :, :], ACT.Copy, scale=partno[0:EP, :]).then_inc(s_part, 1)

            with act.Fori(0, BATCHES // 2) as i:
                for r in range(2):
                    scale_lanes(2 * i + r, r)
            scale_lanes(BATCHES - 1, 0)
            act.wait_ge(s_weights, 16 * 15)

        @block.gpsimd
        def _(pool):
            chain = Chain(pool, p_chain)
            pool.memset(X[:, NB - 1, :], 0.0).then_inc(s_xzero, 1)
            pool.memset(wf1[:, :, :], 0.0).then_inc(s_xzero, 1)
            pool.memset(k["epsc"][:, :], EPS)
            pool.memset(k["halfc"][:, :], 0.5)
            pool.memset(zeros[:, :], 0.0)
            pool.memset(ones3[:, :], 1.0)
            pool.memset(REC[:, :, DST + 1:RW], 0.0)
            chain.link(pool.memset(rec0[:, :], 0.0))
            chain.link(pool.memset(rec0[:, SRCL:KEYD + 1], NOBODY))
            pool.iota(iotab[:, :], [[1, SB]], base=0, channel_multiplier=0, allow_small_or_imprecise_dtypes=True)
            pool.iota(colno[:, :], [[1, EC]], base=1, channel_multiplier=0, allow_small_or_imprecise_dtypes=True)
            pool.iota(partno[:, :], [[0, 1]], base=0, channel_multiplier=1, allow_small_or_imprecise_dtypes=True)
            pool.iota(tcol[:, :], [[1, NT + 1]], base=0, channel_multiplier=0, allow_small_or_imprecise_dtypes=True)
            pool.iota(k["iota64"][:, :], [[1, SW]], base=0, channel_multiplier=0, allow_small_or_imprecise_dtypes=True)
            pool.iota(k["iotah"][:, :], [[1, HALF]], base=0, channel_multiplier=0, allow_small_or_imprecise_dtypes=True)
            chain.link(pool.memset(onesf[:, :], 1.0))
            chain.link(pool.affine_select(out=ident[:, :], in_=onesf[:, :], compare_op=ALU.is_equal, fill=0.0, base=0,
                                          pattern=[[-1, P]], channel_multiplier=1))
            pool.affine_select(out=upper[:, :], in_=onesf[:, :], compare_op=ALU.is_ge, fill=0.0, base=-1,
                               pattern=[[1, P]], channel_multiplier=-1).then_inc(s_const, 1)
            pool.wait_ge(s_const, 1)
            pool.sem_inc(s_iden, 1)
            pool.iota(steps[:, :, :], [[1, TW], [0, BC]], base=0, channel_multiplier=0,
                      allow_small_or_imprecise_dtypes=True).then_inc(s_steps, 1)
            pool.wait_ge(s_pos, 1)
            pool.memset(AT[:, :, :], 0.0).then_inc(p_zero, 1)
            pool.wait_ge(s_le, 1)
            for i in range(2):
                pool.wait_ge(s_gout[i], 16 * (NB // 2))
            pool.wait_ge(s_bias, 1)
            pool.memset(AGG[:, :, :], 0.0).then_inc(p_zero, 1)
            pool.wait_ge(p_zero, 2)

        @block.vector
        def _(dve):
            chain = Chain(dve, v_chain)
            link = chain.link
            dve.wait_ge(s_edges, 32)
            link(dve.tensor_scalar(tmpi[:, :], srci[:, :], 6, None, ALU.logical_shift_right))
            link(dve.tensor_copy(blkf[:, :], tmpi[:, :]))
            link(dve.tensor_scalar(tmpi[:, :], srci[:, :], SW - 1, None, ALU.bitwise_and))
            dve.tensor_scalar(hi[:, :], dsti[:, :], float(HALF), None, ALU.is_ge).then_inc(v_chain, 1)
            chain.count += 1
            dve.tensor_copy(REC[:, :, SRCL], tmpi[:, :]).then_inc(v_chain, 1)
            chain.count += 1
            link(dve.tensor_copy(REC[:, :, DST].bitcast(U32), dsti[:, :]))
            dve.scalar_tensor_tensor(out=REC[:, :, KEYS], in0=hi[:, :], scalar=float(SW), in1=REC[:, :, SRCL],
                                     op0=ALU.mult, op1=ALU.add)
            dve.scalar_tensor_tensor(out=REC[:, :, KEYD], in0=hi[:, :], scalar=-float(HALF), in1=dsti[:, :],
                                     op0=ALU.mult, op1=ALU.add)
            dve.wait_ge(s_iden, 1)
            link(dve.tensor_tensor(MASK, spread(blkf[:, :].rearrange("p (o c) -> p o c", o=1), 1, SB),
                                   spread(iotab[0:EP, :].rearrange("p (b o) -> p b o", o=1), 2, EC), ALU.is_equal))
            link(dve.tensor_tensor_scan(scanflat, maskflat, spread(zeros[:, 0:1], 1, SB * EC), 0.0, ALU.add, ALU.add))
            link(dve.tensor_copy(cum[:, :], SCAN[:, :, EC - 1]))
            link(dve.memset(cumx[:, 0:1], 0.0))
            link(dve.tensor_copy(cumx[:, 1:SB], cum[:, 0:SB - 1]))
            dve.tensor_tensor(cnt[:, :], cum[:, :], cumx[:, :], ALU.subtract).then_inc(s_cnt, 1)
            dve.wait_ge(s_x, 32)
            for b in range(NB):
                bn = dve.bn_stats(stats[:, b, :], X[:, b, :])
            link(bn)
            for b in range(NB):
                bn = dve.bn_aggr(mv[:, b, :], stats[:, b, :])
            bn.then_inc(s_var, 1)
            dve.wait_ge(s_dirs, 32)
            link(dve.tensor_tensor(sq, dirs[:, :, :], dirs[:, :, :], ALU.mult))
            dve.tensor_reduce(gain[:, :], sq, AX_X, ALU.add).then_inc(s_norm2, 1)
            dve.wait_ge(s_std, 1)
            link(dve.reciprocal(rstd[:, :], std[:, :]))
            dve.scalar_tensor_tensor(out=shift[:, :], in0=mv[:, :, 0], scalar=-1.0, in1=rstd[:, :],
                                     op0=ALU.mult, op1=ALU.mult).then_inc(s_ln, 1)
            dve.wait_ge(s_tot, 1)
            link(dve.tensor_scalar(nti[:, :], psC[:, SB:2 * SB], float(P - 1), None, ALU.add))
            link(dve.tensor_scalar(nti[:, :], nti[:, :], 7, None, ALU.logical_shift_right))
            link(dve.tensor_copy(ntf[:, :], nti[:, :]))
            link(dve.tensor_tensor_scan(incl[:, :], ntf[:, :], onesf[:, 0:SB], 0.0, ALU.add, ALU.mult))
            link(dve.tensor_tensor(excl[:, :], incl[:, :], ntf[:, :], ALU.subtract))
            link(dve.tensor_tensor(adj[:, :], psC[0:EP, 0:SB], cumx[:, :], ALU.subtract))
            link(dve.scalar_tensor_tensor(out=adj[:, :], in0=excl[0:EP, :], scalar=float(P), in1=adj[:, :],
                                          op0=ALU.mult, op1=ALU.add))
            link(dve.tensor_tensor(SCAN, SCAN,
                                   spread(adj[:, :].rearrange("p (b o) -> p b o", o=1), 2, EC), ALU.add))
            link(dve.tensor_tensor(SCAN, SCAN, MASK, ALU.mult))
            link(dve.tensor_reduce(blkf[:, :], SCAN.rearrange("p b c -> p c b"), AX_X, ALU.add))
            link(dve.tensor_scalar(tmpi[:, :], blkf[:, :], -1.0, None, ALU.add))
            link(dve.tensor_scalar(dsti[:, :], tmpi[:, :], 7, None, ALU.logical_shift_right))
            link(dve.tensor_copy(tile[:, :], dsti[:, :]))
            link(dve.tensor_scalar(tmpi[:, :], tmpi[:, :], P - 1, None, ALU.bitwise_and))
            dve.tensor_copy(lane[:, :], tmpi[:, :]).then_inc(s_pos, 1)
            dve.wait_ge(s_pos, 1)
            dve.wait_ge(s_norm, 1)
            link(dve.reciprocal(norm[:, :], norm[:, :]))
            link(dve.scalar_tensor_tensor(out=gain[:, :], in0=norm[:, :], scalar=Y1, in1=rcut[:, :],
                                          op0=ALU.mult, op1=ALU.mult))
            dve.wait_ge(s_attr, 16)
            for i in range(3):
                link(dve.tensor_tensor(REC[:, :, CO + 1 + i], dirs[:, :, i], gain[:, :], ALU.mult))
            dve.tensor_scalar(REC[:, :, CO], rcut[:, :], Y0, None, ALU.mult).then_inc(s_rec, 1)
            link(dve.tensor_tensor(le, spread(tcol[:, :].rearrange("p (t o) -> p t o", o=1), 2, SB - 1),
                                   spread(incl[0:1, 0:SB - 1].rearrange("p (o b) -> p o b", o=1), 1, NT + 1), ALU.is_ge))
            link(dve.tensor_reduce(blkt[:, 1:NT + 2], le, AX_X, ALU.add))
            dve.sem_inc(s_le, 1)
            link(dve.tensor_scalar(blkt[:, 0:1], blkt[:, 1:2], 0.0, None, ALU.add))
            link(dve.memset(blkt[:, NT + 1:NT + 2], float(SB)))
            link(dve.tensor_tensor(neq[:, :], blkt[:, 0:NT + 1], blkt[:, 1:NT + 2], ALU.not_equal))
            for u in range(UN):
                last = dve.tensor_scalar(bits[:, :, u], neq[:, 0:NT].rearrange("p (i u) -> p i u", u=UN)[:, :, u],
                                         float(1 << u), None, ALU.mult)
            link(last)
            link(dve.tensor_reduce(mask[:, :], bits[:, :, :], AX_X, ALU.add))
            dve.tensor_copy(FLUSH[:, :], mask[:, :])
            dve.tensor_copy(k["BLOCK"][:, :], blkt[:, 0:NT + 1])
            dve.wait_ge(s_raw, 16 * 12)
            dve.tensor_copy(w2p[:, :, :].rearrange("p (k h) f -> p h f k", k=2),
                            wf2raw[:, :].rearrange("p (h f k) -> p h f k", h=2, k=2))
            link(dve.tensor_copy(bsum[:, :].rearrange("p (k h f) -> p h f k", k=2, h=2),
                                 bf2r[:, :].rearrange("p (h f k) -> p h f k", h=2, k=2)))
            link(dve.tensor_copy(bhi[:, :], bsum[:, :]))
            link(dve.tensor_tensor(bres[:, :], bsum[:, :], bhi[:, :], ALU.subtract))
            link(dve.tensor_copy(bmid[:, :], bres[:, :]))
            link(dve.tensor_tensor(bres[:, :], bres[:, :], bmid[:, :], ALU.subtract))
            link(dve.tensor_scalar(bsum[:, :], bhi[:, :], ident[0:3, 0:1], None, ALU.mult))
            link(dve.scalar_tensor_tensor(out=bsum[:, :], in0=bmid[:, :], scalar=ident[0:3, 1:2], in1=bsum[:, :],
                                          op0=ALU.mult, op1=ALU.add))
            dve.scalar_tensor_tensor(out=bias3[:, :], in0=bres[:, :], scalar=ident[0:3, 2:3], in1=bsum[:, :],
                                     op0=ALU.mult, op1=ALU.add).then_inc(s_bias, 1)
            dve.wait_ge(s_weights, 16 * 15)
            dve.tensor_scalar(k["w1s"][:, 0, :], k["w1s"][:, 0, :], float(2 * C) ** -0.5, None, ALU.mult)
            dve.tensor_scalar(k["w1s"][:, 1, :], k["w1s"][:, 1, :], float(6 * C) ** -0.5, None, ALU.mult)
            dve.tensor_scalar(k["w1v"][:, :, :], k["w1v"][:, :, :], float(2 * C) ** -0.5, None, ALU.mult)
            dve.tensor_scalar(k["w2s"][:, :], k["w2s"][:, :], float(C) ** -0.5, None, ALU.mult)
            link(dve.tensor_scalar(k["w2v"][:, :], k["w2v"][:, :], float(C) ** -0.5, None, ALU.mult))
            dve.wait_ge(s_steps, 1)

            def one_hots(n, r):
                dve.wait_ge(s_hotfree, n + 1)
                cols = bass.ds(BC * n, BC)
                dve.tensor_tensor(lhot[:, r, :, :], steps[0:EP, 0:P, :],
                                  spread(lane[:, cols].rearrange("p (o c) -> p o c", o=1), 1, P),
                                  ALU.is_equal).then_inc(s_lane, 1)
                dve.tensor_tensor(thot[:, r, :, :], steps[0:EP, :, :],
                                  spread(tile[:, cols].rearrange("p (o c) -> p o c", o=1), 1, TW), ALU.is_equal)
                dve.wait_ge(s_lane, n + 1)
                dve.tensor_tensor(lcol[:, r, :, :], lhot[:, r, :, :],
                                  spread(colno[0:EP, cols].rearrange("p (o c) -> p o c", o=1), 1, P),
                                  ALU.mult).then_inc(s_hot, 1)

            with dve.Fori(0, BATCHES // 2) as i:
                for r in range(2):
                    one_hots(2 * i + r, r)
            one_hots(BATCHES - 1, 0)
            dve.wait_ge(s_perm, 1)
            link(dve.tensor_scalar(eidf[:, :], psE[:, 0:NTX], float(EC), None, ALU.mult))
            link(dve.tensor_tensor(EIDX[:, :], psE[:, TW:TW + NTX], eidf[:, :], ALU.add))

        @block.tensor
        def _(pe):
            pe.wait_ge(s_cnt, 1)
            pe.wait_ge(s_iden, 1)
            pe.matmul(psC[0:EP, 0:SB], upper[0:EP, 0:EP], cnt[:, :], start=True, stop=True)
            pe.matmul(psC[:, SB:2 * SB], onesf[0:EP, :], cnt[:, :], start=True, stop=True).then_inc(s_tot, 1)

            def transposes(b):
                pe.wait_ge(s_h, b + 1)
                if b >= 2:
                    pe.wait_ge(s_htc, b - 1)
                h = H[:, b % 2, :]
                hv = h[:, C:D].rearrange("p (c i) -> p i c", i=3)
                pe.transpose(psT[:, b % 2, 0:P], h[:, 0:C], ident[:, :])
                for i in range(3):
                    last = pe.transpose(psT[:, b % 2, P * (i + 1):P * (i + 2)], hv[:, i, :], ident[:, :])
                last.then_inc(s_ht, 1)

            pe.wait_ge(s_raw, 16 * 12)
            transposes(0)
            for b in range(NB):
                if b + 1 < NB:
                    transposes(b + 1)
                pe.wait_ge(s_htc, b + 1)
                if b >= 2:
                    pe.wait_ge(s_gc, b - 1)
                for c in range(4):
                    last = pe.matmul(psG[:, b % 2, P * c:P * (c + 1)], HT[:, b % 2, c, :], win[:, min(c, 1), :],
                                     start=True, stop=True)
                last.then_inc(s_g, 1)
            wd1v = wd1raw[:, :, :].rearrange("p i n -> p (i n)")
            jobs = [
                [(w1raw[:, P * j:P * j + P], P * j, P) for j in range(4)],
                [(w2raw[:, :], 0, SW), (wd1v, P, P), (wd2raw[:, 0, :], 2 * P, P), (wd2raw[:, 1, :], 3 * P, P)],
                [(wd3raw[:, j, 0:P], P * j, P) for j in range(4)],
                [(wd3raw[:, j, P:2 * P], P * j, P) for j in range(4)],
            ]
            for n, job in enumerate(jobs):
                if n:
                    pe.wait_ge(s_wtc, n)
                for src, at, rows in job:
                    last = pe.transpose(psW[:, at:at + rows], src, ident[0:rows, 0:rows])
                last.then_inc(s_wt, 1)
            pe.matmul(psE[:, 0:2 * TW], zeros[0:1, 0:P], zeros[0:1, 0:2 * TW], start=True, stop=False,
                      skip_group_check=True).then_inc(s_hotfree, 2)

            def place(n, r):
                pe.wait_ge(s_hot, n + 1)
                pe.wait_ge(s_part, n + 1)
                for c in range(BC):
                    pe.matmul(psE[:, 0:TW], lpart[:, r, :, c], thot[:, r, :, c], start=False, stop=False,
                              skip_group_check=True)
                    last = pe.matmul(psE[:, TW:2 * TW], lcol[:, r, :, c], thot[:, r, :, c], start=False, stop=False,
                                     skip_group_check=True)
                last.then_inc(s_hotfree, 1)

            with pe.Fori(0, BATCHES // 2) as i:
                for r in range(2):
                    place(2 * i + r, r)
            place(BATCHES - 1, 0)
            pe.matmul(psE[:, 0:2 * TW], zeros[0:1, 0:P], zeros[0:1, 0:2 * TW], start=False, stop=True,
                      skip_group_check=True).then_inc(s_perm, 1)


def edge_loop(nc, k):
    AGG, AT, EIDX, FLUSH, BLOCK = k["AGG"], k["AT"], k["EIDX"], k["FLUSH"], k["BLOCK"]
    ident, w2p, bias3, ones3, wf1, bf1c = k["ident"], k["w2p"], k["bias3"], k["ones3"], k["wf1"], k["bf1c"]
    halfc, iota64, iotah = k["halfc"], k["iota64"], k["iotah"]
    rec_dram, node_dram = k["rec_dram"], k["node_dram"]
    with ExitStack() as ctx:
        def sb(name, shape, dt):
            return ctx.enter_context(nc.sbuf_tensor("loop_" + name, shape, dt))

        def ps(name, shape, dt=F32):
            return ctx.enter_context(nc.psum_tensor("loop_" + name, shape, dt))

        def sem(name):
            return ctx.enter_context(nc.semaphore("loop_" + name))

        stage = sb("stage", [P, 2, GT], U32)
        rec = sb("rec", [P, 2, GT, RW], F32)
        node = sb("node", [P, 2, GT, D], F32)
        fT = sb("fT", [GT * RW, P], F32)
        absz = sb("absz", [P, GT * P], F32)
        expz = sb("expz", [P, GT * P], F32)
        logz = sb("logz", [P, GT * P], F32)
        relz = sb("relz", [P, GT * P], F32)
        h = sb("h", [P, 2, GT * P], F32)
        hot = sb("hot", [P, 2, GT, SW], F32)
        shot = sb("shot", [P, 2, GT, 4, SW], F32)
        khot = sb("khot", [P, 2, GT, P], BF16)
        dhot = sb("dhot", [P, 2, GT, HALF], BF16)
        along = sb("along", [P, 2, GT, C], F32)
        prod = sb("prod", [P, 2, 6, C], F32)
        zrow = sb("zrow", [1, D], BF16)
        zerof = sb("zerof", [P, D], F32)

        psW = ps("psW", [P, 2, D])
        psZ = ps("psZ", [P, D])
        psF = ps("psF", [P, D])
        psA = ps("psA", [P, D])
        psN = ps("psN", [P, 2, D])

        staged = sem("staged")
        rec_in = [sem(f"rec_in{q}") for q in range(2)]
        node_in = [sem(f"node_in{q}") for q in range(2)]
        rec_turned = sem("rec_turned")
        fT_ready = sem("fT_ready")
        z_ready = sem("z_ready")
        z_used = sem("z_used")
        abs_done = sem("abs_done")
        exp_done = sem("exp_done")
        soft_done = sem("soft_done")
        h_ready = sem("h_ready")
        hot_ready = sem("hot_ready")
        keys_ready = sem("keys_ready")
        shot_ready = sem("shot_ready")
        along_begun = sem("along_begun")
        along_x = sem("along_x")
        along_ready = sem("along_ready")
        w_ready = sem("w_ready")
        prod_done = sem("prod_done")
        summed = sem("summed")
        copied = sem("copied")
        flushed = sem("flushed")
        counts_copied = sem("counts_copied")
        counts_flushed = sem("counts_flushed")
        zeroed = sem("zeroed")
        pool_turn = sem("pool_turn")
        block = ctx.enter_context(nc.Block())

        @block.gpsimd
        def _(pool):
            def gather_rec(q):
                for j in range(GT):
                    pool.indirect_dma_start(out=rec[:, q, j, :], out_offset=None, in_=rec_dram,
                                            in_offset=bass.IndirectOffsetOnAxis(ap=stage[:, q, j:j + 1], axis=0)
                                            ).then_inc(rec_in[q], 16)

            def gather_node(q):
                for j in range(GT):
                    pool.indirect_dma_start(out=node[:, q, j, :], out_offset=None, in_=node_dram,
                                            in_offset=bass.IndirectOffsetOnAxis(
                                                ap=rec[:, q, j, DST:DST + 1].bitcast(U32), axis=0)
                                            ).then_inc(node_in[q], 16)

            pool.wait_ge(staged, 1)
            gather_rec(0)
            pool.wait_ge(staged, 2)
            gather_rec(1)
            pool.wait_ge(rec_in[0], 16 * GT)
            gather_node(0)
            with pool.Fori(0, GROUPS // 2) as i:
                for q in range(2):
                    s = 2 * i + q
                    pool.wait_ge(rec_in[1 - q], 16 * GT * (i + 1 + q))
                    pool.wait_ge(prod_done, GT * s + 1)
                    pool.sem_inc(pool_turn, 1)
                    gather_node(1 - q)
                    pool.wait_ge(staged, s + 3)
                    pool.wait_ge(keys_ready, s + 1)
                    pool.wait_ge(shot_ready, s + 1)
                    pool.wait_ge(along_ready, s + 1)
                    pool.wait_ge(rec_turned, s + 1)
                    pool.wait_ge(node_in[q], 16 * GT * (i + 1))
                    pool.sem_inc(pool_turn, 1)
                    gather_rec(q)
            for q in range(2):
                pool.wait_ge(rec_in[q], 16 * GT * (GROUPS // 2 + 1))
            pool.wait_ge(node_in[0], 16 * GT * (GROUPS // 2 + 1))

        @block.scalar
        def _(act):
            def attributes():
                for j in range(GT):
                    rows = slice(RW * j, RW * j + RBF)
                    last = act.copy(fT[rows, :], psF[rows, 0:P])
                last.then_inc(fT_ready, 1)

            def soften(n):
                act.wait_ge(z_ready, n + 1)
                act.wait_ge(h_ready, n + 1)
                act.activation(absz[:, :], psZ[:, 0:GT * P], ACT.Abs, bias=bf1c[:, 0:1]).then_inc(abs_done, 1)
                act.activation(relz[:, :], psZ[:, 0:GT * P], ACT.Relu, bias=bf1c[:, 0:1]).then_inc(z_used, 1)
                act.wait_ge(abs_done, n + 1)
                act.activation(expz[:, :], absz[:, :], ACT.Exp, scale=-1.0).then_inc(exp_done, 1)
                act.wait_ge(exp_done, n + 1)
                act.activation(logz[:, :], expz[:, :], ACT.Ln, bias=halfc[:, 0:1], scale=0.5).then_inc(soft_done, 1)

            def factors(q, n, tiles):
                act.wait_ge(hot_ready, n + 1)
                for j in tiles:
                    for c in range(4):
                        last = act.activation(shot[:, q, j, c, :], hot[:, q, j, :], ACT.Copy,
                                              scale=rec[:, q, j, CO + c:CO + c + 1])
                if tiles[-1] == GT - 1:
                    last.then_inc(shot_ready, 1)

            def begin_along(q):
                for j in range(GT):
                    last = act.activation(along[:, q, j, :], node[:, q, j, C:2 * C], ACT.Copy,
                                          scale=rec[:, q, j, CO + 1:CO + 2])
                last.then_inc(along_begun, 1)

            def empty(t):
                b = act.value_load(BLOCK[0:1, bass.ds(t, 1)], min_val=0, max_val=SB - 1)
                act.wait_ge(summed, t + 1)
                act.copy(AT[:, bass.ds(b, 1), 0:D].rearrange("p o d -> p (o d)"), psN[:, 0, :])
                act.copy(AT[:, bass.ds(b, 1), D:HALF].rearrange("p o d -> p (o d)"),
                         psN[:, 1, 0:HALF - D]).then_inc(counts_copied, 1)
                act.wait_ge(counts_copied, t + 1)
                act.copy(psN[:, 0, :], zerof[:, :])
                act.copy(psN[:, 1, 0:HALF - D], zerof[:, 0:HALF - D]).then_inc(counts_flushed, 1)

            def flush(t, ended):
                with act.If(ended > 0):
                    empty(t)
                with act.Else():
                    act.wait_ge(summed, t + 1)
                    act.sem_inc(counts_copied, 1)
                    act.sem_inc(counts_flushed, 1)

            act.preload_act_table_set("natural_log_exp_and_others")
            act.wait_ge(zeroed, 3)
            act.wait_ge(rec_turned, 1)
            attributes()
            soften(0)
            factors(0, 0, (0, 1, 2))
            act.wait_ge(node_in[0], 16 * GT)
            begin_along(0)
            act.wait_ge(rec_turned, 2)
            act.wait_ge(z_ready, 1)
            attributes()
            with act.Fori(0, GROUPS // 2) as i:
                for q in range(2):
                    s = 2 * i + q
                    if q == 0:
                        ends = act.value_load(FLUSH[0:1, bass.ds(i, 1)], min_val=0, max_val=(1 << UN) - 1)
                    flush(UN * i + GT * q, (ends >> (GT * q)) & 1)
                    soften(s + 1)
                    factors(1 - q, s + 1, (0,))
                    flush(UN * i + GT * q + 1, (ends >> (GT * q + 1)) & 1)
                    factors(1 - q, s + 1, (1,))
                    act.wait_ge(node_in[1 - q], 16 * GT * (i + 1 + q))
                    begin_along(1 - q)
                    flush(UN * i + GT * q + 2, (ends >> (GT * q + 2)) & 1)
                    act.wait_ge(rec_turned, s + 3)
                    attributes()
                    factors(1 - q, s + 1, (2,))
            empty(NT)

        @block.vector
        def _(dve):
            def number(q, n):
                dve.tensor_copy(stage[:, q, :], EIDX[:, bass.ds(GT * n, GT)]).then_inc(staged, 1)

            def hots(q, n):
                dve.tensor_tensor(hot[:, q, :, :], spread(iota64[:, :].rearrange("p (o w) -> p o w", o=1), 1, GT),
                                  spread(rec[:, q, :, SRCL:SRCL + 1], 2, SW), ALU.is_equal).then_inc(hot_ready, 1)

            def keys(q):
                for j in range(GT):
                    dve.tensor_scalar(khot[:, q, j, :], iotah[:, 0:P], rec[:, q, j, KEYS:KEYS + 1], None, ALU.is_equal)
                    last = dve.tensor_scalar(dhot[:, q, j, :], iotah[:, :], rec[:, q, j, KEYD:KEYD + 1], None,
                                             ALU.is_equal)
                last.then_inc(keys_ready, 1)

            def hidden(q, n, free=None):
                dve.wait_ge(soft_done, n + 1)
                dve.wait_ge(z_used, n + 1)
                dve.tensor_tensor(h[:, q, :], relz[:, :], logz[:, :], ALU.add).then_inc(h_ready, 1)

            def end_along(q, n):
                dve.wait_ge(along_begun, n + 1)
                for i in (1, 2):
                    for j in range(GT):
                        if i == 2:
                            dve.wait_ge(along_x, GT * n + j + 1)
                        last = dve.scalar_tensor_tensor(out=along[:, q, j, :], in0=node[:, q, j, C * (1 + i):C * (2 + i)],
                                                        scalar=rec[:, q, j, CO + 1 + i:CO + 2 + i],
                                                        in1=along[:, q, j, :], op0=ALU.mult, op1=ALU.add)
                        if i == 1:
                            last.then_inc(along_x, 1)
                last.then_inc(along_ready, 1)

            def products(q, j, r):
                xs = spread(node[:, q, j, 0:C].rearrange("p (o f) -> p o f", o=1), 1, 2)
                dve.tensor_tensor(prod[:, r, 0:2, :], psW[:, r, 0:2 * C].rearrange("p (k f) -> p k f", k=2), xs, ALU.mult)
                dve.tensor_tensor(prod[:, r, 2, :], psW[:, r, 2 * C:3 * C], along[:, q, j, :], ALU.mult)
                xv = node[:, q, j, C:D].rearrange("p (i f) -> p i f", i=3)
                wd = spread(psW[:, r, 3 * C:4 * C].rearrange("p (o f) -> p o f", o=1), 1, 3)
                dve.tensor_tensor(prod[:, r, 3:6, :], wd, xv, ALU.mult).then_inc(prod_done, 1)

            def empty(t):
                b = dve.value_load(BLOCK[0:1, bass.ds(t, 1)], min_val=0, max_val=SB - 1)
                dve.wait_ge(summed, t + 1)
                dve.tensor_copy(AGG[:, bass.ds(b, 1), :].rearrange("p o d -> p (o d)"), psA[:, :]).then_inc(copied, 1)
                dve.wait_ge(copied, t + 1)
                dve.memset(psA[:, :], 0.0).then_inc(flushed, 1)

            def flush(t, ended):
                with dve.If(ended > 0):
                    empty(t)
                with dve.Else():
                    dve.wait_ge(summed, t + 1)
                    dve.sem_inc(copied, 1)
                    dve.sem_inc(flushed, 1)

            dve.memset(zrow[:, :], 0.0).then_inc(zeroed, 1)
            dve.memset(fT[:, :], 0.0).then_inc(zeroed, 1)
            dve.memset(zerof[:, :], 0.0).then_inc(zeroed, 1)
            number(0, 0)
            number(1, 1)
            dve.sem_inc(prod_done, 1)
            dve.sem_inc(h_ready, 1)
            dve.wait_ge(rec_in[0], 16 * GT)
            number(0, 2)
            hots(0, 0)
            keys(0)
            hidden(0, 0)
            end_along(0, 0)
            with dve.Fori(0, GROUPS // 2) as i:
                for q in range(2):
                    s = 2 * i + q
                    for j in range(GT):
                        u = GT * q + j
                        t = UN * i + u
                        if u == 0:
                            ends = dve.value_load(FLUSH[0:1, bass.ds(i, 1)], min_val=0, max_val=(1 << UN) - 1)
                        if j == 0:
                            dve.wait_ge(along_ready, s + 1)
                        dve.wait_ge(w_ready, t + 1)
                        products(q, j, u % 2)
                        if j == 1:
                            hidden(1 - q, s + 1)
                        flush(t, (ends >> u) & 1)
                        if j == GT - 1:
                            end_along(1 - q, s + 1)
                        if j == 0:
                            dve.wait_ge(rec_in[1 - q], 16 * GT * (i + 1 + q))
                            hots(1 - q, s + 1)
                            number(1 - q, s + 3)
                        if j == 1:
                            keys(1 - q)
            empty(NT)

        @block.tensor
        def _(pe):
            def turn(q):
                pe.transpose(psF[0:GT * RW, 0:P], rec[:, q, :, :].rearrange("p j w -> p (j w)"),
                             ident[:, :]).then_inc(rec_turned, 1)

            def z():
                for j in range(GT):
                    last = pe.matmul(psZ[:, P * j:P * (j + 1)], wf1[:, j, :], fT[:, :], start=True, stop=True)
                last.then_inc(z_ready, 1)

            def filter_(q, j, r):
                pe.matmul(psW[:, r, :], ones3[:, :], bias3[:, :], start=True, stop=False)
                pe.matmul(psW[:, r, :], h[:, q, P * j:P * (j + 1)], w2p[:, :, :].rearrange("p k f -> p (k f)"),
                          start=False, stop=True).then_inc(w_ready, 1)

            def open_sums(start, stop):
                pe.matmul(psA[:, :], zrow[:, 0:P], zrow[:, :], start=start, stop=stop, skip_group_check=True)
                pe.matmul(psN[:, 0, :], zrow[:, 0:P], zrow[:, :], start=start, stop=stop, skip_group_check=True)
                return pe.matmul(psN[:, 1, 0:HALF - D], zrow[:, 0:P], zrow[:, 0:HALF - D], start=start, stop=stop,
                                 skip_group_check=True)

            def add(dst, left, right):
                return pe.matmul(dst, left, right, start=False, stop=False, skip_group_check=True)

            def sums(q, j, r):
                def to(kind):
                    return psA[:, SW * kind:SW * (kind + 1)]

                add(to(0), prod[:, r, 0, :], shot[:, q, j, 0, :])
                add(psA[:, SW * 2:SW * 5], prod[:, r, 1, :], shot[:, q, j, 1:4, :].rearrange("p c w -> p (c w)"))
                add(to(1), prod[:, r, 2, :], hot[:, q, j, :])
                for i in range(3):
                    add(to(5 + i), prod[:, r, 3 + i, :], shot[:, q, j, 0, :])

            def counts(q, j):
                add(psN[:, 0, :], khot[:, q, j, :], dhot[:, q, j, 0:D])
                add(psN[:, 1, 0:HALF - D], khot[:, q, j, :], dhot[:, q, j, D:HALF]).then_inc(summed, 1)

            pe.wait_ge(zeroed, 2)
            open_sums(True, False).then_inc(summed, 1)
            pe.wait_ge(rec_in[0], 16 * GT)
            turn(0)
            pe.wait_ge(fT_ready, 1)
            z()
            pe.wait_ge(rec_in[1], 16 * GT)
            turn(1)
            pe.wait_ge(h_ready, 2)
            filter_(0, 0, 0)
            with pe.Fori(0, GROUPS // 2) as i:
                for q in range(2):
                    s = 2 * i + q
                    for j in range(GT):
                        u = GT * q + j
                        t = UN * i + u
                        if j == 0:
                            pe.wait_ge(fT_ready, s + 2)
                            pe.wait_ge(z_used, s + 1)
                            z()
                        if j == GT - 1:
                            pe.wait_ge(rec_in[q], 16 * GT * (i + 2))
                            pe.wait_ge(fT_ready, s + 2)
                            turn(q)
                            pe.wait_ge(h_ready, s + 3)
                        pe.wait_ge(prod_done, t + 1)
                        filter_(q if j < GT - 1 else 1 - q, (j + 1) % GT, (u + 1) % 2)
                        if j == 0:
                            pe.wait_ge(keys_ready, s + 1)
                            pe.wait_ge(shot_ready, s + 1)
                        pe.wait_ge(prod_done, t + 2)
                        pe.wait_ge(flushed, t + 1)
                        sums(q, j, u % 2)
                        pe.wait_ge(counts_flushed, t + 1)
                        counts(q, j)
            pe.wait_ge(flushed, NT + 1)
            pe.wait_ge(counts_flushed, NT + 1)
            open_sums(False, True)


def epilogue(nc, out, k):
    AGG, AT, X, ident, onesf = k["AGG"], k["AT"], k["X"], k["ident"], k["onesf"]
    w1s, w1v, w2s, w2v = k["w1s"], k["w1v"], k["w2s"], k["w2v"]
    w1T, w2T, wd1T, wd2T, wd3T = k["w1T"], k["w2T"], k["wd1T"], k["wd2T"], k["wd3T"]
    b1c, b2c, bd1c, bd2c, bd3r, epsc, halfc = (k[n] for n in ("b1c", "b2c", "bd1c", "bd2c", "bd3r", "epsc", "halfc"))
    COLS = [(0, 512), (512, 512), (1024, 256)]
    HCOLS = [(0, 512), (512, HALF - 512)]
    with ExitStack() as ctx:
        def sb(name, shape, dt):
            return ctx.enter_context(nc.sbuf_tensor("end_" + name, shape, dt))

        def ps(name, shape, dt=F32):
            return ctx.enter_context(nc.psum_tensor("end_" + name, shape, dt))

        def sem(name):
            return ctx.enter_context(nc.semaphore("end_" + name))

        ST = sb("ST", [P, NPAD], F32)
        VT = sb("VT", [P, 3, NPAD], F32)
        absS = sb("absS", [P, NPAD], F32)
        relS = sb("relS", [P, NPAD], F32)
        stats = sb("stats2", [P, NB, 6], F32)
        mv = sb("mv2", [P, NB, 2], F32)
        std = sb("std2", [P, NB], F32)
        rstd = sb("rstd2", [P, NB], F32)
        shift = sb("shift2", [P, NB], F32)
        H = sb("H2", [P, 2, D], F32)
        dsum = sb("dsum", [P, HALF], F32)
        dinv = sb("dinv", [P, NPAD], F32)
        dcol = sb("dcol", [P, NB], F32)
        N1 = sb("N1", [P, NB, P], F32)
        N2 = sb("N2", [P, NB, SW], F32)
        YO = sb("YO", [P, 2, D], F32)
        agg = AGG[:, :, :].rearrange("p b d -> p (b d)")
        HT = agg[:, 0:4 * NPAD].rearrange("p (c n) -> p c n", c=4)
        G1 = agg[:, 4 * NPAD:6 * NPAD].rearrange("p (b f) -> p b f", b=SB)
        G2 = agg[:, 6 * NPAD:8 * NPAD].rearrange("p (b f) -> p b f", b=SB)
        vt = VT[:, :, :].rearrange("p i n -> p (i n)")
        Y2T = vt[:, 0:2 * NPAD].rearrange("p (m n) -> p m n", m=2)
        Y1T = vt[:, 2 * NPAD:3 * NPAD]
        H1T = ST[:, :]
        Z = absS[:, 0:HALF]
        SC = relS[:, :]

        psA = [ps(f"psA{i}", [P, D]) for i in range(4)]
        psB = [ps(f"psB{i}", [P, D]) for i in range(4)]

        mm1 = sem("mm1")
        ev1 = sem("ev1")
        softS = sem("softS")
        a_chain = sem("a_chain")
        v_chain = sem("v_chain2")
        mm2 = sem("mm2")
        x_new = sem("x_new")
        var_ok = sem("var_ok")
        std_ok = sem("std_ok")
        ln_ok = sem("ln_ok")
        h_ok = sem("h_ok")
        tr = sem("tr")
        trc = sem("trc")
        deg_ok = sem("deg_ok")
        deg_mm = sem("deg_mm")
        sqrt_ok = sem("sqrt_ok")
        dinv_ok = sem("dinv_ok")
        col_mm = sem("col_mm")
        col_ok = sem("col_ok")
        g1m = sem("g1m")
        g1c = sem("g1c")
        g1d = sem("g1d")
        g2d = sem("g2d")
        l1m = sem("l1m")
        l1v = sem("l1v")
        l1c = sem("l1c")
        g2z = sem("g2z")
        g2m = sem("g2m")
        g2c = sem("g2c")
        l2m = sem("l2m")
        l2v = sem("l2v")
        zc = sem("zc")
        y1m = sem("y1m")
        y1c = sem("y1c")
        y2m = sem("y2m")
        y2c = sem("y2c")
        y3m = sem("y3m")
        y3c = sem("y3c")
        s_out = [sem(f"s_out{i}") for i in range(2)]
        block = ctx.enter_context(nc.Block())

        @block.sync
        def _(sp):
            sp.wait_ge(g1c, NB)
            for par in range(2):
                for hf in range(2):
                    sp.dma_start(G1[SW * hf:SW * hf + SW, par::2, :], N1[SW * par:SW * par + SW, :, :]).then_inc(g1d, 16)
            sp.wait_ge(g2z, 1)
            sp.wait_ge(g2c, NB)
            for par in range(2):
                for hf in range(2):
                    sp.dma_start(G2[SW * hf:SW * hf + SW, par::2, SW * hf:SW * hf + SW],
                                 N2[SW * par:SW * par + SW, :, :]).then_inc(g2d, 16)
            for b in range(NB):
                sp.wait_ge(y3c, b + 1)
                rows = P if b < NB - 1 else LAST
                sp.dma_start(out[b * P:b * P + rows, :], YO[0:rows, b % 2, :]).then_inc(s_out[b % 2], 16)
            for i in range(2):
                sp.wait_ge(s_out[i], 16 * (NB // 2))

        @block.gpsimd
        def _(pool):
            pool.wait_ge(mm1, 12)
            pool.memset(G2, 0.0).then_inc(g2z, 1)

        @block.tensor
        def _(pe):
            def sums(kind, c0, n):
                return AGG[:, c0 // SW:(c0 + n) // SW, SW * kind:SW * (kind + 1)]

            n = 0
            for c0, w in COLS:
                for o in range(4):
                    if n >= 4:
                        pe.wait_ge(ev1, n - 3)
                    left = w1s if o == 0 else w1v
                    even, odd = (0, 1) if o == 0 else (1 + o, 4 + o)
                    pe.matmul(psA[n % 4][:, 0:w], left[:, 0, :], sums(even, c0, w), start=True, stop=False)
                    pe.matmul(psA[n % 4][:, 0:w], left[:, 1, :], sums(odd, c0, w), start=False, stop=True).then_inc(mm1, 1)
                    n += 1
            pe.wait_ge(ev1, 12)
            pe.wait_ge(deg_ok, 1)
            for hf in range(2):
                for m, (c0, w) in enumerate(HCOLS):
                    last = pe.matmul(psA[2 * hf + m][:, 0:w], onesf[SW * hf:SW * hf + SW, :],
                                     dsum[SW * hf:SW * hf + SW, c0:c0 + w], start=True, stop=True)
            last.then_inc(deg_mm, 1)
            pe.wait_ge(ev1, 12)
            pe.wait_ge(softS, 1)
            for b in range(NB):
                if b >= 2:
                    pe.wait_ge(x_new, b - 1)
                bank = psB[b % 2]
                cols = slice(b * P, (b + 1) * P)
                pe.matmul(bank[:, 0:C], ST[:, cols], w2s[:, :], start=True, stop=True)
                for i in range(3):
                    last = pe.matmul(bank[:, C * (i + 1):C * (i + 2)], VT[:, i, cols], w2v[:, :], start=True, stop=True)
                last.then_inc(mm2, 1)
            pe.wait_ge(dinv_ok, 1)
            for b in range(NB):
                last = pe.matmul(psA[0][:, b:b + 1], dinv[0:1, b * P:(b + 1) * P], onesf[0:1, 0:1], start=True, stop=True)
            last.then_inc(col_mm, 1)
            for b in range(NB):
                pe.wait_ge(h_ok, b + 1)
                if b >= 2:
                    pe.wait_ge(trc, b - 1)
                for c in range(4):
                    last = pe.transpose(psB[2 + b % 2][:, P * c:P * (c + 1)], H[:, b % 2, P * c:P * (c + 1)], ident[:, :])
                last.then_inc(tr, 1)
            pe.wait_ge(trc, NB)
            pe.wait_ge(col_ok, 1)
            for b in range(NB):
                if b >= 2:
                    pe.wait_ge(g1c, b - 1)
                for c in range(4):
                    last = pe.matmul(psB[b % 2][:, 0:P], HT[:, c, b * P:(b + 1) * P], w1T[:, c, :],
                                     start=(c == 0), stop=(c == 3))
                last.then_inc(g1m, 1)
            pe.wait_ge(g1d, 64)
            for b in range(SB):
                for hf in range(2):
                    rows = slice(SW * hf, SW * hf + SW)
                    for m, (c0, w) in enumerate(HCOLS):
                        last = pe.matmul(psA[2 * hf + m][:, 0:w], G1[rows, b, :], AT[rows, b, c0:c0 + w],
                                         start=(b == 0), stop=(b == SB - 1))
            last.then_inc(l1m, 1)
            pe.wait_ge(l1c, 4)
            for b in range(NB):
                if b >= 2:
                    pe.wait_ge(g2c, b - 1)
                pe.matmul(psB[b % 2][:, 0:SW], H1T[:, b * P:(b + 1) * P], w2T[:, :], start=True, stop=True).then_inc(g2m, 1)
            pe.wait_ge(g2d, 64)
            for b in range(SB):
                for m, (c0, w) in enumerate(HCOLS):
                    last = pe.matmul(psA[m][:, 0:w], G2[:, b, :], AT[:, b, c0:c0 + w], start=(b == 0), stop=(b == SB - 1))
            last.then_inc(l2m, 1)
            pe.wait_ge(zc, 1)
            for hf in range(2):
                rows = slice(SW * hf, SW * hf + SW)
                for m, (c0, w) in enumerate(HCOLS):
                    pe.matmul(psB[2 * hf + m][:, 0:w], wd1T[rows, :], Z[rows, c0:c0 + w], start=True,
                              stop=True).then_inc(y1m, 1)
            pe.wait_ge(y1c, 4)
            n = 0
            for c0, w in COLS:
                for m in range(2):
                    if n >= 4:
                        pe.wait_ge(y2c, n - 3)
                    pe.matmul(psA[n % 4][:, 0:w], wd2T[:, P * m:P * m + P], Y1T[:, c0:c0 + w], start=True,
                              stop=True).then_inc(y2m, 1)
                    n += 1
            pe.wait_ge(y2c, 6)
            for b in range(NB):
                if b >= 4:
                    pe.wait_ge(y3c, b - 3)
                cols = slice(b * P, (b + 1) * P)
                pe.matmul(psB[b % 4][:, :], Y2T[:, 0, cols], wd3T[:, 0, :], start=True, stop=False)
                pe.matmul(psB[b % 4][:, :], Y2T[:, 1, cols], wd3T[:, 1, :], start=False, stop=True).then_inc(y3m, 1)

        @block.scalar
        def _(act):
            chain = Chain(act, a_chain)
            n = 0
            for c0, w in COLS:
                for o in range(4):
                    act.wait_ge(mm1, n + 1)
                    dst = relS[:, c0:c0 + w] if o == 0 else VT[:, o - 1, c0:c0 + w]
                    act.copy(dst, psA[n % 4][:, 0:w]).then_inc(ev1, 1)
                    n += 1
            act.preload_act_table_set("natural_log_exp_and_others")
            act.wait_ge(ev1, 12)
            chain.link(act.activation(absS[:, :], relS[:, :], ACT.Abs))
            chain.link(act.activation(absS[:, :], absS[:, :], ACT.Exp, scale=-1.0))
            chain.link(act.activation(absS[:, :], absS[:, :], ACT.Ln, bias=halfc[:, 0:1], scale=0.5))
            act.activation(relS[:, :], relS[:, :], ACT.Relu).then_inc(ev1, 1)
            act.wait_ge(deg_mm, 1)
            for hf in range(2):
                for m, (c0, w) in enumerate(HCOLS):
                    act.activation(dinv[:, HALF * hf + c0:HALF * hf + c0 + w], psA[2 * hf + m][:, 0:w],
                                   ACT.Sqrt).then_inc(sqrt_ok, 1)
            act.wait_ge(var_ok, 1)
            act.activation(std[:, :], mv[:, :, 1], ACT.Sqrt, bias=epsc[:, 0:1]).then_inc(std_ok, 1)
            act.wait_ge(ln_ok, 1)

            def normalise(b):
                if b >= 2:
                    act.wait_ge(tr, b - 1)
                act.activation(H[:, b % 2, :], X[:, b, :], ACT.Relu, bias=shift[:, b:b + 1],
                               scale=rstd[:, b:b + 1]).then_inc(h_ok, 1)

            normalise(0)
            for b in range(NB):
                if b + 1 < NB:
                    normalise(b + 1)
                act.wait_ge(tr, b + 1)
                act.copy(HT[:, :, b * P:(b + 1) * P],
                         psB[2 + b % 2][:, :].rearrange("p (c n) -> p c n", c=4)).then_inc(trc, 1)
            act.wait_ge(col_ok, 1)
            for b in range(NB):
                act.wait_ge(g1m, b + 1)
                act.activation(N1[:, b, :], psB[b % 2][:, 0:P], ACT.Copy, scale=dcol[:, b:b + 1]).then_inc(g1c, 1)
            n = 0
            for hf in range(2):
                for c0, w in HCOLS:
                    act.wait_ge(l1v, n + 1)
                    at = HALF * hf + c0
                    act.activation(H1T[:, at:at + w], SC[:, at:at + w], ACT.Relu, bias=b1c[:, 0:1]).then_inc(l1c, 1)
                    n += 1
            for b in range(NB):
                act.wait_ge(g2m, b + 1)
                act.activation(N2[:, b, :], psB[b % 2][:, 0:SW], ACT.Copy, scale=dcol[:, b:b + 1]).then_inc(g2c, 1)
            act.wait_ge(l2v, 1)
            act.activation(Z, SC[:, 0:HALF], ACT.Identity, bias=b2c[:, 0:1]).then_inc(zc, 1)
            n = 0
            for hf in range(2):
                for m, (c0, w) in enumerate(HCOLS):
                    act.wait_ge(y1m, n + 1)
                    at = HALF * hf + c0
                    act.activation(Y1T[:, at:at + w], psB[2 * hf + m][:, 0:w], ACT.Relu, bias=bd1c[:, 0:1]).then_inc(y1c, 1)
                    n += 1
            n = 0
            for c0, w in COLS:
                for m in range(2):
                    act.wait_ge(y2m, n + 1)
                    act.activation(Y2T[:, m, c0:c0 + w], psA[n % 4][:, 0:w], ACT.Relu,
                                   bias=bd2c[:, m:m + 1]).then_inc(y2c, 1)
                    n += 1

        @block.vector
        def _(dve):
            chain = Chain(dve, v_chain)
            for b in range(SB):
                hf = b * SW // HALF
                rows = slice(SW * hf, SW * hf + SW)
                col = b * SW - HALF * hf
                last = dve.tensor_tensor(AT[rows, b, col:col + SW], AT[rows, b, col:col + SW], ident[rows, rows], ALU.add)
            chain.link(last)
            dve.tensor_reduce(dsum[:, :], AT[:, :, :].rearrange("p b n -> p n b"), AX_X, ALU.add).then_inc(deg_ok, 1)
            dve.wait_ge(ev1, 13)
            dve.tensor_tensor(ST[:, :], relS[:, :], absS[:, :], ALU.add).then_inc(softS, 1)
            dve.wait_ge(sqrt_ok, 4)
            dve.reciprocal(dinv[:, :], dinv[:, :]).then_inc(dinv_ok, 1)
            for b in range(NB):
                dve.wait_ge(mm2, b + 1)
                dve.tensor_tensor(X[:, b, 0:C], psB[b % 2][:, 0:C], X[:, b, 0:C], ALU.add)
                xv = X[:, b, C:D].rearrange("p (d i) -> p i d", i=3)
                dve.tensor_tensor(xv, psB[b % 2][:, C:D].rearrange("p (i d) -> p i d", i=3), xv, ALU.add).then_inc(x_new, 1)
                dve.wait_ge(x_new, b + 1)
                last = dve.bn_stats(stats[:, b, :], X[:, b, :])
            chain.link(last)
            for b in range(NB):
                last = dve.bn_aggr(mv[:, b, :], stats[:, b, :])
            last.then_inc(var_ok, 1)
            dve.wait_ge(std_ok, 1)
            chain.link(dve.reciprocal(rstd[:, :], std[:, :]))
            dve.scalar_tensor_tensor(out=shift[:, :], in0=mv[:, :, 0], scalar=-1.0, in1=rstd[:, :],
                                     op0=ALU.mult, op1=ALU.mult).then_inc(ln_ok, 1)
            dve.wait_ge(col_mm, 1)
            dve.tensor_copy(dcol[:, :], psA[0][:, 0:NB]).then_inc(col_ok, 1)
            dve.wait_ge(h_ok, NB)
            chain.link(dve.tensor_tensor(X[:, :, :], X[:, :, :],
                                         spread(bd3r[:, :].rearrange("p (o d) -> p o d", o=1), 1, NB), ALU.add))
            dve.wait_ge(l1m, 1)
            for hf in range(2):
                for m, (c0, w) in enumerate(HCOLS):
                    at = HALF * hf + c0
                    dve.tensor_tensor(SC[:, at:at + w], psA[2 * hf + m][:, 0:w], dinv[:, at:at + w],
                                      ALU.mult).then_inc(l1v, 1)
            dve.wait_ge(l2m, 1)
            dve.wait_ge(l1c, 4)
            for hf in range(2):
                rows = slice(SW * hf, SW * hf + SW)
                for m, (c0, w) in enumerate(HCOLS):
                    at = HALF * hf + c0
                    last = dve.tensor_tensor(SC[rows, c0:c0 + w], psA[m][rows, 0:w], dinv[rows, at:at + w], ALU.mult)
            last.then_inc(l2v, 1)
            for b in range(NB):
                dve.wait_ge(y3m, b + 1)
                if b >= 2:
                    dve.wait_ge(s_out[b % 2], 16 * (b // 2))
                dve.tensor_tensor(YO[:, b % 2, :], psB[b % 4][:, :], X[:, b, :], ALU.add).then_inc(y3c, 1)


_INS = ["x", "src", "dst", "edge_attr_20", "edge_attr_3", "edge_weight",
        "L0_gnn_W_in2f_s", "L0_gnn_W_in2f_v", "L0_gnn_Wf1", "L0_gnn_bf1", "L0_gnn_Wf2", "L0_gnn_bf2",
        "L0_gnn_W1_s", "L0_gnn_W1_v", "L0_gnn_W2_s", "L0_gnn_W2_v",
        "L1_gnn_W1", "L1_gnn_b1", "L1_gnn_W2", "L1_gnn_b2", "L1_gnn_Wd1", "L1_gnn_bd1",
        "L1_gnn_Wd2", "L1_gnn_bd2", "L1_gnn_Wd3", "L1_gnn_bd3"]


def kernel(**inputs):
    import numpy as _np
    import concourse.bacc as _bacc
    from concourse import mybir as _mybir
    from concourse.bass_utils import run_bass_kernel_spmd as _run

    nc = _bacc.Bacc("TRN2", target_bir_lowering=False, num_devices=1)
    arrays, args = {}, {}
    for name in _INS:
        v = _np.ascontiguousarray(inputs[name])
        arrays[f"in_{name}_dram"] = v
        args[name] = nc.dram_tensor(f"in_{name}_dram", v.shape, _mybir.dt.from_np(v.dtype), kind="ExternalInput").ap()
    out = nc.dram_tensor("out_0_dram", (N, D), _mybir.dt.float32, kind="ExternalOutput").ap()
    gnn_kernel(nc, args, out)
    r = _run(nc, [arrays], core_ids=[0])
    return r.results[0]["out_0_dram"]
```

```python
from contextlib import ExitStack

import numpy as np

import concourse.bass as bass
import concourse.mybir as mybir

F32 = mybir.dt.float32
BF16 = mybir.dt.bfloat16
F16 = mybir.dt.float16
I32 = mybir.dt.int32
U32 = mybir.dt.uint32
F32R = mybir.dt.float32r
ALU = mybir.AluOpType
ACT = mybir.ActivationFunctionType
AX_X = mybir.AxisListType.X

P = 128
N = 1250
NB = (N + P - 1) // P
NPAD = NB * P
LAST = N - (NB - 1) * P
E = 21250
EP, EC = 125, 170
SW = 64
SB = NPAD // SW
HALF = NPAD // 2
GT = 3
GROUPS = 62
NT = GROUPS * GT
assert NT >= (E + SB * (P - 1)) // P and GROUPS % 2 == 0
NTX = NT + 3 * GT
D = 512
C = 128
RBF = 20
RW = 32
CO, SRCL, KEYS, KEYD, DST = 20, 24, 25, 26, 27
NOBODY = 2000.0
Y0 = float(1.0 / np.sqrt(4.0 * np.pi))
Y1 = float(np.sqrt(3.0 / (4.0 * np.pi)))
EPS = 1e-5
UPPER = -(1 << 12)
UN = 2 * GT
TW = NTX + NTX % 2
BC = 10
BATCHES = EC // BC
assert BATCHES % 2 == 1 and EC % BC == 0


def gnn_kernel(nc, a, out):
    ctx = ExitStack()
    with ctx:
        def sem(name):
            return ctx.enter_context(nc.semaphore(name))

        def keep(name, shape, dt):
            return ctx.enter_context(nc.sbuf_tensor(name, shape, dt))

        rec_dram = nc.dram_tensor("rec_dram", [E + 1, RW], F32).ap()
        node_dram = nc.dram_tensor("node_dram", [NPAD, D], F32).ap()

        AGG = keep("AGG", [P, SB, D], F32)
        AT = keep("AT", [P, SB, HALF], F32)
        X = keep("X", [P, NB, D], F32)
        EIDX = keep("EIDX", [P, NTX], U32)
        FLUSH = keep("FLUSH", [1, NT // UN], I32)
        BLOCK = keep("BLOCK", [1, NT + 1], I32)
        ident = keep("ident", [P, P], F32)
        onesf = keep("onesf", [P, P], F32)
        w2u = keep("w2u", [P, D], F32R)
        w2r = keep("w2r", [P, D], F32R)
        bias3 = keep("bias3", [3, D], BF16)
        ones3 = keep("ones3", [3, P], BF16)
        wf1 = keep("wf1", [GT * RW, GT, C], F32)
        bf1c = keep("bf1c", [P, 1], F32)
        w1s = keep("w1s", [P, 2, C], F32)
        w1v = keep("w1v", [P, 2, C], F32)
        w2s = keep("w2s", [P, C], F32)
        w2v = keep("w2v", [P, C], F32)
        w1T = keep("w1T", [P, 4, P], F32)
        w2T = keep("w2T", [P, SW], F32)
        wd1T = keep("wd1T", [P, P], F32)
        wd2T = keep("wd2T", [P, 2 * P], F32)
        wd3T = keep("wd3T", [P, 2, D], F32)
        b1c = keep("b1c", [P, 1], F32)
        b2c = keep("b2c", [P, 1], F32)
        bd1c = keep("bd1c", [P, 1], F32)
        bd2c = keep("bd2c", [P, 2], F32)
        bd3r = keep("bd3r", [P, D], F32)
        epsc = keep("epsc", [P, 1], F32)
        halfc = keep("halfc", [P, 1], F32)
        iota64 = keep("iota64", [P, SW], F32)
        iotah = keep("iotah", [P, HALF], F16)

        prologue(nc, a, locals())
        edge_loop(nc, locals())
        epilogue(nc, out, locals())


def spread(ap, axis, n):
    shape = list(ap.shape)
    shape[axis] = n
    return ap.broadcast_to(shape)


class Chain:

    def __init__(self, engine, semaphore):
        self.engine, self.semaphore, self.count = engine, semaphore, 0

    def link(self, instruction):
        self.count += 1
        instruction.then_inc(self.semaphore, 1)
        self.engine.wait_ge(self.semaphore, self.count)


def prologue(nc, a, k):
    AGG, AT, X, EIDX, FLUSH = k["AGG"], k["AT"], k["X"], k["EIDX"], k["FLUSH"]
    ident, onesf = k["ident"], k["onesf"]
    rec_dram, node_dram = k["rec_dram"], k["node_dram"]
    w2u, w2r, bias3, ones3, wf1 = k["w2u"], k["w2r"], k["bias3"], k["ones3"], k["wf1"]
    with ExitStack() as ctx:
        def sb(name, shape, dt):
            return ctx.enter_context(nc.sbuf_tensor("sort_" + name, shape, dt))

        def ps(name, shape, dt=F32):
            return ctx.enter_context(nc.psum_tensor("sort_" + name, shape, dt))

        def sem(name):
            return ctx.enter_context(nc.semaphore("sort_" + name))

        REC = sb("REC", [EP, EC, RW], F32)
        rec0 = sb("rec0", [1, RW], F32)
        srci = sb("srci", [EP, EC], I32)
        dsti = sb("dsti", [EP, EC], I32)
        tmpi = sb("tmpi", [EP, EC], I32)
        dirs = sb("dirs", [EP, EC, 3], F32)
        rcut = sb("rcut", [EP, EC], F32)
        norm = sb("norm", [EP, EC], F32)
        gain = sb("gain", [EP, EC], F32)
        hi = sb("hi", [EP, EC], F32)
        blkf = sb("blkf", [EP, EC], F32)
        lane = sb("lane", [EP, EC], BF16)
        tile = sb("tile", [EP, EC], BF16)
        maskflat = AT[:, :, :].rearrange("p b d -> p (b d)")[0:EP, 0:SB * EC]
        MASK = maskflat.rearrange("p (b c) -> p b c", b=SB)
        scanflat = AGG[:, :, :].rearrange("p b d -> p (b d)")[0:EP, 0:SB * EC]
        SCAN = scanflat.rearrange("p (b c) -> p b c", b=SB)
        zeros = sb("zeros", [EP, 2 * TW], BF16)
        tno = sb("tno", [P, 2], F32)
        le = sb("le", [P, 2, SB - 1], F32)
        ended = sb("ended", [P, 2], F32)
        cum = sb("cum", [EP, SB], F32)
        cumx = sb("cumx", [EP, SB], F32)
        cnt = sb("cnt", [EP, SB], F32)
        adj = sb("adj", [EP, SB], F32)
        nti = sb("nti", [P, SB], I32)
        ntf = sb("ntf", [P, SB], F32)
        incl = sb("incl", [P, SB], F32)
        excl = sb("excl", [P, SB], F32)
        blkt = sb("blkt", [1, NT + 2], F32)
        neq = sb("neq", [1, NT + 1], F32)
        bits = sb("bits", [1, NT // UN, UN], F32)
        mask = sb("mask", [1, NT // UN], F32)
        upper = sb("upper", [P, P], F32)
        iotab = sb("iotab", [P, SB], F32)
        steps = sb("steps", [P, TW, BC], BF16)
        colno = sb("colno", [P, EC], BF16)
        partno = sb("partno", [P, 1], F32)
        lhot = sb("lhot", [EP, 2, P, BC], BF16)
        lpart = sb("lpart", [EP, 2, P, BC], BF16)
        lcol = sb("lcol", [EP, 2, P, BC], BF16)
        thot = sb("thot", [EP, 2, TW, BC], BF16)
        eidf = sb("eidf", [P, NTX], F32)
        win = sb("win", [P, 2, C], F32)
        w1raw = sb("w1raw", [P, D], F32)
        w2raw = sb("w2raw", [SW, P], F32)
        wd1raw = sb("wd1raw", [P, 2, SW], F32)
        wd2raw = sb("wd2raw", [P, 2, P], F32)
        wd3raw = sb("wd3raw", [P, 4, 2 * P], F32)
        stats = sb("stats", [P, NB, 6], F32)
        mv = sb("mv", [P, NB, 2], F32)
        std = sb("std", [P, NB], F32)
        rstd = sb("rstd", [P, NB], F32)
        shift = sb("shift", [P, NB], F32)
        spare = AGG[:, :, :].rearrange("p b d -> p (b d)")[:, SB * EC + EC:]
        H = spare[:, 0:2 * D].rearrange("p (i d) -> p i d", i=2)
        HT = spare[:, 2 * D:4 * D].rearrange("p (i c n) -> p i c n", i=2, c=4)
        GS = spare[:, 4 * D:6 * D].rearrange("p (i d) -> p i d", i=2)
        bf2r, bsum, bres = (spare[0:3, D * i:D * (i + 1)] for i in (6, 7, 8))
        bhi, bmid = (spare[0:3, D * 9:D * 10].bitcast(BF16)[:, D * i:D * (i + 1)] for i in (0, 1))
        wf2raw = spare[:, 12 * D:13 * D]
        bpick = bf2r
        w2p = spare[:, 11 * D:12 * D]
        w2cut = spare[:, 10 * D:11 * D]
        sq = spare[0:EP, 10 * D:10 * D + 3 * EC].rearrange("p (c i) -> p c i", i=3)

        psT = ps("psT", [P, 2, D])
        psG = ps("psG", [P, 2, D])
        psW = ps("psW", [P, D])
        psC = ps("psC", [P, D])
        psE = ps("psE", [P, D])
        psR = ps("psR", [P, D])

        s_edges = sem("s_edges")
        s_attr = sem("s_attr")
        s_dirs = sem("s_dirs")
        s_x = sem("s_x")
        s_weights = sem("s_weights")
        s_raw = sem("s_raw")
        s_xzero = sem("s_xzero")
        s_const = sem("s_const")
        s_iden = sem("s_iden")
        s_steps = sem("s_steps")
        s_rec = sem("s_rec")
        s_recs = sem("s_recs")
        s_norm2 = sem("s_norm2")
        s_norm = sem("s_norm")
        s_cnt = sem("s_cnt")
        s_tot = sem("s_tot")
        s_pos = sem("s_pos")
        s_ended = sem("s_ended")
        s_row = sem("s_row")
        s_lane = sem("s_lane")
        s_hot = sem("s_hot")
        s_part = sem("s_part")
        s_hotfree = sem("s_hotfree")
        s_perm = sem("s_perm")
        s_var = sem("s_var")
        s_std = sem("s_std")
        s_ln = sem("s_ln")
        s_h = sem("s_h")
        s_ht = sem("s_ht")
        s_htc = sem("s_htc")
        s_g = sem("s_g")
        s_gc = sem("s_gc")
        s_gout = [sem(f"s_gout{i}") for i in range(2)]
        s_wt = sem("s_wt")
        s_wtc = sem("s_wtc")
        s_bias = sem("s_bias")
        s_w2 = sem("s_w2")
        v_chain = sem("v_chain")
        p_chain = sem("p_chain")
        p_zero = sem("p_zero")
        block = ctx.enter_context(nc.Block())

        @block.sync
        def _(sp):
            sp.dma_start(srci[:, :], a["src"].rearrange("(p c) -> p c", p=EP)).then_inc(s_edges, 16)
            sp.dma_start(dsti[:, :], a["dst"].rearrange("(p c) -> p c", p=EP)).then_inc(s_edges, 16)
            sp.dma_start(dirs[:, :, :], a["edge_attr_3"].rearrange("(p c) i -> p c i", p=EP)).then_inc(s_dirs, 16)
            sp.dma_start(rcut[:, :], a["edge_weight"].rearrange("(p c) -> p c", p=EP)).then_inc(s_dirs, 16)
            sp.wait_ge(s_xzero, 1)
            sp.dma_start(X[:, 0:NB - 1, :],
                         a["x"][0:(NB - 1) * P, :].rearrange("(b p) d -> p b d", p=P)).then_inc(s_x, 16)
            sp.dma_start(X[0:LAST, NB - 1, :], a["x"][(NB - 1) * P:N, :]).then_inc(s_x, 16)
            for i, name in enumerate(("W_in2f_s", "W_in2f_v")):
                sp.dma_start(win[:, i, :], a["L0_gnn_" + name]).then_inc(s_raw, 16)
            sp.dma_start(w1raw[:, :], a["L1_gnn_W1"]).then_inc(s_raw, 16)
            sp.dma_start(w2raw[:, :], a["L1_gnn_W2"]).then_inc(s_raw, 16)
            for i in range(2):
                sp.dma_start(wd1raw[:, i, :], a["L1_gnn_Wd1"]).then_inc(s_raw, 16)
            sp.dma_start(wd2raw[:, :, :], a["L1_gnn_Wd2"].rearrange("(j p) n -> p j n", p=P)).then_inc(s_raw, 16)
            sp.dma_start(wd3raw[:, :, :], a["L1_gnn_Wd3"].rearrange("(j p) n -> p j n", p=P)).then_inc(s_raw, 16)
            sp.dma_start(wf2raw, a["L0_gnn_Wf2"][:, 0:D]).then_inc(s_raw, 16)
            for i in range(3):
                sp.dma_start(bf2r[i:i + 1, :], a["L0_gnn_bf2"][0:D].rearrange("(o n) -> o n", o=1)).then_inc(s_raw, 16)
            for b in range(NB):
                sp.wait_ge(s_gc, b + 1)
                sp.dma_start(node_dram[b * P:(b + 1) * P, :], GS[:, b % 2, :]).then_inc(s_gout[b % 2], 16)
            sp.wait_ge(s_rec, 1)
            sp.dma_start(rec_dram[1:E + 1, :].rearrange("(p c) w -> p c w", p=EP), REC[:, :, :]).then_inc(s_recs, 16)
            sp.dma_start(rec_dram[0:1, :], rec0[:, :]).then_inc(s_recs, 16)
            for i in range(2):
                sp.wait_ge(s_gout[i], 16 * (NB // 2))
            sp.wait_ge(s_recs, 32)

        @block.scalar
        def _(act):
            act.dma_start(REC[:, :, 0:RBF], a["edge_attr_20"].rearrange("(p c) w -> p c w", p=EP)).then_inc(s_attr, 16)
            n = 0
            act.wait_ge(s_xzero, 2)
            for i in range(GT):
                act.dma_start(wf1[RW * i:RW * i + RBF, i, :], a["L0_gnn_Wf1"]).then_inc(s_weights, 16)
            act.dma_start(k["bf1c"][:, :], a["L0_gnn_bf1"].rearrange("(p o) -> p o", o=1)).then_inc(s_weights, 16)
            for w, name in ((k["w1s"], "W1_s"), (k["w1v"], "W1_v")):
                act.dma_start(w[:, :, :], a["L0_gnn_" + name].rearrange("(f k) c -> f k c", k=2)).then_inc(s_weights, 16)
            for w, name in ((k["w2s"], "W2_s"), (k["w2v"], "W2_v")):
                act.dma_start(w[:, :], a["L0_gnn_" + name]).then_inc(s_weights, 16)
            act.dma_start(k["b1c"][:, :], a["L1_gnn_b1"].rearrange("(p o) -> p o", o=1)).then_inc(s_weights, 16)
            for i in range(2):
                act.dma_start(k["b2c"][SW * i:SW * i + SW, :],
                              a["L1_gnn_b2"].rearrange("(p o) -> p o", o=1)).then_inc(s_weights, 16)
            act.dma_start(k["bd1c"][:, :], a["L1_gnn_bd1"].rearrange("(p o) -> p o", o=1)).then_inc(s_weights, 16)
            for i in range(2):
                act.dma_start(k["bd2c"][:, i:i + 1],
                              a["L1_gnn_bd2"][P * i:P * i + P].rearrange("(p o) -> p o", o=1)).then_inc(s_weights, 16)
            act.dma_start(k["bd3r"][:, :], spread(a["L1_gnn_bd3"].rearrange("(o n) -> o n", o=1), 0, P)).then_inc(s_weights, 16)
            for n, dst in enumerate((k["w1T"][:, :, :].rearrange("p c n -> p (c n)"), None,
                                     k["wd3T"][:, 0, :], k["wd3T"][:, 1, :])):
                act.wait_ge(s_wt, n + 1)
                if dst is not None:
                    act.copy(dst, psW[:, :]).then_inc(s_wtc, 1)
                else:
                    act.copy(k["w2T"][:, :], psW[:, 0:SW])
                    act.copy(k["wd1T"][:, :], psW[:, P:2 * P])
                    act.copy(k["wd2T"][:, :], psW[:, 2 * P:4 * P]).then_inc(s_wtc, 1)
            act.wait_ge(s_var, 1)
            act.wait_ge(s_const, 1)
            act.activation(std[:, :], mv[:, :, 1], ACT.Sqrt, bias=k["epsc"][:, 0:1]).then_inc(s_std, 1)
            act.wait_ge(s_norm2, 1)
            act.activation(norm[:, :], gain[:, :], ACT.Sqrt).then_inc(s_norm, 1)
            act.wait_ge(s_ln, 1)

            def normalise(b):
                if b >= 2:
                    act.wait_ge(s_ht, b - 1)
                act.activation(H[:, b % 2, :], X[:, b, :], ACT.Relu, bias=shift[:, b:b + 1],
                               scale=rstd[:, b:b + 1]).then_inc(s_h, 1)

            def turned(b):
                act.wait_ge(s_ht, b + 1)
                if b >= 2:
                    act.wait_ge(s_g, b - 1)
                act.copy(HT[:, b % 2, :, :].rearrange("p c n -> p (c n)"), psT[:, b % 2, :]).then_inc(s_htc, 1)

            normalise(0)
            normalise(1)
            turned(0)
            for b in range(NB):
                if b + 2 < NB:
                    normalise(b + 2)
                if b + 1 < NB:
                    turned(b + 1)
                act.wait_ge(s_g, b + 1)
                if b >= 2:
                    act.wait_ge(s_gout[b % 2], 16 * (b // 2))
                act.mul(GS[:, b % 2, :], psG[:, b % 2, :], float(C) ** -0.5).then_inc(s_gc, 1)

            def scale_lanes(n, r):
                act.wait_ge(s_lane, n + 1)
                act.activation(lpart[:, r, :, :], lhot[:, r, :, :], ACT.Copy, scale=partno[0:EP, :]).then_inc(s_part, 1)

            with act.Fori(0, BATCHES // 2) as i:
                for r in range(2):
                    scale_lanes(2 * i + r, r)
            scale_lanes(BATCHES - 1, 0)
            act.wait_ge(s_weights, 16 * 15)

        @block.gpsimd
        def _(pool):
            chain = Chain(pool, p_chain)
            pool.memset(X[:, NB - 1, :], 0.0).then_inc(s_xzero, 1)
            pool.memset(wf1[:, :, :], 0.0).then_inc(s_xzero, 1)
            pool.memset(k["epsc"][:, :], EPS)
            pool.memset(k["halfc"][:, :], 0.5)
            pool.memset(zeros[:, :], 0.0)
            pool.memset(ones3[:, :], 1.0)
            pool.memset(REC[:, :, DST + 1:RW], 0.0)
            chain.link(pool.memset(rec0[:, :], 0.0))
            chain.link(pool.memset(rec0[:, SRCL:KEYD + 1], NOBODY))
            pool.iota(iotab[:, :], [[1, SB]], base=0, channel_multiplier=0, allow_small_or_imprecise_dtypes=True)
            pool.iota(colno[:, :], [[1, EC]], base=1, channel_multiplier=0, allow_small_or_imprecise_dtypes=True)
            pool.iota(partno[:, :], [[0, 1]], base=0, channel_multiplier=1, allow_small_or_imprecise_dtypes=True)
            pool.iota(tno[:, :], [[P, 2]], base=0, channel_multiplier=1, allow_small_or_imprecise_dtypes=True)
            pool.iota(k["iota64"][:, :], [[1, SW]], base=0, channel_multiplier=0, allow_small_or_imprecise_dtypes=True)
            pool.iota(k["iotah"][:, :], [[1, HALF]], base=0, channel_multiplier=0, allow_small_or_imprecise_dtypes=True)
            chain.link(pool.memset(onesf[:, :], 1.0))
            chain.link(pool.affine_select(out=ident[:, :], in_=onesf[:, :], compare_op=ALU.is_equal, fill=0.0, base=0,
                                          pattern=[[-1, P]], channel_multiplier=1))
            pool.affine_select(out=upper[:, :], in_=onesf[:, :], compare_op=ALU.is_ge, fill=0.0, base=-1,
                               pattern=[[1, P]], channel_multiplier=-1).then_inc(s_const, 1)
            pool.wait_ge(s_const, 1)
            pool.sem_inc(s_iden, 1)
            pool.iota(steps[:, :, :], [[1, TW], [0, BC]], base=0, channel_multiplier=0,
                      allow_small_or_imprecise_dtypes=True).then_inc(s_steps, 1)
            pool.wait_ge(s_raw, 16 * 12)
            pool.tensor_copy(w2p.rearrange("p (k h f) -> p h f k", k=2, h=2),
                             wf2raw.rearrange("p (h f k) -> p h f k", h=2, k=2)).then_inc(s_w2, 1)
            chain.link(pool.tensor_copy(bsum[:, :].rearrange("p (k h f) -> p h f k", k=2, h=2),
                                        bf2r[:, :].rearrange("p (h f k) -> p h f k", h=2, k=2)))
            chain.link(pool.tensor_copy(bhi[:, :], bsum[:, :]))
            chain.link(pool.tensor_tensor(bres[:, :], bsum[:, :], bhi[:, :], ALU.subtract))
            chain.link(pool.tensor_copy(bmid[:, :], bres[:, :]))
            chain.link(pool.tensor_tensor(bres[:, :], bres[:, :], bmid[:, :], ALU.subtract))
            chain.link(pool.tensor_scalar(bsum[:, :], bhi[:, :], ident[0:3, 0:1], None, ALU.mult))
            chain.link(pool.tensor_scalar(bpick[:, :], bmid[:, :], ident[0:3, 1:2], None, ALU.mult))
            chain.link(pool.tensor_tensor(bsum[:, :], bsum[:, :], bpick[:, :], ALU.add))
            chain.link(pool.tensor_scalar(bpick[:, :], bres[:, :], ident[0:3, 2:3], None, ALU.mult))
            pool.tensor_tensor(bias3[:, :], bsum[:, :], bpick[:, :], ALU.add).then_inc(s_bias, 1)
            pool.wait_ge(s_weights, 16 * 15)
            pool.tensor_scalar(k["w1s"][:, 0, :], k["w1s"][:, 0, :], float(2 * C) ** -0.5, None, ALU.mult)
            pool.tensor_scalar(k["w1s"][:, 1, :], k["w1s"][:, 1, :], float(6 * C) ** -0.5, None, ALU.mult)
            pool.tensor_scalar(k["w1v"][:, :, :], k["w1v"][:, :, :], float(2 * C) ** -0.5, None, ALU.mult)
            pool.tensor_scalar(k["w2s"][:, :], k["w2s"][:, :], float(C) ** -0.5, None, ALU.mult)
            chain.link(pool.tensor_scalar(k["w2v"][:, :], k["w2v"][:, :], float(C) ** -0.5, None, ALU.mult))
            pool.wait_ge(s_pos, 1)
            pool.memset(AT[:, :, :], 0.0).then_inc(p_zero, 1)
            for i in range(2):
                pool.wait_ge(s_gout[i], 16 * (NB // 2))
            pool.wait_ge(s_bias, 1)
            pool.wait_ge(s_w2, 2)
            pool.memset(AGG[:, :, :], 0.0).then_inc(p_zero, 1)
            pool.wait_ge(p_zero, 2)

        @block.vector
        def _(dve):
            chain = Chain(dve, v_chain)
            link = chain.link
            dve.wait_ge(s_edges, 32)
            link(dve.tensor_scalar(tmpi[:, :], srci[:, :], 6, None, ALU.logical_shift_right))
            link(dve.tensor_copy(blkf[:, :], tmpi[:, :]))
            link(dve.tensor_scalar(tmpi[:, :], srci[:, :], SW - 1, None, ALU.bitwise_and))
            dve.tensor_scalar(hi[:, :], dsti[:, :], float(HALF), None, ALU.is_ge).then_inc(v_chain, 1)
            chain.count += 1
            dve.tensor_copy(REC[:, :, SRCL], tmpi[:, :]).then_inc(v_chain, 1)
            chain.count += 1
            link(dve.tensor_copy(REC[:, :, DST].bitcast(U32), dsti[:, :]))
            dve.scalar_tensor_tensor(out=REC[:, :, KEYS], in0=hi[:, :], scalar=float(SW), in1=REC[:, :, SRCL],
                                     op0=ALU.mult, op1=ALU.add)
            dve.scalar_tensor_tensor(out=REC[:, :, KEYD], in0=hi[:, :], scalar=-float(HALF), in1=dsti[:, :],
                                     op0=ALU.mult, op1=ALU.add)
            dve.wait_ge(s_iden, 1)
            link(dve.tensor_tensor(MASK, spread(blkf[:, :].rearrange("p (o c) -> p o c", o=1), 1, SB),
                                   spread(iotab[0:EP, :].rearrange("p (b o) -> p b o", o=1), 2, EC), ALU.is_equal))
            link(dve.tensor_tensor_scan(scanflat, maskflat, spread(zeros[:, 0:1], 1, SB * EC), 0.0, ALU.add, ALU.add))
            link(dve.tensor_copy(cum[:, :], SCAN[:, :, EC - 1]))
            link(dve.memset(cumx[:, 0:1], 0.0))
            link(dve.tensor_copy(cumx[:, 1:SB], cum[:, 0:SB - 1]))
            dve.tensor_tensor(cnt[:, :], cum[:, :], cumx[:, :], ALU.subtract).then_inc(s_cnt, 1)
            dve.wait_ge(s_x, 32)
            for b in range(NB):
                bn = dve.bn_stats(stats[:, b, :], X[:, b, :])
            link(bn)
            for b in range(NB):
                bn = dve.bn_aggr(mv[:, b, :], stats[:, b, :])
            bn.then_inc(s_var, 1)
            dve.wait_ge(s_dirs, 32)
            link(dve.tensor_tensor(sq, dirs[:, :, :], dirs[:, :, :], ALU.mult))
            dve.tensor_reduce(gain[:, :], sq, AX_X, ALU.add).then_inc(s_norm2, 1)
            dve.wait_ge(s_tot, 1)
            link(dve.tensor_scalar(nti[:, :], psC[:, SB:2 * SB], float(P - 1), None, ALU.add))
            link(dve.tensor_scalar(nti[:, :], nti[:, :], 7, None, ALU.logical_shift_right))
            link(dve.tensor_copy(ntf[:, :], nti[:, :]))
            link(dve.tensor_tensor_scan(incl[:, :], ntf[:, :], onesf[:, 0:SB], 0.0, ALU.add, ALU.mult))
            link(dve.tensor_tensor(le[:, :, :], spread(tno[:, :].rearrange("p (t o) -> p t o", o=1), 2, SB - 1),
                                   spread(incl[:, 0:SB - 1].rearrange("p (o b) -> p o b", o=1), 1, 2), ALU.is_ge))
            dve.tensor_reduce(ended[:, :], le[:, :, :], AX_X, ALU.add).then_inc(s_ended, 1)
            link(dve.tensor_tensor(excl[:, :], incl[:, :], ntf[:, :], ALU.subtract))
            link(dve.tensor_tensor(adj[:, :], psC[0:EP, 0:SB], cumx[:, :], ALU.subtract))
            link(dve.scalar_tensor_tensor(out=adj[:, :], in0=excl[0:EP, :], scalar=float(P), in1=adj[:, :],
                                          op0=ALU.mult, op1=ALU.add))
            link(dve.tensor_tensor(SCAN, SCAN,
                                   spread(adj[:, :].rearrange("p (b o) -> p b o", o=1), 2, EC), ALU.add))
            dve.wait_ge(s_std, 1)
            link(dve.reciprocal(rstd[:, :], std[:, :]))
            dve.scalar_tensor_tensor(out=shift[:, :], in0=mv[:, :, 0], scalar=-1.0, in1=rstd[:, :],
                                     op0=ALU.mult, op1=ALU.mult).then_inc(s_ln, 1)
            link(dve.tensor_tensor(SCAN, SCAN, MASK, ALU.mult))
            link(dve.tensor_reduce(blkf[:, :], SCAN.rearrange("p b c -> p c b"), AX_X, ALU.add))
            link(dve.tensor_scalar(tmpi[:, :], blkf[:, :], -1.0, None, ALU.add))
            link(dve.tensor_scalar(dsti[:, :], tmpi[:, :], 7, None, ALU.logical_shift_right))
            link(dve.tensor_copy(tile[:, :], dsti[:, :]))
            link(dve.tensor_scalar(tmpi[:, :], tmpi[:, :], P - 1, None, ALU.bitwise_and))
            dve.tensor_copy(lane[:, :], tmpi[:, :]).then_inc(s_pos, 1)
            dve.wait_ge(s_pos, 1)
            dve.wait_ge(s_norm, 1)
            link(dve.reciprocal(norm[:, :], norm[:, :]))
            link(dve.scalar_tensor_tensor(out=gain[:, :], in0=norm[:, :], scalar=Y1, in1=rcut[:, :],
                                          op0=ALU.mult, op1=ALU.mult))
            dve.wait_ge(s_attr, 16)
            for i in range(3):
                link(dve.tensor_tensor(REC[:, :, CO + 1 + i], dirs[:, :, i], gain[:, :], ALU.mult))
            dve.tensor_scalar(REC[:, :, CO], rcut[:, :], Y0, None, ALU.mult).then_inc(s_rec, 1)
            dve.wait_ge(s_row, 1)
            link(dve.tensor_copy(blkt[:, 1:NT + 2], psR[0:1, 0:NT + 1]))
            link(dve.tensor_scalar(blkt[:, 0:1], blkt[:, 1:2], 0.0, None, ALU.add))
            link(dve.memset(blkt[:, NT + 1:NT + 2], float(SB)))
            link(dve.tensor_tensor(neq[:, :], blkt[:, 0:NT + 1], blkt[:, 1:NT + 2], ALU.not_equal))
            for u in range(UN):
                last = dve.tensor_scalar(bits[:, :, u], neq[:, 0:NT].rearrange("p (i u) -> p i u", u=UN)[:, :, u],
                                         float(1 << u), None, ALU.mult)
            link(last)
            link(dve.tensor_reduce(mask[:, :], bits[:, :, :], AX_X, ALU.add))
            dve.tensor_copy(FLUSH[:, :], mask[:, :])
            dve.tensor_copy(k["BLOCK"][:, :], blkt[:, 0:NT + 1])
            dve.wait_ge(s_w2, 1)
            link(dve.tensor_scalar(w2cut.bitcast(I32), w2p.bitcast(I32), UPPER, None, ALU.bitwise_and))
            dve.tensor_copy(w2u[:, :], w2cut)
            dve.tensor_tensor(w2r[:, :], w2p, w2cut, ALU.subtract).then_inc(s_w2, 1)
            dve.wait_ge(s_steps, 1)

            def one_hots(n, r):
                dve.wait_ge(s_hotfree, n + 1)
                cols = bass.ds(BC * n, BC)
                dve.tensor_tensor(lhot[:, r, :, :], steps[0:EP, 0:P, :],
                                  spread(lane[:, cols].rearrange("p (o c) -> p o c", o=1), 1, P),
                                  ALU.is_equal).then_inc(s_lane, 1)
                dve.tensor_tensor(thot[:, r, :, :], steps[0:EP, :, :],
                                  spread(tile[:, cols].rearrange("p (o c) -> p o c", o=1), 1, TW), ALU.is_equal)
                dve.wait_ge(s_lane, n + 1)
                dve.tensor_tensor(lcol[:, r, :, :], lhot[:, r, :, :],
                                  spread(colno[0:EP, cols].rearrange("p (o c) -> p o c", o=1), 1, P),
                                  ALU.mult).then_inc(s_hot, 1)

            with dve.Fori(0, BATCHES // 2) as i:
                for r in range(2):
                    one_hots(2 * i + r, r)
            one_hots(BATCHES - 1, 0)
            dve.wait_ge(s_perm, 1)
            link(dve.tensor_scalar(eidf[:, :], psE[:, 0:NTX], float(EC), None, ALU.mult))
            link(dve.tensor_tensor(EIDX[:, :], psE[:, TW:TW + NTX], eidf[:, :], ALU.add))

        @block.tensor
        def _(pe):
            pe.wait_ge(s_cnt, 1)
            pe.wait_ge(s_iden, 1)
            pe.matmul(psC[0:EP, 0:SB], upper[0:EP, 0:EP], cnt[:, :], start=True, stop=True)
            pe.matmul(psC[:, SB:2 * SB], onesf[0:EP, :], cnt[:, :], start=True, stop=True).then_inc(s_tot, 1)

            def transposes(b):
                pe.wait_ge(s_h, b + 1)
                if b >= 2:
                    pe.wait_ge(s_htc, b - 1)
                h = H[:, b % 2, :]
                hv = h[:, C:D].rearrange("p (c i) -> p i c", i=3)
                pe.transpose(psT[:, b % 2, 0:P], h[:, 0:C], ident[:, :])
                for i in range(3):
                    last = pe.transpose(psT[:, b % 2, P * (i + 1):P * (i + 2)], hv[:, i, :], ident[:, :])
                last.then_inc(s_ht, 1)

            pe.wait_ge(s_raw, 16 * 12)
            wd1v = wd1raw[:, :, :].rearrange("p i n -> p (i n)")
            jobs = [
                [(w1raw[:, P * j:P * j + P], P * j, P) for j in range(4)],
                [(w2raw[:, :], 0, SW), (wd1v, P, P), (wd2raw[:, 0, :], 2 * P, P), (wd2raw[:, 1, :], 3 * P, P)],
                [(wd3raw[:, j, 0:P], P * j, P) for j in range(4)],
                [(wd3raw[:, j, P:2 * P], P * j, P) for j in range(4)],
            ]
            for n, job in enumerate(jobs):
                if n:
                    pe.wait_ge(s_wtc, n)
                for src, at, rows in job:
                    last = pe.transpose(psW[:, at:at + rows], src, ident[0:rows, 0:rows])
                last.then_inc(s_wt, 1)
            pe.wait_ge(s_ended, 1)
            pe.matmul(psR[0:1, 0:P], ended[:, 0:1], ident[:, :], start=True, stop=True)
            pe.matmul(psR[0:1, P:2 * P], ended[:, 1:2], ident[:, :], start=True, stop=True).then_inc(s_row, 1)
            pe.matmul(psE[:, 0:2 * TW], zeros[0:1, 0:P], zeros[0:1, 0:2 * TW], start=True, stop=False,
                      skip_group_check=True).then_inc(s_hotfree, 2)
            pe.wait_ge(s_wtc, 4)
            transposes(0)
            for b in range(NB):
                if b + 1 < NB:
                    transposes(b + 1)
                pe.wait_ge(s_htc, b + 1)
                if b >= 2:
                    pe.wait_ge(s_gc, b - 1)
                for c in range(4):
                    last = pe.matmul(psG[:, b % 2, P * c:P * (c + 1)], HT[:, b % 2, c, :], win[:, min(c, 1), :],
                                     start=True, stop=True)
                last.then_inc(s_g, 1)
            def place(n, r):
                pe.wait_ge(s_hot, n + 1)
                pe.wait_ge(s_part, n + 1)
                for c in range(BC):
                    pe.matmul(psE[:, 0:TW], lpart[:, r, :, c], thot[:, r, :, c], start=False, stop=False,
                              skip_group_check=True)
                    last = pe.matmul(psE[:, TW:2 * TW], lcol[:, r, :, c], thot[:, r, :, c], start=False, stop=False,
                                     skip_group_check=True)
                last.then_inc(s_hotfree, 1)

            with pe.Fori(0, BATCHES // 2) as i:
                for r in range(2):
                    place(2 * i + r, r)
            place(BATCHES - 1, 0)
            pe.matmul(psE[:, 0:2 * TW], zeros[0:1, 0:P], zeros[0:1, 0:2 * TW], start=False, stop=True,
                      skip_group_check=True).then_inc(s_perm, 1)


def edge_loop(nc, k):
    AGG, AT, EIDX, FLUSH, BLOCK = k["AGG"], k["AT"], k["EIDX"], k["FLUSH"], k["BLOCK"]
    ident, w2u, w2r, bias3, ones3, wf1, bf1c = k["ident"], k["w2u"], k["w2r"], k["bias3"], k["ones3"], k["wf1"], k["bf1c"]
    halfc, iota64, iotah = k["halfc"], k["iota64"], k["iotah"]
    rec_dram, node_dram = k["rec_dram"], k["node_dram"]
    with ExitStack() as ctx:
        def sb(name, shape, dt):
            return ctx.enter_context(nc.sbuf_tensor("loop_" + name, shape, dt))

        def ps(name, shape, dt=F32):
            return ctx.enter_context(nc.psum_tensor("loop_" + name, shape, dt))

        def sem(name):
            return ctx.enter_context(nc.semaphore("loop_" + name))

        stage = sb("stage", [P, 2, GT], U32)
        rec = sb("rec", [P, 2, GT, RW], F32)
        node = sb("node", [P, 2, GT, D], F32)
        fT = sb("fT", [GT * RW, P], F32)
        absz = sb("absz", [P, GT * P], F32)
        expz = sb("expz", [P, GT * P], F32)
        logz = sb("logz", [P, GT * P], F32)
        relz = sb("relz", [P, GT * P], F32)
        hsum = sb("hsum", [P, GT * P], F32)
        hcut = sb("hcut", [P, GT * P], F32)
        hu = sb("hu", [P, 2, GT * P], F32R)
        hr = sb("hr", [P, 2, GT * P], F32R)
        hot = sb("hot", [P, 2, GT, SW], F32)
        shot = sb("shot", [P, 2, GT, 4, SW], F32)
        khot = sb("khot", [P, 2, GT, P], BF16)
        dhot = sb("dhot", [P, 2, GT, HALF], BF16)
        along = sb("along", [P, 2, GT, C], F32)
        prod = sb("prod", [P, 2, 6, C], F32)
        zrow = sb("zrow", [1, D], BF16)
        zerof = sb("zerof", [P, D], F32)

        psW = ps("psW", [P, 2, D])
        psZ = ps("psZ", [P, D])
        psF = ps("psF", [P, D])
        psA = ps("psA", [P, D])
        psN = ps("psN", [P, 2, D])

        staged = sem("staged")
        rec_in = [sem(f"rec_in{q}") for q in range(2)]
        node_in = [sem(f"node_in{q}") for q in range(2)]
        rec_turned = sem("rec_turned")
        fT_ready = sem("fT_ready")
        z_ready = sem("z_ready")
        z_used = sem("z_used")
        abs_done = sem("abs_done")
        exp_done = sem("exp_done")
        soft_done = sem("soft_done")
        h_added = sem("h_added")
        h_cut = sem("h_cut")
        hu_ready = sem("hu_ready")
        hr_ready = sem("hr_ready")
        hot_ready = sem("hot_ready")
        keys_ready = sem("keys_ready")
        shot_ready = sem("shot_ready")
        along_begun = sem("along_begun")
        along_x = sem("along_x")
        along_ready = sem("along_ready")
        w_ready = sem("w_ready")
        prod_done = sem("prod_done")
        summed = sem("summed")
        copied = sem("copied")
        flushed = [sem(f"flushed{r}") for r in range(2)]
        counts_copied = sem("counts_copied")
        counts_flushed = [sem(f"counts_flushed{r}") for r in range(2)]
        zeroed = sem("zeroed")
        pool_turn = sem("pool_turn")
        block = ctx.enter_context(nc.Block())

        @block.gpsimd
        def _(pool):
            def gather_rec(q):
                for j in range(GT):
                    pool.indirect_dma_start(out=rec[:, q, j, :], out_offset=None, in_=rec_dram,
                                            in_offset=bass.IndirectOffsetOnAxis(ap=stage[:, q, j:j + 1], axis=0)
                                            ).then_inc(rec_in[q], 16)

            def gather_node(q):
                for j in range(GT):
                    pool.indirect_dma_start(out=node[:, q, j, :], out_offset=None, in_=node_dram,
                                            in_offset=bass.IndirectOffsetOnAxis(
                                                ap=rec[:, q, j, DST:DST + 1].bitcast(U32), axis=0)
                                            ).then_inc(node_in[q], 16)

            pool.wait_ge(staged, 1)
            gather_rec(0)
            pool.wait_ge(rec_in[0], 16 * GT)
            gather_node(0)
            pool.wait_ge(staged, 2)
            gather_rec(1)
            with pool.Fori(0, GROUPS // 2) as i:
                for q in range(2):
                    s = 2 * i + q
                    pool.wait_ge(rec_in[1 - q], 16 * GT * (i + 1 + q))
                    pool.wait_ge(prod_done, GT * s + 1)
                    pool.sem_inc(pool_turn, 1)
                    gather_node(1 - q)
                    pool.wait_ge(staged, s + 3)
                    pool.wait_ge(keys_ready, s + 1)
                    pool.wait_ge(shot_ready, s + 1)
                    pool.wait_ge(along_ready, s + 1)
                    pool.wait_ge(rec_turned, s + 1)
                    pool.wait_ge(node_in[q], 16 * GT * (i + 1))
                    pool.sem_inc(pool_turn, 1)
                    gather_rec(q)
            for q in range(2):
                pool.wait_ge(rec_in[q], 16 * GT * (GROUPS // 2 + 1))
            pool.wait_ge(node_in[0], 16 * GT * (GROUPS // 2 + 1))

        @block.scalar
        def _(act):
            def attributes():
                for j in range(GT):
                    rows = slice(RW * j, RW * j + RBF)
                    last = act.copy(fT[rows, :], psF[rows, 0:P])
                last.then_inc(fT_ready, 1)

            def soften(n):
                act.wait_ge(z_ready, n + 1)
                act.wait_ge(h_added, n + 1)
                act.activation(absz[:, :], psZ[:, 0:GT * P], ACT.Abs, bias=bf1c[:, 0:1]).then_inc(abs_done, 1)
                act.activation(relz[:, :], psZ[:, 0:GT * P], ACT.Relu, bias=bf1c[:, 0:1]).then_inc(z_used, 1)
                act.wait_ge(abs_done, n + 1)
                act.activation(expz[:, :], absz[:, :], ACT.Exp, scale=-1.0).then_inc(exp_done, 1)
                act.wait_ge(exp_done, n + 1)
                act.activation(logz[:, :], expz[:, :], ACT.Ln, bias=halfc[:, 0:1], scale=0.5).then_inc(soft_done, 1)

            def upper(q, n):
                act.wait_ge(h_cut, n + 1)
                act.copy(hu[:, q, :], hcut[:, :]).then_inc(hu_ready, 1)

            def factors(q, n, tiles):
                act.wait_ge(hot_ready, n + 1)
                for j in tiles:
                    for c in range(4):
                        last = act.activation(shot[:, q, j, c, :], hot[:, q, j, :], ACT.Copy,
                                              scale=rec[:, q, j, CO + c:CO + c + 1])
                if tiles[-1] == GT - 1:
                    last.then_inc(shot_ready, 1)

            def begin_along(q):
                for j in range(GT):
                    last = act.activation(along[:, q, j, :], node[:, q, j, C:2 * C], ACT.Copy,
                                          scale=rec[:, q, j, CO + 1:CO + 2])
                last.then_inc(along_begun, 1)

            def empty(t, r):
                b = act.value_load(BLOCK[0:1, bass.ds(t, 1)], min_val=0, max_val=SB - 1)
                act.wait_ge(summed, t + 2)
                act.copy(AGG[:, bass.ds(b, 1), :].rearrange("p o d -> p (o d)"), psA[:, :]).then_inc(copied, 1)
                act.wait_ge(copied, t + 1)
                act.copy(psA[:, :], zerof[:, :]).then_inc(flushed[r], 1)

            def flush(t, r, ended):
                with act.If(ended > 0):
                    empty(t, r)
                with act.Else():
                    act.sem_inc(copied, 1)
                    act.wait_ge(summed, t + 1)
                    act.sem_inc(flushed[r], 1)

            act.preload_act_table_set("natural_log_exp_and_others")
            act.wait_ge(zeroed, 3)
            act.wait_ge(rec_turned, 1)
            attributes()
            soften(0)
            upper(0, 0)
            act.wait_ge(node_in[0], 16 * GT)
            begin_along(0)
            factors(0, 0, (0, 1, 2))
            act.wait_ge(rec_turned, 2)
            act.wait_ge(z_ready, 1)
            attributes()
            with act.Fori(0, GROUPS // 2) as i:
                for q in range(2):
                    s = 2 * i + q
                    if q == 0:
                        ends = act.value_load(FLUSH[0:1, bass.ds(i, 1)], min_val=0, max_val=(1 << UN) - 1)
                    flush(UN * i + GT * q, GT * q % 2, (ends >> (GT * q)) & 1)
                    soften(s + 1)
                    act.wait_ge(summed, GT * s + 2)
                    flush(UN * i + GT * q + 1, (GT * q + 1) % 2, (ends >> (GT * q + 1)) & 1)
                    factors(1 - q, s + 1, (0,))
                    upper(1 - q, s + 1)
                    factors(1 - q, s + 1, (1,))
                    act.wait_ge(node_in[1 - q], 16 * GT * (i + 1 + q))
                    begin_along(1 - q)
                    flush(UN * i + GT * q + 2, (GT * q + 2) % 2, (ends >> (GT * q + 2)) & 1)
                    act.wait_ge(rec_turned, s + 3)
                    attributes()
                    factors(1 - q, s + 1, (2,))
            empty(NT, NT % 2)

        @block.vector
        def _(dve):
            def number(q, n):
                dve.tensor_copy(stage[:, q, :], EIDX[:, bass.ds(GT * n, GT)]).then_inc(staged, 1)

            def hots(q, n):
                dve.tensor_tensor(hot[:, q, :, :], spread(iota64[:, :].rearrange("p (o w) -> p o w", o=1), 1, GT),
                                  spread(rec[:, q, :, SRCL:SRCL + 1], 2, SW), ALU.is_equal).then_inc(hot_ready, 1)

            def keys(q, tiles):
                for j in tiles:
                    dve.tensor_scalar(khot[:, q, j, :], iotah[:, 0:P], rec[:, q, j, KEYS:KEYS + 1], None, ALU.is_equal)
                    last = dve.tensor_scalar(dhot[:, q, j, :], iotah[:, :], rec[:, q, j, KEYD:KEYD + 1], None,
                                             ALU.is_equal)
                if tiles[-1] == GT - 1:
                    last.then_inc(keys_ready, 1)

            def add_hidden(n, first=False):
                dve.wait_ge(soft_done, n + 1)
                dve.wait_ge(z_used, n + 1)
                if not first:
                    dve.wait_ge(hr_ready, n)
                dve.tensor_tensor(hsum[:, :], relz[:, :], logz[:, :], ALU.add).then_inc(h_added, 1)
                dve.wait_ge(h_added, n + 2)
                if not first:
                    dve.wait_ge(hu_ready, n)
                dve.tensor_scalar(hcut[:, :].bitcast(I32), hsum[:, :].bitcast(I32), UPPER, None,
                                  ALU.bitwise_and).then_inc(h_cut, 1)

            def rest(q, n):
                dve.wait_ge(h_cut, n + 1)
                dve.tensor_tensor(hr[:, q, :], hsum[:, :], hcut[:, :], ALU.subtract).then_inc(hr_ready, 1)

            def end_along(q, n):
                dve.wait_ge(along_begun, n + 1)
                for i in (1, 2):
                    for j in range(GT):
                        if i == 2:
                            dve.wait_ge(along_x, GT * n + j + 1)
                        last = dve.scalar_tensor_tensor(out=along[:, q, j, :], in0=node[:, q, j, C * (1 + i):C * (2 + i)],
                                                        scalar=rec[:, q, j, CO + 1 + i:CO + 2 + i],
                                                        in1=along[:, q, j, :], op0=ALU.mult, op1=ALU.add)
                        if i == 1:
                            last.then_inc(along_x, 1)
                last.then_inc(along_ready, 1)

            def products(q, j, r):
                xs = spread(node[:, q, j, 0:C].rearrange("p (o f) -> p o f", o=1), 1, 2)
                dve.tensor_tensor(prod[:, r, 0:2, :], psW[:, r, 0:2 * C].rearrange("p (k f) -> p k f", k=2), xs, ALU.mult)
                dve.tensor_tensor(prod[:, r, 2, :], psW[:, r, 2 * C:3 * C], along[:, q, j, :], ALU.mult)
                xv = node[:, q, j, C:D].rearrange("p (i f) -> p i f", i=3)
                wd = spread(psW[:, r, 3 * C:4 * C].rearrange("p (o f) -> p o f", o=1), 1, 3)
                dve.tensor_tensor(prod[:, r, 3:6, :], wd, xv, ALU.mult).then_inc(prod_done, 1)

            def empty(t, r):
                b = dve.value_load(BLOCK[0:1, bass.ds(t, 1)], min_val=0, max_val=SB - 1)
                dve.wait_ge(summed, t + 2)
                dve.tensor_copy(AT[:, bass.ds(b, 1), 0:D].rearrange("p o d -> p (o d)"), psN[:, 0, :])
                dve.tensor_copy(AT[:, bass.ds(b, 1), D:HALF].rearrange("p o d -> p (o d)"),
                                psN[:, 1, 0:HALF - D]).then_inc(counts_copied, 1)
                dve.wait_ge(counts_copied, t + 1)
                dve.memset(psN[:, 0, :], 0.0)
                dve.memset(psN[:, 1, 0:HALF - D], 0.0).then_inc(counts_flushed[r], 1)

            def flush(t, r, ended):
                with dve.If(ended > 0):
                    empty(t, r)
                with dve.Else():
                    dve.sem_inc(counts_copied, 1)
                    dve.sem_inc(counts_flushed[r], 1)

            dve.memset(zrow[:, :], 0.0).then_inc(zeroed, 1)
            dve.memset(fT[:, :], 0.0).then_inc(zeroed, 1)
            dve.memset(zerof[:, :], 0.0).then_inc(zeroed, 1)
            number(0, 0)
            number(1, 1)
            dve.sem_inc(prod_done, 1)
            dve.sem_inc(h_added, 1)
            dve.wait_ge(rec_in[0], 16 * GT)
            number(0, 2)
            hots(0, 0)
            keys(0, (0, 1, 2))
            add_hidden(0, first=True)
            rest(0, 0)
            end_along(0, 0)
            with dve.Fori(0, GROUPS // 2) as i:
                for q in range(2):
                    s = 2 * i + q
                    for j in range(GT):
                        u = GT * q + j
                        t = UN * i + u
                        if u == 0:
                            ends = dve.value_load(FLUSH[0:1, bass.ds(i, 1)], min_val=0, max_val=(1 << UN) - 1)
                        if j == 0:
                            dve.wait_ge(along_ready, s + 1)
                        dve.wait_ge(w_ready, t + 1)
                        dve.wait_ge(summed, t + 1)
                        products(q, j, u % 2)
                        flush(t, u % 2, (ends >> u) & 1)
                        if j == GT - 1:
                            end_along(1 - q, s + 1)
                            keys(1 - q, (GT - 1,))
                        if j == 0:
                            dve.wait_ge(summed, t + 2)
                            dve.wait_ge(rec_in[1 - q], 16 * GT * (i + 1 + q))
                            hots(1 - q, s + 1)
                            number(1 - q, s + 3)
                        if j == 1:
                            add_hidden(s + 1)
                            rest(1 - q, s + 1)
                            keys(1 - q, (0, 1))
            empty(NT, NT % 2)

        @block.tensor
        def _(pe):
            def turn(q):
                pe.transpose(psF[0:GT * RW, 0:P], rec[:, q, :, :].rearrange("p j w -> p (j w)"),
                             ident[:, :]).then_inc(rec_turned, 1)

            def z():
                for j in range(GT):
                    last = pe.matmul(psZ[:, P * j:P * (j + 1)], wf1[:, j, :], fT[:, :], start=True, stop=True)
                last.then_inc(z_ready, 1)

            def filter_(q, j, r):
                pe.matmul(psW[:, r, :], ones3[:, :], bias3[:, :], start=True, stop=False)
                cols = slice(P * j, P * (j + 1))
                pe.matmul(psW[:, r, :], hu[:, q, cols], w2u[:, :], start=False, stop=False)
                pe.matmul(psW[:, r, :], hu[:, q, cols], w2r[:, :], start=False, stop=False)
                pe.matmul(psW[:, r, :], hr[:, q, cols], w2u[:, :], start=False, stop=True).then_inc(w_ready, 1)

            def open_sums(start, stop):
                pe.matmul(psA[:, :], zrow[:, 0:P], zrow[:, :], start=start, stop=stop, skip_group_check=True)
                pe.matmul(psN[:, 0, :], zrow[:, 0:P], zrow[:, :], start=start, stop=stop, skip_group_check=True)
                return pe.matmul(psN[:, 1, 0:HALF - D], zrow[:, 0:P], zrow[:, 0:HALF - D], start=start, stop=stop,
                                 skip_group_check=True)

            def add(dst, left, right):
                return pe.matmul(dst, left, right, start=False, stop=False, skip_group_check=True)

            def sums(q, j, r):
                def to(kind):
                    return psA[:, SW * kind:SW * (kind + 1)]

                add(to(0), prod[:, r, 0, :], shot[:, q, j, 0, :])
                add(psA[:, SW * 2:SW * 5], prod[:, r, 1, :], shot[:, q, j, 1:4, :].rearrange("p c w -> p (c w)"))
                add(to(1), prod[:, r, 2, :], hot[:, q, j, :])
                for i in range(3):
                    add(to(5 + i), prod[:, r, 3 + i, :], shot[:, q, j, 0, :])

            def counts(q, j):
                add(psN[:, 0, :], khot[:, q, j, :], dhot[:, q, j, 0:D])
                add(psN[:, 1, 0:HALF - D], khot[:, q, j, :], dhot[:, q, j, D:HALF]).then_inc(summed, 1)

            pe.wait_ge(zeroed, 2)
            open_sums(True, False).then_inc(summed, 2)
            pe.wait_ge(rec_in[0], 16 * GT)
            turn(0)
            pe.wait_ge(fT_ready, 1)
            z()
            pe.wait_ge(rec_in[1], 16 * GT)
            turn(1)
            pe.wait_ge(hu_ready, 1)
            pe.wait_ge(hr_ready, 1)
            filter_(0, 0, 0)
            with pe.Fori(0, GROUPS // 2) as i:
                for q in range(2):
                    s = 2 * i + q
                    for j in range(GT):
                        u = GT * q + j
                        t = UN * i + u
                        if j == 0:
                            pe.wait_ge(fT_ready, s + 2)
                            pe.wait_ge(z_used, s + 1)
                            z()
                        if j == GT - 1:
                            pe.wait_ge(hu_ready, s + 2)
                            pe.wait_ge(hr_ready, s + 2)
                        pe.wait_ge(prod_done, t + 1)
                        filter_(q if j < GT - 1 else 1 - q, (j + 1) % GT, (u + 1) % 2)
                        if j == GT - 1:
                            pe.wait_ge(rec_in[q], 16 * GT * (i + 2))
                            pe.wait_ge(fT_ready, s + 2)
                            turn(q)
                        if j == 0:
                            pe.wait_ge(keys_ready, s + 1)
                            pe.wait_ge(shot_ready, s + 1)
                        pe.wait_ge(prod_done, t + 2)
                        pe.wait_ge(flushed[u % 2], UN // 2 * i + u // 2 + 1)
                        sums(q, j, u % 2)
                        pe.wait_ge(counts_flushed[u % 2], UN // 2 * i + u // 2 + 1)
                        counts(q, j)
            pe.wait_ge(flushed[NT % 2], NT // 2 + 1)
            pe.wait_ge(counts_flushed[NT % 2], NT // 2 + 1)
            open_sums(False, True)


def epilogue(nc, out, k):
    AGG, AT, X, ident, onesf = k["AGG"], k["AT"], k["X"], k["ident"], k["onesf"]
    w1s, w1v, w2s, w2v = k["w1s"], k["w1v"], k["w2s"], k["w2v"]
    w1T, w2T, wd1T, wd2T, wd3T = k["w1T"], k["w2T"], k["wd1T"], k["wd2T"], k["wd3T"]
    b1c, b2c, bd1c, bd2c, bd3r, epsc, halfc = (k[n] for n in ("b1c", "b2c", "bd1c", "bd2c", "bd3r", "epsc", "halfc"))
    COLS = [(0, 512), (512, 512), (1024, 256)]
    OF = [range(0, 4), range(4, 8), range(8, 10)]
    TAIL = HALF - D
    CUT = 384
    CHUNKS = [range(0, NB // 2), range(NB // 2, NB)]
    with ExitStack() as ctx:
        def sb(name, shape, dt):
            return ctx.enter_context(nc.sbuf_tensor("end_" + name, shape, dt))

        def sem(name):
            return ctx.enter_context(nc.semaphore("end_" + name))

        ST = sb("ST", [P, NPAD], F32)
        VT = sb("VT", [P, 3, NPAD], F32)
        absS = sb("absS", [P, NPAD], F32)
        relS = sb("relS", [P, NPAD], F32)
        stats = sb("stats", [P, NB, 6], F32)
        mv = sb("mv", [P, NB, 2], F32)
        std = sb("std", [P, NB], F32)
        rstd = sb("rstd", [P, NB], F32)
        shift = sb("shift", [P, NB], F32)
        H = sb("H", [P, 2, D], F32)
        dsum = sb("dsum", [P, HALF], F32)
        dinv = sb("dinv", [P, NPAD], F32)
        dcol = sb("dcol", [P, NB], F32)
        YO = sb("YO", [P, 2, D], F32)
        swap = sb("swap", [P, NB, HALF], F32)
        A = AT[:, :, :].rearrange("p (n two) c -> p n (two c)", two=2)
        agg = AGG[:, :, :].rearrange("p b d -> p (b d)")
        HT = agg[:, 0:4 * NPAD].rearrange("p (c n) -> p c n", c=4)
        N1 = agg[:, 4 * NPAD:5 * NPAD].rearrange("p (b f) -> p b f", b=NB)
        N2 = agg[:, 5 * NPAD:5 * NPAD + NB * SW].rearrange("p (b f) -> p b f", b=NB)
        vt = VT[:, :, :].rearrange("p i n -> p (i n)")
        Y2T = vt[:, 0:2 * NPAD].rearrange("p (m n) -> p m n", m=2)
        Y1T = vt[:, 2 * NPAD:3 * NPAD]
        H1T = ST[:, :]
        Z = absS[0:SW, :]
        SC = relS[:, :]

        bank = [ctx.enter_context(nc.psum_tensor(f"end_bank{i}", [P, D], F32)) for i in range(8)]
        SBANK, VBANK = bank[0:3], (bank[3], bank[6], bank[7], bank[2], bank[0], bank[1])
        XBANK = bank[4:6]
        TBANK, GBANK = (bank[1], bank[3]), (bank[0], bank[2])
        L1BANK, L2BANK = bank[4:7], (bank[1], bank[3], bank[7])
        Y1BANK, Y2BANK, Y3BANK = bank[4:7], (bank[0], bank[2]), (bank[7], bank[1], bank[3])

        s_mm, s_in = sem("s_mm"), sem("s_in")
        exp_ok, ln2_ok = sem("exp_ok"), sem("ln2_ok")
        v_mm, v_in = sem("v_mm"), sem("v_in")
        soft = sem("soft")
        loops = sem("loops")
        swapped = sem("swapped")
        restored = sem("restored")
        sum_dve = sem("sum_dve")
        sum_pool = sem("sum_pool")
        pool_chain = sem("pool_chain")
        v_chain = sem("v_chain")
        deg_mm = sem("deg_mm")
        dcol_sqrt, dcol_ok = sem("dcol_sqrt"), sem("dcol_ok")
        row_sqrt, dinv_ok = sem("row_sqrt"), sem("dinv_ok")
        x_mm, x_new = sem("x_mm"), sem("x_new")
        var_ok, std_ok, ln_ok = sem("var_ok"), sem("std_ok"), sem("ln_ok")
        h_ok = sem("h_ok")
        x_bias = sem("x_bias")
        tr, trc = sem("tr"), sem("trc")
        g1_mm, g1_in = sem("g1_mm"), sem("g1_in")
        l1_mm, l1_scaled, l1_in = sem("l1_mm"), sem("l1_scaled"), sem("l1_in")
        g2_mm, g2_in = sem("g2_mm"), sem("g2_in")
        l2_mm, l2_scaled, l2_in = sem("l2_mm"), sem("l2_scaled"), sem("l2_in")
        y1_mm, y1_in = sem("y1_mm"), sem("y1_in")
        y2_mm, y2_in = sem("y2_mm"), sem("y2_in")
        y3_mm, y3_in = sem("y3_mm"), sem("y3_in")
        s_out = [sem(f"s_out{i}") for i in range(2)]
        block = ctx.enter_context(nc.Block())

        @block.sync
        def _(sp):
            sp.wait_ge(loops, 1)
            sp.dma_start(swap[0:SW, :, :], AT[SW:P, 0::2, :]).then_inc(swapped, 16)
            sp.dma_start(swap[SW:P, :, :], AT[0:SW, 1::2, :]).then_inc(swapped, 16)
            for b in range(NB):
                sp.wait_ge(y3_in, b + 1)
                rows = P if b < NB - 1 else LAST
                sp.dma_start(out[b * P:b * P + rows, :], YO[0:rows, b % 2, :]).then_inc(s_out[b % 2], 16)
            for i in range(2):
                sp.wait_ge(s_out[i], 16 * (NB // 2))

        @block.gpsimd
        def _(pool):
            chain = Chain(pool, pool_chain)
            pool.wait_ge(loops, 1)
            chain.link(pool.tensor_tensor(dsum[:, CUT:HALF], AT[:, 0, CUT:HALF], AT[:, 1, CUT:HALF], ALU.add))
            for b in range(2, SB):
                chain.link(pool.tensor_tensor(dsum[:, CUT:HALF], dsum[:, CUT:HALF], AT[:, b, CUT:HALF], ALU.add))
            pool.sem_inc(sum_pool, 1)

        @block.tensor
        def _(pe):
            def sums(kind, c0, n):
                return AGG[:, c0 // SW:(c0 + n) // SW, SW * kind:SW * (kind + 1)]

            for m, (c0, w) in enumerate(COLS):
                pe.matmul(SBANK[m][:, 0:w], w1s[:, 0, :], sums(0, c0, w), start=True, stop=False)
                pe.matmul(SBANK[m][:, 0:w], w1s[:, 1, :], sums(1, c0, w), start=False, stop=True).then_inc(s_mm, 1)
            def vectors(m):
                c0, w = COLS[m]
                pe.wait_ge(s_in, 3)
                for i in range(3):
                    n = 3 * m + i
                    if n >= 6:
                        pe.wait_ge(v_in, n - 5)
                    v = VBANK[n % 6]
                    pe.matmul(v[:, 0:w], w1v[:, 0, :], sums(2 + i, c0, w), start=True, stop=False)
                    pe.matmul(v[:, 0:w], w1v[:, 1, :], sums(5 + i, c0, w), start=False, stop=True).then_inc(v_mm, 1)

            def degrees():
                pe.wait_ge(sum_dve, 1)
                pe.wait_ge(sum_pool, 1)
                pe.wait_ge(v_in, 9)
                for hf in range(2):
                    rows = slice(SW * hf, SW * hf + SW)
                    pe.matmul(bank[1 + 2 * hf][:, :], onesf[rows, :], dsum[rows, 0:D], start=True, stop=True)
                    pe.matmul(bank[2 * hf][:, 0:TAIL], onesf[rows, :], dsum[rows, D:HALF], start=True, stop=True)
                    for d in range(NB // 2):
                        last = pe.matmul(bank[2 * hf][:, TAIL + d:TAIL + d + 1], dsum[rows, d * P:(d + 1) * P],
                                         onesf[rows, 0:1], start=True, stop=True)
                last.then_inc(deg_mm, 1)

            def layer_rows(m):
                pe.wait_ge(soft, 1)
                pe.wait_ge(v_in, 3 * m + 3)
                for b in OF[m]:
                    if b == 6:
                        degrees()
                    if b >= 2:
                        pe.wait_ge(x_new, b - 1)
                    x, cols = XBANK[b % 2], slice(b * P, (b + 1) * P)
                    pe.matmul(x[:, 0:C], ST[:, cols], w2s[:, :], start=True, stop=True)
                    for i in range(3):
                        last = pe.matmul(x[:, C * (i + 1):C * (i + 2)], VT[:, i, cols], w2v[:, :], start=True, stop=True)
                    last.then_inc(x_mm, 1)

            vectors(0)
            vectors(1)
            layer_rows(0)
            vectors(2)
            layer_rows(1)
            layer_rows(2)

            def transposes(b):
                pe.wait_ge(h_ok, b + 1)
                if b >= 2:
                    pe.wait_ge(trc, b - 1)
                for c in range(4):
                    last = pe.transpose(TBANK[b % 2][:, P * c:P * (c + 1)], H[:, b % 2, P * c:P * (c + 1)], ident[:, :])
                last.then_inc(tr, 1)

            pe.wait_ge(dcol_sqrt, 1)
            pe.wait_ge(row_sqrt, 1)
            transposes(0)
            for b in range(NB):
                if b + 1 < NB:
                    transposes(b + 1)
                pe.wait_ge(trc, b + 1)
                if b >= 2:
                    pe.wait_ge(g1_in, b - 1)
                for c in range(4):
                    last = pe.matmul(GBANK[b % 2][:, 0:P], HT[:, c, b * P:(b + 1) * P], w1T[:, c, :],
                                     start=(c == 0), stop=(c == 3))
                last.then_inc(g1_mm, 1)

            def neighbours(banks, left, rows, m, done):
                c0, w = COLS[m]
                for b in range(NB):
                    last = pe.matmul(banks[m][0:rows, 0:w], left[:, b, :], A[:, b, c0:c0 + w],
                                     start=(b == 0), stop=(b == NB - 1))
                last.then_inc(done, 1)

            def second(m):
                pe.wait_ge(l1_in, m + 1)
                for b in OF[m]:
                    if b >= 2:
                        pe.wait_ge(g2_in, b - 1)
                    pe.matmul(GBANK[b % 2][:, 0:SW], H1T[:, b * P:(b + 1) * P], w2T[:, :], start=True,
                              stop=True).then_inc(g2_mm, 1)

            pe.wait_ge(g1_in, NB)
            pe.wait_ge(x_new, NB)
            pe.wait_ge(restored, 2)
            neighbours(L1BANK, N1, P, 0, l1_mm)
            neighbours(L1BANK, N1, P, 1, l1_mm)
            second(0)
            neighbours(L1BANK, N1, P, 2, l1_mm)
            second(1)
            second(2)

            def decode1(m):
                c0, w = COLS[m]
                pe.wait_ge(l2_in, m + 1)
                pe.matmul(Y1BANK[m][:, 0:w], wd1T[0:SW, :], Z[:, c0:c0 + w], start=True, stop=True).then_inc(y1_mm, 1)

            def decode2(m):
                c0, w = COLS[m]
                pe.wait_ge(y1_in, m + 1)
                for n in range(2):
                    if m:
                        pe.wait_ge(y2_in, 2 * m + n - 1)
                    pe.matmul(Y2BANK[n][:, 0:w], wd2T[:, P * n:P * n + P], Y1T[:, c0:c0 + w], start=True,
                              stop=True).then_inc(y2_mm, 1)

            def decode3(m):
                pe.wait_ge(y2_in, 2 * m + 2)
                for b in OF[m]:
                    if b >= 3:
                        pe.wait_ge(y3_in, b - 2)
                    y, cols = Y3BANK[b % 3], slice(b * P, (b + 1) * P)
                    pe.matmul(y[:, :], Y2T[:, 0, cols], wd3T[:, 0, :], start=True, stop=False)
                    pe.matmul(y[:, :], Y2T[:, 1, cols], wd3T[:, 1, :], start=False, stop=True).then_inc(y3_mm, 1)

            pe.wait_ge(g2_in, NB)
            neighbours(L2BANK, N2, SW, 0, l2_mm)
            neighbours(L2BANK, N2, SW, 1, l2_mm)
            decode1(0)
            decode2(0)
            neighbours(L2BANK, N2, SW, 2, l2_mm)
            decode1(1)
            decode2(1)
            pe.wait_ge(l2_scaled, 3)
            decode3(0)
            decode1(2)
            decode2(2)
            decode3(1)
            decode3(2)

        @block.scalar
        def _(act):
            act.preload_act_table_set("natural_log_exp_and_others")
            for m, (c0, w) in enumerate(COLS):
                act.wait_ge(s_mm, m + 1)
                act.activation(absS[:, c0:c0 + w], SBANK[m][:, 0:w], ACT.Abs)
                act.activation(relS[:, c0:c0 + w], SBANK[m][:, 0:w], ACT.Relu).then_inc(s_in, 1)
            act.wait_ge(s_in, 3)
            act.activation(absS[:, :], absS[:, :], ACT.Exp, scale=-1.0).then_inc(exp_ok, 1)
            act.wait_ge(exp_ok, 1)
            act.activation(absS[:, :], absS[:, :], ACT.Ln, bias=halfc[:, 0:1], scale=0.5).then_inc(ln2_ok, 1)
            n = 0
            for c0, w in COLS:
                for i in range(3):
                    act.wait_ge(v_mm, n + 1)
                    act.copy(VT[:, i, c0:c0 + w], VBANK[n % 6][:, 0:w]).then_inc(v_in, 1)
                    n += 1
            act.wait_ge(deg_mm, 1)
            for hf in range(2):
                last = act.activation(dcol[:, NB // 2 * hf:NB // 2 * (hf + 1)], bank[2 * hf][:, TAIL:TAIL + NB // 2], ACT.Sqrt)
            last.then_inc(dcol_sqrt, 1)
            for hf in range(2):
                at = HALF * hf
                act.activation(dinv[:, at:at + D], bank[1 + 2 * hf][:, :], ACT.Sqrt)
                last = act.activation(dinv[:, at + D:at + HALF], bank[2 * hf][:, 0:TAIL], ACT.Sqrt)
            last.then_inc(row_sqrt, 1)

            def deviations(m):
                blocks = slice(CHUNKS[m][0], CHUNKS[m][-1] + 1)
                act.wait_ge(var_ok, m + 1)
                act.activation(std[:, blocks], mv[:, blocks, 1], ACT.Sqrt, bias=epsc[:, 0:1]).then_inc(std_ok, 1)
                act.wait_ge(ln_ok, m + 1)

            def normalise(b):
                if b == CHUNKS[1][0]:
                    deviations(1)
                if b >= 2:
                    act.wait_ge(tr, b - 1)
                act.activation(H[:, b % 2, :], X[:, b, :], ACT.Relu, bias=shift[:, b:b + 1],
                               scale=rstd[:, b:b + 1]).then_inc(h_ok, 1)

            def turned(b):
                act.wait_ge(tr, b + 1)
                act.copy(HT[:, :, b * P:(b + 1) * P],
                         TBANK[b % 2][:, :].rearrange("p (c n) -> p c n", c=4)).then_inc(trc, 1)

            deviations(0)
            normalise(0)
            normalise(1)
            turned(0)
            for b in range(NB):
                if b + 2 < NB:
                    normalise(b + 2)
                if b + 1 < NB:
                    turned(b + 1)
                if b == 0:
                    act.wait_ge(dcol_ok, 1)
                act.wait_ge(g1_mm, b + 1)
                act.activation(N1[:, b, :], GBANK[b % 2][:, 0:P], ACT.Copy, scale=dcol[:, b:b + 1]).then_inc(g1_in, 1)

            def first_out(m):
                c0, w = COLS[m]
                act.wait_ge(l1_scaled, m + 1)
                act.activation(H1T[:, c0:c0 + w], SC[:, c0:c0 + w], ACT.Relu, bias=b1c[:, 0:1]).then_inc(l1_in, 1)

            def second_in(m):
                for b in OF[m]:
                    act.wait_ge(g2_mm, b + 1)
                    act.activation(N2[:, b, :], GBANK[b % 2][:, 0:SW], ACT.Copy, scale=dcol[:, b:b + 1]).then_inc(g2_in, 1)

            first_out(0)
            first_out(1)
            second_in(0)
            first_out(2)
            second_in(1)
            second_in(2)

            def second_out(m):
                c0, w = COLS[m]
                act.wait_ge(l2_scaled, m + 1)
                act.activation(Z[:, c0:c0 + w], SC[0:SW, c0:c0 + w], ACT.Identity, bias=b2c[0:SW, 0:1]).then_inc(l2_in, 1)

            def decoded(m):
                c0, w = COLS[m]
                act.wait_ge(y1_mm, m + 1)
                act.activation(Y1T[:, c0:c0 + w], Y1BANK[m][:, 0:w], ACT.Relu, bias=bd1c[:, 0:1]).then_inc(y1_in, 1)
                for n in range(2):
                    act.wait_ge(y2_mm, 2 * m + n + 1)
                    act.activation(Y2T[:, n, c0:c0 + w], Y2BANK[n][:, 0:w], ACT.Relu,
                                   bias=bd2c[:, n:n + 1]).then_inc(y2_in, 1)

            second_out(0)
            second_out(1)
            decoded(0)
            second_out(2)
            decoded(1)
            decoded(2)

        @block.vector
        def _(dve):
            chain = Chain(dve, v_chain)
            for b in range(SB):
                hf = b * SW // HALF
                rows = slice(SW * hf, SW * hf + SW)
                col = b * SW - HALF * hf
                last = dve.tensor_tensor(AT[rows, b, col:col + SW], AT[rows, b, col:col + SW], ident[rows, rows], ALU.add)
            last.then_inc(loops, 1)
            dve.wait_ge(loops, 1)
            dve.tensor_reduce(dsum[:, 0:CUT], AT[:, :, 0:CUT].rearrange("p b n -> p n b"), AX_X, ALU.add).then_inc(sum_dve, 1)
            dve.wait_ge(ln2_ok, 1)
            dve.tensor_tensor(ST[:, :], relS[:, :], absS[:, :], ALU.add).then_inc(soft, 1)

            def update(b):
                x = XBANK[b % 2]
                dve.wait_ge(x_mm, b + 1)
                dve.tensor_tensor(X[:, b, 0:C], x[:, 0:C], X[:, b, 0:C], ALU.add)
                xv = X[:, b, C:D].rearrange("p (d i) -> p i d", i=3)
                dve.tensor_tensor(xv, x[:, C:D].rearrange("p (i d) -> p i d", i=3), xv, ALU.add).then_inc(x_new, 1)
                dve.wait_ge(x_new, b + 1)
                return dve.bn_stats(stats[:, b, :], X[:, b, :])

            def variances(m):
                for b in CHUNKS[m]:
                    last = dve.bn_aggr(mv[:, b, :], stats[:, b, :])
                last.then_inc(var_ok, 1)

            def scales(m):
                blocks = slice(CHUNKS[m][0], CHUNKS[m][-1] + 1)
                dve.wait_ge(std_ok, m + 1)
                chain.link(dve.reciprocal(rstd[:, blocks], std[:, blocks]))
                dve.scalar_tensor_tensor(out=shift[:, blocks], in0=mv[:, blocks, 0], scalar=-1.0, in1=rstd[:, blocks],
                                         op0=ALU.mult, op1=ALU.mult).then_inc(ln_ok, 1)

            for b in CHUNKS[0]:
                last = update(b)
            chain.link(last)
            variances(0)
            for b in CHUNKS[1]:
                last = update(b)
                if b == CHUNKS[1][1]:
                    scales(0)
                    dve.wait_ge(dcol_sqrt, 1)
                    dve.reciprocal(dcol[:, :], dcol[:, :]).then_inc(dcol_ok, 1)
            chain.link(last)
            variances(1)
            scales(1)
            dve.wait_ge(sum_dve, 1)
            dve.wait_ge(sum_pool, 1)
            dve.wait_ge(swapped, 32)
            dve.tensor_copy(AT[0:SW, 1::2, :], swap[0:SW, :, :]).then_inc(restored, 1)
            dve.tensor_copy(AT[SW:P, 0::2, :], swap[SW:P, :, :]).then_inc(restored, 1)
            dve.wait_ge(row_sqrt, 1)
            dve.reciprocal(dinv[:, :], dinv[:, :]).then_inc(dinv_ok, 1)
            dve.wait_ge(h_ok, NB)
            dve.tensor_tensor(X[:, :, :], X[:, :, :], spread(bd3r[:, :].rearrange("p (o d) -> p o d", o=1), 1, NB),
                              ALU.add).then_inc(x_bias, 1)
            dve.wait_ge(dinv_ok, 1)
            for m, (c0, w) in enumerate(COLS):
                dve.wait_ge(l1_mm, m + 1)
                dve.tensor_tensor(SC[:, c0:c0 + w], L1BANK[m][:, 0:w], dinv[:, c0:c0 + w], ALU.mult).then_inc(l1_scaled, 1)
            for m, (c0, w) in enumerate(COLS):
                dve.wait_ge(l2_mm, m + 1)
                dve.wait_ge(l1_in, m + 1)
                dve.tensor_tensor(SC[0:SW, c0:c0 + w], L2BANK[m][0:SW, 0:w], dinv[0:SW, c0:c0 + w],
                                  ALU.mult).then_inc(l2_scaled, 1)
            dve.wait_ge(x_bias, 1)
            for b in range(NB):
                dve.wait_ge(y3_mm, b + 1)
                if b >= 2:
                    dve.wait_ge(s_out[b % 2], 16 * (b // 2))
                dve.tensor_tensor(YO[:, b % 2, :], Y3BANK[b % 3][:, :], X[:, b, :], ALU.add).then_inc(y3_in, 1)


_INS = ["x", "src", "dst", "edge_attr_20", "edge_attr_3", "edge_weight",
        "L0_gnn_W_in2f_s", "L0_gnn_W_in2f_v", "L0_gnn_Wf1", "L0_gnn_bf1", "L0_gnn_Wf2", "L0_gnn_bf2",
        "L0_gnn_W1_s", "L0_gnn_W1_v", "L0_gnn_W2_s", "L0_gnn_W2_v",
        "L1_gnn_W1", "L1_gnn_b1", "L1_gnn_W2", "L1_gnn_b2", "L1_gnn_Wd1", "L1_gnn_bd1",
        "L1_gnn_Wd2", "L1_gnn_bd2", "L1_gnn_Wd3", "L1_gnn_bd3"]


def kernel(**inputs):
    import numpy as _np
    import concourse.bacc as _bacc
    from concourse import mybir as _mybir
    from concourse.bass_utils import run_bass_kernel_spmd as _run

    nc = _bacc.Bacc("TRN2", target_bir_lowering=False, num_devices=1)
    arrays, args = {}, {}
    for name in _INS:
        v = _np.ascontiguousarray(inputs[name])
        arrays[f"in_{name}_dram"] = v
        args[name] = nc.dram_tensor(f"in_{name}_dram", v.shape, _mybir.dt.from_np(v.dtype), kind="ExternalInput").ap()
    out = nc.dram_tensor("out_0_dram", (N, D), _mybir.dt.float32, kind="ExternalOutput").ap()
    gnn_kernel(nc, args, out)
    r = _run(nc, [arrays], core_ids=[0])
    return r.results[0]["out_0_dram"]
```
